# Optimizing a Trainium2 kernel written in Bass

```python
import numpy as np
import jax
import jax.numpy as jnp

def _softmax(x, axis=-1):
    return jax.nn.softmax(x, axis=axis)

def _gelu(x):
    return jax.nn.gelu(x, approximate=True)

def _silu(x):
    return jax.nn.silu(x)

def _sigmoid(x):
    return jax.nn.sigmoid(x)

def _layernorm(x, axis=-1, eps=1e-05):
    m = jnp.mean(x, axis=axis, keepdims=True)
    v = jnp.var(x, axis=axis, keepdims=True)
    return (x - m) / jnp.sqrt(v + eps)

def _scatter_add(tgt, idx, src, axis=0):
    return tgt.at[idx].add(src)

def _segment_sum(src, seg, n):
    return jax.ops.segment_sum(src, seg, n)
kernel_name = 'mk_gnn_ffn_d2_gnn_r8_c8ee6a'

def setup_inputs(seed: int=0):
    np.random.seed(seed)
    _w = jnp.asarray

    def _rec_inputs():
        import jax
        import jax.numpy as jnp
        _gk = jax.random.key(seed)
        x = -0.0006008 + 1.001 * jax.random.normal(jax.random.fold_in(_gk, 1), (6250, 512), jnp.float32)
        src = jax.random.randint(jax.random.fold_in(_gk, 2), (100000,), 0, 6250, jnp.int32)
        dst = jnp.minimum((6250 * jax.random.uniform(jax.random.fold_in(_gk, 3), (100000,)) ** 2.0).astype(jnp.int32), 49999)
        _o = jnp.argsort(dst, stable=True)
        src = src[_o]
        dst = dst[_o]
        edge_attr_20 = jax.random.uniform(jax.random.fold_in(_gk, 12), (100000, 20), jnp.float32, 0.0, 0.999999)
        edge_attr_3 = -0.0005747 + 0.998114 * jax.random.normal(jax.random.fold_in(_gk, 13), (100000, 3), jnp.float32)
        edge_weight = jax.random.uniform(jax.random.fold_in(_gk, 15), (100000,), jnp.float32, 0.0, 0.999973)
        return (x, src, dst, edge_attr_20, edge_attr_3, edge_weight)
    x, src, dst, edge_attr_20, edge_attr_3, edge_weight = _rec_inputs()

    def _L0_gnn_setup():
        import jax, jax.numpy as jnp
        import numpy as np
        N_ATOMS = 625
        N_EDGES = 6250
        C = 128
        F = 128
        N_RBF = 20
        LOG2 = float(np.log(2.0))
        Y0 = float(1.0 / np.sqrt(4.0 * np.pi))
        Y1_SCALE = float(np.sqrt(3.0 / (4.0 * np.pi)))

        def shifted_softplus(x):
            return jax.nn.softplus(x) - LOG2

        def _forward(x, idx_i, idx_j, f_ij, rcut_ij, r_ij, W_in2f_s, W_in2f_v, Wf1, bf1, Wf2, bf2, W1_s, W1_v, W2_s, W2_v):
            n = x.shape[0]
            e = r_ij.shape[0]
            xs = x[:, :C] @ (W_in2f_s / np.sqrt(C))
            xv = jnp.einsum('nci,cf->nfi', x[:, C:].reshape(n, C, 3), W_in2f_v) / np.sqrt(C)
            sj = xs[idx_j]
            vj = xv[idx_j]
            u = r_ij / jnp.linalg.norm(r_ij, axis=-1, keepdims=True)
            Yv = Y1_SCALE * u
            o0a = sj * Y0
            o0b = jnp.einsum('efi,ei->ef', vj, Yv) / np.sqrt(3.0)
            s2 = jnp.stack([o0a, o0b], axis=-1).reshape(e, 2 * F)
            ova = sj[:, :, None] * Yv[:, None, :]
            ovb = vj * Y0
            v2 = jnp.stack([ova, ovb], axis=2)
            w1 = jnp.cross(vj, Yv[:, None, :]) / np.sqrt(2.0)
            ax, ay, az = (vj[..., 0], vj[..., 1], vj[..., 2])
            bx, by, bz = (Yv[:, None, 0], Yv[:, None, 1], Yv[:, None, 2])
            t = jnp.stack([(ax * by + ay * bx) / np.sqrt(2.0), (ay * bz + az * by) / np.sqrt(2.0), (2.0 * az * bz - ax * bx - ay * by) / np.sqrt(6.0), (az * bx + ax * bz) / np.sqrt(2.0), (ax * bx - ay * by) / np.sqrt(2.0)], axis=-1)
            h = shifted_softplus(f_ij @ Wf1 + bf1)
            W = (h @ Wf2 + bf2) * rcut_ij[:, None]
            m_s = s2 * W[:, :2 * F]
            m_v = (v2.reshape(e, 2 * F, 3) * W[:, 2 * F:4 * F, None]).reshape(e, 6 * F)
            m_w = (w1 * W[:, 4 * F:5 * F, None]).reshape(e, 3 * F)
            m_t = (t * W[:, 5 * F:6 * F, None]).reshape(e, 5 * F)
            x_ij = jnp.concatenate([m_s, m_v, m_w, m_t], axis=1)
            agg = jax.ops.segment_sum(x_ij, idx_i, num_segments=n)
            S = agg[:, :2 * F] @ (W1_s / np.sqrt(2 * F))
            V = jnp.einsum('nmi,mc->nci', agg[:, 2 * F:8 * F].reshape(n, 2 * F, 3), W1_v) / np.sqrt(2 * F)
            S = shifted_softplus(S)
            S = S @ (W2_s / np.sqrt(C))
            V = jnp.einsum('nci,cd->ndi', V, W2_v) / np.sqrt(C)
            return jnp.concatenate([S, V.reshape(n, 3 * C)], axis=1)
        key = jax.random.key(seed)
        ks = jax.random.split(key, 16)
        f32 = jnp.float32
        x = jax.random.normal(ks[0], (N_ATOMS, 4 * C), f32)
        idx_i = jnp.sort(jax.random.randint(ks[1], (N_EDGES,), 0, N_ATOMS))
        idx_j = jax.random.randint(ks[2], (N_EDGES,), 0, N_ATOMS)
        f_ij = jax.random.uniform(ks[3], (N_EDGES, N_RBF), f32)
        rcut_ij = jax.random.uniform(ks[4], (N_EDGES,), f32)
        r_ij = jax.random.normal(ks[5], (N_EDGES, 3), f32)
        W_in2f_s = jax.random.normal(ks[6], (C, F), f32)
        W_in2f_v = jax.random.normal(ks[7], (C, F), f32)
        Wf1 = jax.random.normal(ks[8], (N_RBF, F), f32) / np.sqrt(N_RBF)
        bf1 = 0.1 * jax.random.normal(ks[9], (F,), f32)
        Wf2 = jax.random.normal(ks[10], (F, 6 * F), f32) / np.sqrt(F)
        bf2 = 0.1 * jax.random.normal(ks[11], (6 * F,), f32)
        W1_s = jax.random.normal(ks[12], (2 * F, C), f32)
        W1_v = jax.random.normal(ks[13], (2 * F, C), f32)
        W2_s = jax.random.normal(ks[14], (C, C), f32)
        W2_v = jax.random.normal(ks[15], (C, C), f32)
        return dict(x=x, idx_i=idx_i, idx_j=idx_j, f_ij=f_ij, rcut_ij=rcut_ij, r_ij=r_ij, W_in2f_s=W_in2f_s, W_in2f_v=W_in2f_v, Wf1=Wf1, bf1=bf1, Wf2=Wf2, bf2=bf2, W1_s=W1_s, W1_v=W1_v, W2_s=W2_s, W2_v=W2_v)
    _L0_gnn_all = _L0_gnn_setup()
    _L0_gnn_in = {k: v for k, v in _L0_gnn_all.items() if k in ('W_in2f_s', 'W_in2f_v', 'Wf1', 'bf1', 'Wf2', 'bf2', 'W1_s', 'W1_v', 'W2_s', 'W2_v')}
    del _L0_gnn_all

    def _L0_ffn_setup():
        import jax, jax.numpy as jnp
        import numpy as np
        EPS = 1e-05

        def _bitlinear(x, w):
            w_scale = jnp.clip(jnp.mean(jnp.abs(w)), EPS, None)
            w_q = jnp.clip(jnp.round(w / w_scale), -1.0, 1.0) * w_scale
            w_eff = w + jax.lax.stop_gradient(w_q - w)
            x_scale = 127.0 / jnp.clip(jnp.max(jnp.abs(x), axis=-1, keepdims=True), EPS, None)
            x_q = jnp.clip(jnp.round(x * x_scale), -128.0, 127.0) / x_scale
            x_eff = x + jax.lax.stop_gradient(x_q - x)
            return jnp.einsum('bsi,oi->bso', x_eff, w_eff)

        def _ste_round_clamp_int8(h):
            h_q = jnp.clip(jnp.round(h), -128.0, 127.0)
            return h + jax.lax.stop_gradient(h_q - h)
        key = jax.random.key(seed)
        k1, k2, k3 = jax.random.split(key, 3)
        B, S, D, F = (8, 1024, 512, 256)
        x = jax.random.normal(k1, (B, S, D), dtype=jnp.float32)
        w_up = jax.random.normal(k2, (F, D), dtype=jnp.float32) * (1.0 / np.sqrt(D))
        w_down = jax.random.normal(k3, (D, F), dtype=jnp.float32) * (1.0 / np.sqrt(F))
        return {'x': x, 'w_up': w_up, 'w_down': w_down}
    _L0_ffn_all = _L0_ffn_setup()
    _L0_ffn_in = {k: v for k, v in _L0_ffn_all.items() if k in ('w_up', 'w_down')}
    del _L0_ffn_all

    def _L1_gnn_setup():
        import jax, jax.numpy as jnp
        import numpy as np
        N_NODES = 6250
        N_EDGES = 200000
        IN_F = 512
        OUT_F = 512
        key = jax.random.key(seed)
        k1, k2, k3, k4, k5 = jax.random.split(key, 5)
        input = jax.random.normal(k1, (N_NODES, IN_F), dtype=jnp.float32)
        edge_index = jax.random.randint(k2, (2, N_EDGES), 0, N_NODES, dtype=jnp.int64)
        edge_vals = jax.random.uniform(k3, (N_EDGES,), dtype=jnp.float32)
        stdv = 1.0 / np.sqrt(OUT_F)
        weight = jax.random.uniform(k4, (IN_F, OUT_F), dtype=jnp.float32, minval=-stdv, maxval=stdv)
        bias = jax.random.uniform(k5, (OUT_F,), dtype=jnp.float32, minval=-stdv, maxval=stdv)
        return {'input': input, 'edge_index': edge_index, 'edge_vals': edge_vals, 'weight': weight, 'bias': bias}
    _L1_gnn_all = _L1_gnn_setup()
    _L1_gnn_in = {k: v for k, v in _L1_gnn_all.items() if k in ('weight', 'bias')}
    del _L1_gnn_all

    def _L1_ffn_setup():
        import jax, jax.numpy as jnp
        import numpy as np
        D_MODEL = 512
        D_FF = 256
        N_EXPERTS = 8
        TOP_K = 2
        key = jax.random.key(seed)
        ks = jax.random.split(key, 8)
        x = jax.random.normal(ks[0], (2, 256, D_MODEL), dtype=jnp.float32)
        router_w = jax.random.normal(ks[1], (D_MODEL, N_EXPERTS), dtype=jnp.float32) * 0.02
        router_b = jnp.zeros((N_EXPERTS,), dtype=jnp.float32)
        s1 = 1.0 / np.sqrt(D_MODEL)
        s2 = 1.0 / np.sqrt(D_FF)
        W1 = jax.random.uniform(ks[2], (N_EXPERTS, D_MODEL, D_FF), jnp.float32, -s1, s1)
        b1 = jax.random.uniform(ks[3], (N_EXPERTS, D_FF), jnp.float32, -s1, s1)
        W2 = jax.random.uniform(ks[4], (N_EXPERTS, D_FF, D_MODEL), jnp.float32, -s2, s2)
        b2 = jax.random.uniform(ks[5], (N_EXPERTS, D_MODEL), jnp.float32, -s2, s2)
        return {'x': x, 'router_w': router_w, 'router_b': router_b, 'W1': W1, 'b1': b1, 'W2': W2, 'b2': b2}
    _L1_ffn_all = _L1_ffn_setup()
    _L1_ffn_in = {k: v for k, v in _L1_ffn_all.items() if k in ('router_w', 'router_b', 'W1', 'b1', 'W2', 'b2')}
    del _L1_ffn_all
    return {'x': x, 'src': src, 'dst': dst, 'edge_attr_20': edge_attr_20, 'edge_attr_3': edge_attr_3, 'edge_weight': edge_weight, 'L0_gnn_W_in2f_s': _L0_gnn_in['W_in2f_s'], 'L0_gnn_W_in2f_v': _L0_gnn_in['W_in2f_v'], 'L0_gnn_Wf1': _L0_gnn_in['Wf1'], 'L0_gnn_bf1': _L0_gnn_in['bf1'], 'L0_gnn_Wf2': _L0_gnn_in['Wf2'], 'L0_gnn_bf2': _L0_gnn_in['bf2'], 'L0_gnn_W1_s': _L0_gnn_in['W1_s'], 'L0_gnn_W1_v': _L0_gnn_in['W1_v'], 'L0_gnn_W2_s': _L0_gnn_in['W2_s'], 'L0_gnn_W2_v': _L0_gnn_in['W2_v'], 'L0_ffn_w_up': _L0_ffn_in['w_up'], 'L0_ffn_w_down': _L0_ffn_in['w_down'], 'L1_gnn_weight': _L1_gnn_in['weight'], 'L1_gnn_bias': _L1_gnn_in['bias'], 'L1_ffn_router_w': _L1_ffn_in['router_w'], 'L1_ffn_router_b': _L1_ffn_in['router_b'], 'L1_ffn_W1': _L1_ffn_in['W1'], 'L1_ffn_b1': _L1_ffn_in['b1'], 'L1_ffn_W2': _L1_ffn_in['W2'], 'L1_ffn_b2': _L1_ffn_in['b2']}

def reference(x, src, dst, edge_attr_20, edge_attr_3, edge_weight, L0_gnn_W_in2f_s, L0_gnn_W_in2f_v, L0_gnn_Wf1, L0_gnn_bf1, L0_gnn_Wf2, L0_gnn_bf2, L0_gnn_W1_s, L0_gnn_W1_v, L0_gnn_W2_s, L0_gnn_W2_v, L0_ffn_w_up, L0_ffn_w_down, L1_gnn_weight, L1_gnn_bias, L1_ffn_router_w, L1_ffn_router_b, L1_ffn_W1, L1_ffn_b1, L1_ffn_W2, L1_ffn_b2):
    import jax
    import jax.numpy as jnp

    def _L0_gnn_ref(x, idx_i, idx_j, f_ij, rcut_ij, r_ij, W_in2f_s, W_in2f_v, Wf1, bf1, Wf2, bf2, W1_s, W1_v, W2_s, W2_v):
        import jax, jax.numpy as jnp
        import numpy as np
        N_ATOMS = 625
        N_EDGES = 6250
        C = 128
        F = 128
        N_RBF = 20
        LOG2 = float(np.log(2.0))
        Y0 = float(1.0 / np.sqrt(4.0 * np.pi))
        Y1_SCALE = float(np.sqrt(3.0 / (4.0 * np.pi)))

        def shifted_softplus(x):
            return jax.nn.softplus(x) - LOG2

        def _forward(x, idx_i, idx_j, f_ij, rcut_ij, r_ij, W_in2f_s, W_in2f_v, Wf1, bf1, Wf2, bf2, W1_s, W1_v, W2_s, W2_v):
            n = x.shape[0]
            e = r_ij.shape[0]
            xs = x[:, :C] @ (W_in2f_s / np.sqrt(C))
            xv = jnp.einsum('nci,cf->nfi', x[:, C:].reshape(n, C, 3), W_in2f_v) / np.sqrt(C)
            sj = xs[idx_j]
            vj = xv[idx_j]
            u = r_ij / jnp.linalg.norm(r_ij, axis=-1, keepdims=True)
            Yv = Y1_SCALE * u
            o0a = sj * Y0
            o0b = jnp.einsum('efi,ei->ef', vj, Yv) / np.sqrt(3.0)
            s2 = jnp.stack([o0a, o0b], axis=-1).reshape(e, 2 * F)
            ova = sj[:, :, None] * Yv[:, None, :]
            ovb = vj * Y0
            v2 = jnp.stack([ova, ovb], axis=2)
            w1 = jnp.cross(vj, Yv[:, None, :]) / np.sqrt(2.0)
            ax, ay, az = (vj[..., 0], vj[..., 1], vj[..., 2])
            bx, by, bz = (Yv[:, None, 0], Yv[:, None, 1], Yv[:, None, 2])
            t = jnp.stack([(ax * by + ay * bx) / np.sqrt(2.0), (ay * bz + az * by) / np.sqrt(2.0), (2.0 * az * bz - ax * bx - ay * by) / np.sqrt(6.0), (az * bx + ax * bz) / np.sqrt(2.0), (ax * bx - ay * by) / np.sqrt(2.0)], axis=-1)
            h = shifted_softplus(f_ij @ Wf1 + bf1)
            W = (h @ Wf2 + bf2) * rcut_ij[:, None]
            m_s = s2 * W[:, :2 * F]
            m_v = (v2.reshape(e, 2 * F, 3) * W[:, 2 * F:4 * F, None]).reshape(e, 6 * F)
            m_w = (w1 * W[:, 4 * F:5 * F, None]).reshape(e, 3 * F)
            m_t = (t * W[:, 5 * F:6 * F, None]).reshape(e, 5 * F)
            x_ij = jnp.concatenate([m_s, m_v, m_w, m_t], axis=1)
            agg = jax.ops.segment_sum(x_ij, idx_i, num_segments=n)
            S = agg[:, :2 * F] @ (W1_s / np.sqrt(2 * F))
            V = jnp.einsum('nmi,mc->nci', agg[:, 2 * F:8 * F].reshape(n, 2 * F, 3), W1_v) / np.sqrt(2 * F)
            S = shifted_softplus(S)
            S = S @ (W2_s / np.sqrt(C))
            V = jnp.einsum('nci,cd->ndi', V, W2_v) / np.sqrt(C)
            return jnp.concatenate([S, V.reshape(n, 3 * C)], axis=1)
        return _forward(x, idx_i, idx_j, f_ij, rcut_ij, r_ij, W_in2f_s, W_in2f_v, Wf1, bf1, Wf2, bf2, W1_s, W1_v, W2_s, W2_v)

    def _L0_ffn_ref(x, w_up, w_down):
        import jax, jax.numpy as jnp
        import numpy as np
        EPS = 1e-05

        def _bitlinear(x, w):
            w_scale = jnp.clip(jnp.mean(jnp.abs(w)), EPS, None)
            w_q = jnp.clip(jnp.round(w / w_scale), -1.0, 1.0) * w_scale
            w_eff = w + jax.lax.stop_gradient(w_q - w)
            x_scale = 127.0 / jnp.clip(jnp.max(jnp.abs(x), axis=-1, keepdims=True), EPS, None)
            x_q = jnp.clip(jnp.round(x * x_scale), -128.0, 127.0) / x_scale
            x_eff = x + jax.lax.stop_gradient(x_q - x)
            return jnp.einsum('bsi,oi->bso', x_eff, w_eff)

        def _ste_round_clamp_int8(h):
            h_q = jnp.clip(jnp.round(h), -128.0, 127.0)
            return h + jax.lax.stop_gradient(h_q - h)
        h = _bitlinear(x, w_up)
        h = jax.nn.relu(h)
        h = _ste_round_clamp_int8(h)
        return _bitlinear(h, w_down)

    def _L1_gnn_ref(input, edge_index, edge_vals, weight, bias):
        import jax, jax.numpy as jnp
        import numpy as np
        N_NODES = 6250
        N_EDGES = 200000
        IN_F = 512
        OUT_F = 512
        support = jnp.matmul(input, weight)
        dst, src = (edge_index[0], edge_index[1])
        messages = support[src] * edge_vals[:, None]
        output = jax.ops.segment_sum(messages, dst, num_segments=input.shape[0])
        return output + bias

    def _L1_ffn_ref(x, router_w, router_b, W1, b1, W2, b2):
        import jax, jax.numpy as jnp
        import numpy as np
        D_MODEL = 512
        D_FF = 256
        N_EXPERTS = 8
        TOP_K = 2
        leading = x.shape[:-1]
        d = x.shape[-1]
        xf = x.reshape(-1, d)
        n = xf.shape[0]
        logits = xf @ router_w + router_b
        probs = jax.nn.softmax(logits, axis=-1)
        sel_w, sel_idx = jax.lax.top_k(probs, TOP_K)
        sel_w = sel_w / (jnp.sum(sel_w, axis=-1, keepdims=True) + 1e-09)
        comb = jnp.zeros((n, N_EXPERTS), dtype=xf.dtype)
        comb = comb.at[jnp.arange(n)[:, None], sel_idx].add(sel_w)
        h = jnp.einsum('nd,edf->nef', xf, W1) + b1[None]
        h = jax.nn.gelu(h, approximate=False)
        y = jnp.einsum('nef,efd->ned', h, W2) + b2[None]
        out = jnp.einsum('ne,ned->nd', comb, y)
        return out.reshape(*leading, d)
    edge_index = jnp.stack([src, dst])
    x = x + _L0_gnn_ref(_layernorm(x, axis=-1), src, dst, edge_attr_20, edge_weight, edge_attr_3, L0_gnn_W_in2f_s, L0_gnn_W_in2f_v, L0_gnn_Wf1, L0_gnn_bf1, L0_gnn_Wf2, L0_gnn_bf2, L0_gnn_W1_s, L0_gnn_W1_v, L0_gnn_W2_s, L0_gnn_W2_v)
    x = x + _L0_ffn_ref(_layernorm(x, axis=-1)[None], L0_ffn_w_up, L0_ffn_w_down)[0]
    x = x + _L1_gnn_ref(_layernorm(x, axis=-1), edge_index, edge_weight, L1_gnn_weight, L1_gnn_bias)
    x = x + _L1_ffn_ref(_layernorm(x, axis=-1)[None], L1_ffn_router_w, L1_ffn_router_b, L1_ffn_W1, L1_ffn_b1, L1_ffn_W2, L1_ffn_b2)[0]
    return x

_drawn_inputs = setup_inputs


def setup_inputs(seed=0):
    import zlib

    import numpy as np

    out = dict(_drawn_inputs(seed))
    spreads = {'L1_ffn_router_b': (0.0, 0.1)}
    factors = {'L1_gnn_bias': 3.675, 'L1_ffn_b1': 8.0, 'L1_ffn_b2': 3.955}
    for name, (base, spread) in spreads.items():
        noise = np.random.default_rng([zlib.crc32(name.encode()), seed]).standard_normal(out[name].shape)
        drawn = base * np.exp(spread * noise) if base else spread * noise
        out[name] = jnp.asarray(drawn.astype(out[name].dtype))
    for name, factor in factors.items():
        out[name] = (out[name] * factor).astype(out[name].dtype)
    return out
```

```python
from contextlib import ExitStack

import numpy as np

import concourse.bass as bass
from concourse import mybir
from concourse.bass import ds

ALU = mybir.AluOpType
ACT = mybir.ActivationFunctionType
AX = mybir.AxisListType
F32 = mybir.dt.float32
F32R = mybir.dt.float32r
BF16 = mybir.dt.bfloat16
I32 = mybir.dt.int32
U32 = mybir.dt.uint32

P = 128
D = 512
N_NODES = 6250
N_EDGES = 100000
N_RBF = 20
FF = 256
N_EXP = 8

NB = -(-N_NODES // P)
NPAD = NB * P
COLS = 8 * (-(-N_EDGES // (8 * P)))
EPAD = COLS * P
NBKT = NB + 1
GC = 2
GE = GC * P
NG = 2 * (-(-((N_EDGES + NB * (GE - 1)) // GE) // 2))
NQ = NG // 2
NG_ROWS = NG + 8
assert EPAD - N_EDGES <= 2 * GE and NQ % 2 == 0
REC = 32

R_ONE, R_Y, R_CUT, R_TGT, R_DST = 20, 21, 24, 25, 26

C_ID, C_IOTA, C_KEPT = 0, 128, 256
C_TRI, C_BKT, C_GRP, C_END = 256, 384, 448, 448 + NG + 8

EPS = 1e-5
Y0 = float(1.0 / np.sqrt(4.0 * np.pi))
Y1_SCALE = float(np.sqrt(3.0 / (4.0 * np.pi)))
ROUND = 12582912.0


class Link:

    def __init__(self, eng, sem):
        self.eng, self.sem, self.base, self.n = eng, sem, 0, 0

    def __call__(self, ins):
        self.n += 1
        ins.then_inc(self.sem, 1)
        self.eng.wait_ge(self.sem, self.base + self.n)

    def enter(self, i, per):
        self.start, self.per = self.base + self.n, per
        self.base, self.n = self.start + i * per, 0

    def leave(self, count):
        assert self.n == self.per, (self.n, self.per)
        self.base, self.n = self.start + count * self.per, 0


ONE = 4
ONE_DMA = 16


class Space:

    def __init__(self, nc, ctx, tag):
        self.nc, self.ctx, self.tag = nc, ctx, tag
        self.sems, self.dma_sems = [], []

    def sb(self, name, shape, dt=F32):
        return self.ctx.enter_context(self.nc.sbuf_tensor(f"{self.tag}_{name}", shape, dt))

    def psum(self, name, shape, dt=F32):
        return self.ctx.enter_context(self.nc.psum_tensor(f"{self.tag}_{name}", shape, dt))

    def sem(self, name):
        return self.ctx.enter_context(self.nc.semaphore(f"{self.tag}_{name}"))

    def primed(self, name):
        self.sems.append(self.sem(name))
        return self.sems[-1]

    def primed_dma(self, name):
        self.dma_sems.append(self.sem(name))
        return self.dma_sems[-1]

    def prime(self, sp, io, start_word=None):
        for sem in self.sems:
            sp.sem_inc(sem, ONE)
        for k, sem in enumerate(self.dma_sems):
            sp.dma_start(start_word[:, 2 * k:2 * k + 2], io["consts"][:, 0:2]).then_inc(sem, ONE_DMA)


def sort_and_embed(nc, io, shared):
    with ExitStack() as ctx:
        m = Space(nc, ctx, "p1")
        const = m.sb("const", [P, C_END])
        bkt_f = m.sb("bkt_f", [P, NG + 1])
        ident = const[:, C_ID:C_ID + P]
        rec = m.sb("rec", [P, COLS, REC])
        src = m.sb("src", [P, COLS], I32)
        dst = m.sb("dst", [P, COLS], I32)
        work_i = m.sb("work_i", [P, COLS], I32)
        bucket = m.sb("bucket", [P, COLS])
        match = m.sb("match", [P, COLS])
        place = m.sb("place", [P, COLS])
        pos = m.sb("pos", [P, COLS])
        pos_u = m.sb("pos_u", [P, COLS], U32)
        zero = m.sb("zero", [P, COLS])
        count = m.sb("count", [P, 64])
        before = m.sb("before", [P, 64])
        total_i = m.sb("total_i", [P, 64], I32)
        groups = m.sb("groups", [P, 64])
        first = m.sb("first", [P, 64])
        norm = m.sb("norm", [P, COLS])
        pad = m.sb("pad", [P, 4, REC])
        stage = m.sb("stage", [P, 2, 8, REC])
        stage_at = m.sb("stage_at", [P, 2, 8], U32)
        xt = m.sb("xt", [P, 2, D])
        xn = m.sb("xn", [P, D])
        xT = m.sb("xT", [P, 4, P])
        row = m.sb("row", [P, 2, D])
        stats = m.sb("stats", [P, 8])
        mv = m.sb("mv", [P, 4])
        w_s = m.sb("w_s", [P, P])
        w_v = m.sb("w_v", [P, P])
        eps = m.sb("eps", [P, 1])
        ones = m.sb("ones", [P, P])
        zeros = m.sb("zeros", [P, 2 * D])
        ps_c = m.psum("ps_c", [P, 2, 512])
        ps_t = m.psum("ps_t", [P, 4, P])
        ps_o = m.psum("ps_o", [P, 4, P])

        loaded = m.sem("loaded")
        rec_loaded = m.sem("rec_loaded")
        w_loaded = m.sem("w_loaded")
        link_d = m.sem("link_d")
        ready = m.sem("ready")
        squares = m.sem("squares")
        lengths = m.sem("lengths")
        counted = m.sem("counted")
        summed = m.sem("summed")
        placed = m.sem("placed")
        cleared = m.sem("cleared")
        pad_made = m.sem("pad_made")
        padded = m.sem("padded")
        staged = m.sem("staged")
        scattered = [m.sem(f"scattered{k}") for k in range(2)]
        x_in = [m.sem(f"x_in{k}") for k in range(2)]
        x_free = m.sem("x_free")
        stats_ok = m.sem("stats_ok")
        passed_d = m.sem("passed_d")
        passed_p = m.sem("passed_p")
        var_ok = m.sem("var_ok")
        std_ok = m.sem("std_ok")
        xn_ok = m.sem("xn_ok")
        turned = m.sem("turned")
        xT_ok = m.sem("xT_ok")
        embedded = m.sem("embedded")
        row_ok = m.primed("row_ok")
        row_out = [m.primed_dma(f"row_out{k}") for k in range(2)]
        scaled = m.sem("scaled")

        start_word = m.sb("start_word", [P, 2 * len(m.dma_sems)])
        block = ctx.enter_context(nc.Block())

        @block.sync
        def _(sp):
            m.prime(sp, io, start_word)
            sp.dma_start(const[:], io["consts"]).then_inc(loaded, 16)
            sp.dma_start(src[:], io["src"]).then_inc(loaded, 16)
            sp.dma_start(dst[:], io["dst"]).then_inc(loaded, 16)
            sp.dma_start(rec[:], io["edges"]).then_inc(rec_loaded, 16)
            sp.dma_start(w_s[:], io["w_in_s"]).then_inc(w_loaded, 16)
            sp.dma_start(w_v[:], io["w_in_v"]).then_inc(w_loaded, 16)
            sp.wait_ge(pad_made, 2)
            with sp.Fori(0, NG_ROWS // 2) as g:
                sp.dma_start(io["sorted"][ds(g * 4 * P, 4 * P), :].rearrange("(p j) w -> p (j w)", j=4),
                             pad[:].rearrange("p j w -> p (j w)")).then_inc(padded, 16)
            sp.wait_ge(ready, 2)
            with sp.Fori(0, NB) as b:
                sp.dma_start(io["agg"][ds(b * P, P), :], zeros[:]).then_inc(cleared, 16)
            for k in range(2):
                sp.dma_start(xt[:, k, :], io["x"][k * P:(k + 1) * P, :]).then_inc(x_in[k], 16)
            with sp.Fori(0, (NB - 1) // 2) as t:
                for k in range(2):
                    sp.wait_ge(row_ok, ONE + 2 * t + k + 1)
                    sp.dma_start(io["table_a"][ds((2 * t + k) * P, P), :],
                                 row[:, k, :]).then_inc(row_out[k], 16)
                    sp.wait_ge(xn_ok, 2 * t + k + 1)
                    sp.dma_start(xt[:, k, :], io["x"][ds((2 * t + 2 + k) * P, P), :]).then_inc(x_in[k], 16)
            sp.wait_ge(row_ok, ONE + NB)
            sp.dma_start(io["table_a"][(NB - 1) * P:NB * P, :], row[:, 0, :]).then_inc(row_out[0], 16)
            sp.wait_ge(row_out[0], ONE_DMA + 16 * (NB // 2 + 1))
            sp.wait_ge(row_out[1], ONE_DMA + 16 * (NB // 2))
            sp.wait_ge(x_in[1], 16 * (NB // 2 + 1))
            sp.wait_ge(cleared, 16 * NB)

        @block.gpsimd
        def _(pool):
            nc.gpsimd.memset(pad[:], 0.0).then_inc(pad_made, 1)
            pool.wait_ge(pad_made, 1)
            nc.gpsimd.memset(pad[:, :, R_Y:R_Y + 1], 1.0).then_inc(pad_made, 1)
            pool.wait_ge(placed, 1)
            pool.wait_ge(padded, 16 * (NG_ROWS // 2))

            def scatter(q, k):
                col = q * 16 + k * 8
                cols = slice(col, col + 8) if isinstance(q, int) else ds(col, 8)
                nc.gpsimd.tensor_copy(stage[:, k], rec[:, cols, :]).then_inc(staged, 1)
                nc.gpsimd.tensor_copy(stage_at[:, k], pos_u[:, cols]).then_inc(staged, 1)
                pool.wait_ge(staged, q * 4 + k * 2 + 2)
                pool.sem_inc(passed_p, 1)
                for c in range(8):
                    nc.gpsimd.indirect_dma_start(
                        out=io["sorted"], out_offset=bass.IndirectOffsetOnAxis(ap=stage_at[:, k, c:c + 1], axis=0),
                        in_=stage[:, k, c, :], in_offset=None).then_inc(scattered[k], 16)

            scatter(0, 0)
            scatter(0, 1)
            with pool.Fori(1, COLS // 16) as q:
                for k in range(2):
                    pool.wait_ge(scattered[k], q * 128)
                    scatter(q, k)
            for k in range(2):
                pool.wait_ge(scattered[k], (COLS // 16) * 128)

        @block.tensor
        def _(pe):
            pe.wait_ge(counted, 1)
            nc.tensor.matmul(ps_c[:, 0, 0:64], const[:, C_TRI:C_TRI + P], count[:], start=True, stop=True)
            nc.tensor.matmul(ps_c[:, 1, 0:64], ones[:], count[:], start=True, stop=True).then_inc(summed, 1)
            pe.wait_ge(scaled, 2)
            with pe.Fori(0, NB) as t:
                pe.wait_ge(xn_ok, t + 1)
                for k in range(4):
                    part = xn[:, 0:P] if k == 0 else xn[:, P + k - 1:D:3]
                    mm = nc.tensor.transpose(ps_t[:, k, :], part, ident)
                mm.then_inc(turned, 1)
                pe.wait_ge(xT_ok, t + 1)
                pe.wait_ge(row_ok, ONE + t)
                for k in range(4):
                    mm = nc.tensor.matmul(ps_o[:, k, :], xT[:, k, :], (w_s if k == 0 else w_v)[:],
                                          start=True, stop=True)
                mm.then_inc(embedded, 1)

        @block.scalar
        def _(act):
            act.wait_ge(w_loaded, 32)
            nc.scalar.mul(w_s[:], w_s[:], float(1 / np.sqrt(P))).then_inc(scaled, 1)
            nc.scalar.mul(w_v[:], w_v[:], float(1 / np.sqrt(P))).then_inc(scaled, 1)
            act.wait_ge(squares, 1)
            nc.scalar.activation(norm[:], norm[:], ACT.Sqrt).then_inc(lengths, 1)
            act.wait_ge(ready, 1)
            with act.Fori(0, NB) as t:
                act.wait_ge(var_ok, t + 1)
                nc.scalar.activation(mv[:, 2:3], mv[:, 1:2], ACT.Sqrt, bias=eps[:]).then_inc(std_ok, 1)
                act.wait_ge(turned, t + 1)
                nc.scalar.copy(xT[:], ps_t[:]).then_inc(xT_ok, 1)

        @block.vector
        def _(dve):
            link = Link(dve, link_d)
            nc.vector.memset(eps[:], EPS).then_inc(ready, 1)
            nc.vector.memset(zeros[:], 0.0).then_inc(ready, 1)
            link(nc.vector.memset(zero[:], 0.0))
            link(nc.vector.memset(ones[:], 1.0))
            link(nc.vector.memset(pos[:], -1.0))
            link(nc.vector.memset(count[:], 0.0))
            dve.wait_ge(loaded, 48)
            link(nc.vector.tensor_scalar(work_i[:], src[:], 7, None, ALU.arith_shift_right))
            link(nc.vector.tensor_copy(bucket[:], work_i[:]))
            with dve.Fori(0, NBKT) as b:
                link.enter(b, 1)
                link(nc.vector.tensor_scalar(match[:], bucket[:], const[:, ds(C_BKT + b, 1)], 0.0,
                                             ALU.is_equal, ALU.add, accum_out=count[:, ds(b, 1)]))
                link.leave(NBKT)
            nc.vector.memset(before[:], 0.0).then_inc(counted, 1)
            dve.wait_ge(summed, 1)
            link(nc.vector.tensor_scalar(groups[:], ps_c[:, 1, 0:64], float(GE - 1), None, ALU.add))
            link(nc.vector.tensor_copy(total_i[:], groups[:]))
            link(nc.vector.tensor_scalar(total_i[:], total_i[:], 8, None, ALU.arith_shift_right))
            link(nc.vector.tensor_copy(groups[:], total_i[:]))
            link(nc.vector.memset(first[:], 0.0))
            link(nc.vector.tensor_tensor_scan(first[:, 1:64], groups[:, 0:63], zero[:, 0:63], 0.0, ALU.add, ALU.add))
            link(nc.vector.scalar_tensor_tensor(out=before[:], in0=first[:], scalar=float(GE), in1=ps_c[:, 0, 0:64],
                                                op0=ALU.mult, op1=ALU.add))
            with dve.Fori(0, NBKT) as b:
                link.enter(b, 4)
                link(nc.vector.tensor_scalar(match[:], bucket[:], const[:, ds(C_BKT + b, 1)], None, ALU.is_equal))
                link(nc.vector.tensor_tensor_scan(place[:], match[:], zero[:], before[:, ds(b, 1)], ALU.add, ALU.add))
                link(nc.vector.tensor_tensor(place[:], place[:], match[:], ALU.mult))
                link(nc.vector.tensor_tensor(pos[:], pos[:], place[:], ALU.add))
                link.leave(NBKT)
            link(nc.vector.tensor_copy(pos_u[:], pos[:]))
            dve.wait_ge(rec_loaded, 16)
            link(nc.vector.tensor_scalar(work_i[:], src[:], P - 1, None, ALU.bitwise_and))
            link(nc.vector.tensor_copy(rec[:, :, R_TGT], work_i[:]))
            link(nc.vector.tensor_copy(rec[:, :, R_DST].bitcast(I32), dst[:]))
            link(nc.vector.tensor_tensor(place[:], rec[:, :, R_Y], rec[:, :, R_Y], ALU.mult))
            for k in (1, 2):
                link(nc.vector.tensor_tensor(match[:], rec[:, :, R_Y + k], rec[:, :, R_Y + k], ALU.mult))
                link(nc.vector.tensor_tensor(place[:], place[:], match[:], ALU.add))
            nc.vector.tensor_copy(norm[:], place[:]).then_inc(squares, 1)
            dve.wait_ge(lengths, 1)
            link(nc.vector.reciprocal(norm[:], norm[:]))
            for k in range(3):
                link(nc.vector.scalar_tensor_tensor(out=rec[:, :, R_Y + k], in0=rec[:, :, R_Y + k], scalar=Y1_SCALE,
                                                    in1=norm[:], op0=ALU.mult, op1=ALU.mult))
            nc.vector.memset(zero[:], 0.0).then_inc(placed, 1)
            bkt_i, keep = shared["bkt_i"], shared["keep"]
            nc.vector.tensor_copy(shared["const"][:], const[:, 0:C_KEPT])
            link(nc.vector.memset(bkt_f[:], 0.0))
            with dve.Fori(1, NB) as b:
                link.enter(b - 1, 1)
                link(nc.vector.scalar_tensor_tensor(out=bkt_f[:, 1:], in0=const[:, C_GRP:C_GRP + NG],
                                                    scalar=first[:, ds(b, 1)], in1=bkt_f[:, 1:],
                                                    op0=ALU.is_ge, op1=ALU.add))
                link.leave(NB - 1)
            link(nc.vector.tensor_copy(bkt_i[:], bkt_f[:]))
            link(nc.vector.memset(keep[:], 0.0))
            link(nc.vector.tensor_tensor(keep[:, 2:], bkt_f[:, 2:], bkt_f[:, 1:NG], ALU.is_equal))

            def node_tile(t, k, x_count, out_count):
                dve.wait_ge(x_in[k], x_count)
                nc.vector.bn_stats(stats[:, 0:6], xt[:, k, :]).then_inc(stats_ok, 1)
                dve.wait_ge(stats_ok, t + 1)
                dve.sem_inc(passed_d, 1)
                nc.vector.bn_aggr(mv[:, 0:2], stats[:, 0:6]).then_inc(var_ok, 1)
                dve.wait_ge(std_ok, t + 1)
                link(nc.vector.reciprocal(mv[:, 3:4], mv[:, 2:3]))
                nc.vector.tensor_scalar(xn[:], xt[:, k, :], mv[:, 0:1], mv[:, 3:4],
                                        ALU.subtract, ALU.mult).then_inc(xn_ok, 1)
                dve.wait_ge(embedded, t + 1)
                if out_count is not None:
                    dve.wait_ge(row_out[k], ONE_DMA + out_count)
                nc.vector.tensor_copy(row[:, k, :], ps_o[:].rearrange("p k f -> p (k f)")).then_inc(row_ok, 1)

            with dve.Fori(0, NB // 2) as t:
                link.enter(t, 2)
                for k in range(2):
                    node_tile(2 * t + k, k, 16 * t + 16, 16 * t)
                link.leave(NB // 2)
            node_tile(NB - 1, 0, 16 * (NB // 2 + 1), 16 * (NB // 2))


def edge_sums(nc, io, shared):
    with ExitStack() as ctx:
        m = Space(nc, ctx, "p2")
        const, bkt_i, keep = shared["const"], shared["bkt_i"], shared["keep"]
        ident = const[:, C_ID:C_ID + P]
        iota = const[:, C_IOTA:C_IOTA + P]
        wf1 = m.sb("wf1", [N_RBF + 1, P])
        wf2 = m.sb("wf2", [P, 512])
        bf2 = m.sb("bf2", [P, 512])
        bias = m.sb("bias", [P, 512], BF16)
        b_hi = m.sb("b_hi", [P, 3, 512], BF16)
        b_rest = m.sb("b_rest", [P, 512])
        ones = m.sb("ones", [P, P], BF16)
        half = m.sb("half", [P, 1])
        blank = m.sb("blank", [P, 512], BF16)
        rec = m.sb("rec", [P, 2, 2, 2, REC])
        feat = m.sb("feat", [P, 2, 2, 2, REC])
        got = m.sb("got", [P, 2, 4, D])
        fT = m.sb("fT", [N_RBF + 1, 512])
        soft = m.sb("soft", [P, 512])
        h = m.sb("h", [P, 2, 512])
        dot0 = m.sb("dot0", [P, 2, 4, P])
        dot = m.sb("dot", [P, 2, P])
        m02 = m.sb("m02", [P, 4, 2, P])
        m1 = m.sb("m1", [P, 4, P])
        m3 = m.sb("m3", [P, 4, 3, P])
        hot = m.sb("hot", [P, 2, 4, 4, P])
        sums = m.sb("sums", [P, 2, 2 * D])
        ps_f = m.psum("ps_f", [P, 512])
        ps_h = m.psum("ps_h", [P, 512])
        ps_w = m.psum("ps_w", [P, 2, 512])
        ps_a = m.psum("ps_a", [P, 2, 2, 512])

        w_loaded = m.sem("w_loaded")
        link_a = m.sem("link_a")
        link_d = m.sem("link_d")
        weights = m.sem("weights")
        rec_in = [m.sem(f"rec_in{k}") for k in range(2)]
        feat_in = [m.sem(f"feat_in{k}") for k in range(2)]
        got_in = [[m.sem(f"got_in{k}{c}") for c in range(4)] for k in range(2)]
        passed = m.sem("passed")
        passed_s = m.sem("passed_s")
        turned = m.sem("turned")
        fT_ok = m.sem("fT_ok")
        pre_h = m.sem("pre_h")
        soft_ok = m.sem("soft_ok")
        h_ok = m.sem("h_ok")
        w_ok = m.sem("w_ok")
        hot_ok = m.sem("hot_ok")
        dot0_ok = m.sem("dot0_ok")
        msg_ok = m.primed("msg_ok")
        spent = m.primed("spent")
        sums_ok = m.primed("sums_ok")
        sums_out = m.primed_dma("sums_out")

        start_word = m.sb("start_word", [P, 2 * len(m.dma_sems)])
        block = ctx.enter_context(nc.Block())

        def load_records(sp, tile, q, k, sem):
            row = ds(q * 4 * P, 4 * P) if not isinstance(q, int) else slice(q * 4 * P, (q + 1) * 4 * P)
            sp.dma_start(tile[:, k].rearrange("p g j w -> p g (j w)"),
                         io["sorted"][row, :].rearrange("(g p j) w -> p g (j w)", g=2, j=2)).then_inc(sem[k], 16)

        @block.sync
        def _(sp):
            m.prime(sp, io, start_word)
            sp.dma_start(wf1[:], io["wf1"]).then_inc(w_loaded, 16)
            sp.dma_start(wf2[:], io["wf2"]).then_inc(w_loaded, 16)
            sp.dma_start(bf2[:], io["bf2"].to_broadcast([P, 512])).then_inc(w_loaded, 16)
            for k in range(2):
                load_records(sp, rec, k, k, rec_in)
                load_records(sp, feat, k, k, feat_in)
            for k in range(2):
                sp.wait_ge(turned, k + 1)
                load_records(sp, feat, k + 2, k, feat_in)

            def put_sums(entry, k):
                at = sp.value_load(bkt_i[0:1, ds(entry, 1)], min_val=0, max_val=NB - 1)
                sp.wait_ge(sums_ok, ONE + entry + 1)
                sp.sem_inc(passed_s, 1)
                sp.wait_ge(sums_out, ONE_DMA + entry * 16)
                sp.sem_inc(passed_s, 1)
                sp.dma_start(io["agg"][ds(at * P, P), :], sums[:, k, :]).then_inc(sums_out, 16)

            with sp.Fori(0, NQ // 2) as i:
                for u in range(2):
                    put_sums(4 * i + 2 * u, 1)
                    sp.wait_ge(turned, 2 * i + u + 3)
                    load_records(sp, feat, 2 * i + u + 4, u, feat_in)
                    sp.wait_ge(msg_ok, ONE + 8 * i + 4 * u + 5)
                    load_records(sp, rec, 2 * i + u + 2, u, rec_in)
                    put_sums(4 * i + 2 * u + 1, 0)
            put_sums(NG, 1)
            sp.wait_ge(sums_out, ONE_DMA + 16 * (NG + 1))
            for k in range(2):
                sp.wait_ge(rec_in[k], 16 * (NQ // 2 + 1))
                sp.wait_ge(feat_in[k], 16 * (NQ // 2 + 2))

        @block.gpsimd
        def _(pool):
            def gather(k, c):
                nc.gpsimd.indirect_dma_start(
                    out=got[:, k, c, :], out_offset=None, in_=io["table_a"],
                    in_offset=bass.IndirectOffsetOnAxis(
                        ap=rec[:, k, c // 2, c % 2, R_DST:R_DST + 1].bitcast(U32), axis=0)).then_inc(got_in[k][c], 16)

            def one_hots(k):
                for c in range(4):
                    word = rec[:, k, c // 2, c % 2]
                    last = nc.gpsimd.tensor_scalar(hot[:, k, c, 0, :], iota, word[:, R_TGT:R_TGT + 1],
                                                   word[:, R_CUT:R_CUT + 1], ALU.is_equal, ALU.mult)
                last.then_inc(hot_ok, 1)

            for k in range(2):
                pool.wait_ge(rec_in[k], 16)
                for c in range(4):
                    gather(k, c)
                one_hots(k)
            with pool.Fori(1, NQ // 2) as i:
                for k in range(2):
                    pool.wait_ge(rec_in[k], 16 * i + 16)
                    for c in range(4):
                        pool.wait_ge(msg_ok, ONE + 8 * i + 4 * k + c - 6)
                        pool.sem_inc(passed, 1)
                        gather(k, c)
                    pool.wait_ge(spent, ONE + 8 * i + 4 * k - 3)
                    pool.sem_inc(passed, 1)
                    one_hots(k)
            pool.wait_ge(msg_ok, ONE + NQ * 4 - 3)
            pool.wait_ge(rec_in[0], 16 * (NQ // 2) + 16)
            for c in range(4):
                gather(0, c)
            pool.wait_ge(spent, ONE + 4 * NQ - 3)
            one_hots(0)

        @block.tensor
        def _(pe):
            def turn(k, count):
                pe.wait_ge(feat_in[k], count)
                for c in range(4):
                    mm = nc.tensor.transpose(ps_f[0:N_RBF + 1, c * P:(c + 1) * P],
                                             feat[:, k, c // 2, c % 2, 0:N_RBF + 1], ident)
                mm.then_inc(turned, 1)

            def hidden(count):
                pe.wait_ge(fT_ok, count)
                nc.tensor.matmul(ps_h[:], wf1[:], fT[:], start=True, stop=True).then_inc(pre_h, 1)

            def filters(k, c, n=None, count=None):
                if n is not None:
                    pe.wait_ge(msg_ok, ONE + n + 2)
                if count is not None:
                    pe.wait_ge(h_ok, count)
                nc.tensor.matmul(ps_w[:, c % 2, :], ones[0:65, :], bias[0:65, :], start=True, stop=False)
                nc.tensor.matmul(ps_w[:, c % 2, :], h[:, k, c * P:(c + 1) * P], wf2[:],
                                 start=False, stop=True).then_inc(w_ok, 1)

            def add_up(q, c, n, group):
                b, g = c, c // 2
                pe.wait_ge(msg_ok, ONE + n + 2)
                one, times_y = hot[:, q, c, 0, :], hot[:, q, c, 1:4, :].rearrange("p k n -> p (k n)")
                if c % 2 == 0:
                    pe.wait_ge(sums_ok, ONE + group)
                first, last = c % 2 == 0, c % 2 == 1
                A, B = ps_a[:, g, 0, :], ps_a[:, g, 1, :]
                nc.tensor.matmul(A[:, 0:P], m02[:, b, 0, :], one, start=first, stop=False,
                                 skip_group_check=True)
                nc.tensor.matmul(A[:, P:512], m02[:, b, 1, :], times_y,
                                 start=False, stop=last, skip_group_check=True)
                nc.tensor.matmul(B[:, 0:P], m1[:, b, :], one, start=first, stop=False,
                                 skip_group_check=True)
                for k in range(3):
                    mm = nc.tensor.matmul(B[:, (k + 1) * P:(k + 2) * P], m3[:, b, k, :], one,
                                          start=False, stop=last and k == 2, skip_group_check=True)
                mm.then_inc(spent, 1)

            pe.wait_ge(weights, 3)
            for bank in range(2):
                mm = nc.tensor.matmul(ps_a[:, 1, bank, :], blank[:, 0:P], blank[:], start=True, stop=True)
            mm.then_inc(spent, 1)
            for k in range(2):
                turn(k, 16)
                hidden(k + 1)
                filters(0, k, count=1)
            with pe.Fori(0, NQ // 2) as i:
                for u in range(2):
                    n, g = 8 * i + 4 * u, 4 * i + 2 * u
                    filters(u, 2, n)
                    add_up(u, 0, n, g)
                    filters(u, 3, n + 1)
                    add_up(u, 1, n + 1, g)
                    filters(1 - u, 0, n + 2, 2 * i + u + 2)
                    turn(u, 16 * (i + 2))
                    add_up(u, 2, n + 2, g + 1)
                    filters(1 - u, 1, n + 3)
                    hidden(2 * i + u + 3)
                    add_up(u, 3, n + 3, g + 1)

        @block.scalar
        def _(act):
            link = Link(act, link_a)
            act.wait_ge(w_loaded, 48)
            nc.scalar.mul(wf2[:, 0:P], wf2[:, 0:P], Y0)
            nc.scalar.mul(wf2[:, 2 * P:3 * P], wf2[:, 2 * P:3 * P], float(1 / np.sqrt(3)))
            nc.scalar.mul(wf2[:, 3 * P:], wf2[:, 3 * P:], Y0).then_inc(weights, 1)

            def features(count):
                act.wait_ge(turned, count)
                nc.scalar.copy(fT[:], ps_f[0:N_RBF + 1, :]).then_inc(fT_ok, 1)

            def softplus(count):
                act.wait_ge(pre_h, count)
                link(nc.scalar.activation(soft[:], ps_h[:], ACT.Abs))
                link(nc.scalar.activation(soft[:], soft[:], ACT.Exp, scale=-1.0))
                nc.scalar.activation(soft[:], soft[:], ACT.Ln, bias=half[:], scale=0.5).then_inc(soft_ok, 1)

            def products(k, chunks, n, count):
                for c in chunks:
                    word = rec[:, k, c // 2, c % 2]
                    act.wait_ge(got_in[k][c], count)
                    for j in range(3):
                        nc.scalar.mul(hot[:, k, c, 1 + j, :], hot[:, k, c, 0, :], word[:, R_Y + j:R_Y + j + 1])
                    nc.scalar.mul(dot0[:, k, c, :], got[:, k, c, P:2 * P], word[:, R_Y:R_Y + 1]).then_inc(dot0_ok, 1)

            act.wait_ge(weights, 3)
            features(1)
            softplus(1)
            features(2)
            act.wait_ge(hot_ok, 1)
            products(0, range(4), 0, 16)
            with act.Fori(0, NQ // 2) as i:
                link.enter(i, 4)
                for u in range(2):
                    q = 2 * i + u + 1
                    softplus(q + 1)
                    act.wait_ge(hot_ok, q + 1)
                    products(1 - u, range(4), 4 * q, 16 * (i + 1 + u))
                    features(q + 2)
                link.leave(NQ // 2)

        @block.vector
        def _(dve):
            link = Link(dve, link_d)
            link(nc.vector.memset(half[:], 0.5))
            link(nc.vector.memset(ones[:], 1.0))
            link(nc.vector.memset(blank[:], 0.0))
            link(nc.vector.memset(bias[:], 0.0))
            link(nc.vector.memset(sums[:], 0.0))
            dve.wait_ge(w_loaded, 48)
            link(nc.vector.tensor_scalar(bf2[:, 0:P], bf2[:, 0:P], Y0, None, ALU.mult))
            link(nc.vector.tensor_scalar(bf2[:, 2 * P:3 * P], bf2[:, 2 * P:3 * P], float(1 / np.sqrt(3)), None, ALU.mult))
            link(nc.vector.tensor_scalar(bf2[:, 3 * P:], bf2[:, 3 * P:], Y0, None, ALU.mult))
            rest = bf2
            for part in range(3):
                link(nc.vector.tensor_copy(b_hi[:, part, :], rest[:]))
                link(nc.vector.tensor_copy(bias[32 * part:32 * part + 1, :], b_hi[32 * part:32 * part + 1, part, :]))
                link(nc.vector.tensor_tensor(b_rest[:], rest[:], b_hi[:, part, :], ALU.subtract))
                rest = b_rest
            nc.vector.memset(dot[:], 0.0).then_inc(weights, 1)
            nc.vector.memset(m1[:], 0.0).then_inc(weights, 1)
            dve.wait_ge(weights, 3)
            nc.vector.memset(m3[:], 0.0).then_inc(msg_ok, 1)
            dve.wait_ge(msg_ok, ONE + 1)

            def h_part(k, count):
                dve.wait_ge(soft_ok, count)
                nc.vector.scalar_tensor_tensor(out=h[:, k, :], in0=ps_h[:], scalar=0.0, in1=soft[:],
                                               op0=ALU.max, op1=ALU.add).then_inc(h_ok, 1)

            def messages(k, c, n, count):
                b = c % 2
                word = rec[:, k, c // 2, b]
                row = got[:, k, c, :]
                dve.wait_ge(spent, ONE + n - 2)
                dve.wait_ge(dot0_ok, n + 1)
                link(nc.vector.scalar_tensor_tensor(out=dot[:, b, :], in0=row[:, 2 * P:3 * P],
                                                    scalar=word[:, R_Y + 1:R_Y + 2], in1=dot0[:, k, c, :],
                                                    op0=ALU.mult, op1=ALU.add))
                link(nc.vector.scalar_tensor_tensor(out=dot[:, b, :], in0=row[:, 3 * P:4 * P],
                                                    scalar=word[:, R_Y + 2:R_Y + 3], in1=dot[:, b, :],
                                                    op0=ALU.mult, op1=ALU.add))
                dve.wait_ge(w_ok, n + 1)
                W = ps_w[:, b, :]
                nc.vector.tensor_tensor(m1[:, c, :], dot[:, b, :], W[:, 2 * P:3 * P], ALU.mult)
                nc.vector.tensor_tensor(m02[:, c], row[:, 0:P].unsqueeze(1).to_broadcast([P, 2, P]),
                                        W[:, 0:2 * P].rearrange("p (j f) -> p j f", j=2), ALU.mult)
                nc.vector.tensor_tensor(m3[:, c], row[:, P:].rearrange("p (j f) -> p j f", j=3),
                                        W[:, 3 * P:].unsqueeze(1).to_broadcast([P, 3, P]),
                                        ALU.mult).then_inc(msg_ok, 1)

            def add_group(k, entry):
                dve.wait_ge(spent, ONE + 2 * entry + 1)
                dve.wait_ge(sums_out, ONE_DMA + 16 * entry)
                dve.wait_ge(sums_ok, ONE + entry)
                nc.vector.scalar_tensor_tensor(
                    out=sums[:, k, :], in0=sums[:, 1 - k, :], scalar=keep[:, ds(entry, 1)],
                    in1=ps_a[:, k].rearrange("p b n -> p (b n)"), op0=ALU.mult, op1=ALU.add).then_inc(sums_ok, 1)

            h_part(0, 1)
            with dve.Fori(0, NQ // 2) as i:
                link.enter(i, 16)
                for u in range(2):
                    n, entry = 8 * i + 4 * u, 4 * i + 2 * u
                    messages(u, 0, n, 16 * i + 16)
                    messages(u, 1, n + 1, 16 * i + 16)
                    add_group(1, entry)
                    h_part(1 - u, 2 * i + u + 2)
                    messages(u, 2, n + 2, 16 * i + 16)
                    messages(u, 3, n + 3, 16 * i + 16)
                    add_group(0, entry + 1)
                link.leave(NQ // 2)
            add_group(1, NG)


class Norms:

    def __init__(self, nc, m, tiles):
        self.nc, self.tiles = nc, tiles
        self.stats = m.sb("stats", [P, tiles, 6])
        self.mv = m.sb("mv", [P, tiles, 2])
        self.small = m.sb("small", [P, 5, tiles])
        self.stats_ok = m.sem("stats_ok")
        self.passed = m.sem("norm_passed")
        self.var_ok = m.sem("var_ok")
        self.std_ok = m.sem("std_ok")

    def tile(self, dve, j, rows):
        dve.sem_inc(self.passed, 1)
        self.nc.vector.bn_stats(self.stats[:, j, :], rows).then_inc(self.stats_ok, 1)

    def scale(self, dve, link, stats_count, batch):
        v, r, t, out, std = (self.small[:, k, :] for k in range(5))
        dve.wait_ge(self.stats_ok, stats_count)
        dve.sem_inc(self.passed, 1)
        for j in range(self.tiles):
            last = self.nc.vector.bn_aggr(self.mv[:, j, :], self.stats[:, j, :])
        link(last)
        self.nc.vector.tensor_scalar(v, self.mv[:, :, 1], EPS, None, ALU.add).then_inc(self.var_ok, 1)
        dve.wait_ge(self.var_ok, batch)
        dve.wait_ge(self.std_ok, batch)
        link(self.nc.vector.reciprocal(r, std))
        link(self.nc.vector.tensor_tensor(t, r, r, ALU.mult))
        link(self.nc.vector.tensor_tensor(t, t, v, ALU.mult))
        link(self.nc.vector.tensor_scalar(t, t, -0.5, 1.5, ALU.mult, ALU.add))
        link(self.nc.vector.tensor_tensor(out, r, t, ALU.mult))

    LINKS = 6

    def root(self, act, batch):
        act.wait_ge(self.var_ok, batch)
        self.nc.scalar.activation(self.small[:, 4, :], self.small[:, 0, :], ACT.Sqrt).then_inc(self.std_ok, 1)

    def apply(self, out, rows, j):
        return self.nc.vector.tensor_scalar(out, rows, self.mv[:, j, 0:1], self.small[:, 3, j:j + 1],
                                            ALU.subtract, ALU.mult)


def node_layers(nc, io, shared):
    with ExitStack() as ctx:
        m = Space(nc, ctx, "p3")
        const, acc = shared["const"], shared["acc"]
        ident = const[:, C_ID:C_ID + P]
        TB = 7
        NBATCH = NB // TB
        agg = m.sb("agg", [P, 2, 2 * D])
        w1s = m.sb("w1s", [P, 2, P])
        w1v = m.sb("w1v", [P, 2, P])
        w2s = m.sb("w2s", [P, P])
        w2v = m.sb("w2v", [P, P])
        wup = m.sb("wup", [P, 4, FF])
        wdn = m.sb("wdn", [P, 2, D])
        qup = m.sb("qup", [P, 4, FF], BF16)
        qdn = m.sb("qdn", [P, 2, D], BF16)
        wg = m.sb("wg", [P, 4, D])
        bias = m.sb("bias", [P, D])
        ident_b = m.sb("ident_b", [P, P], BF16)
        onesf = m.sb("onesf", [P, P])
        half = m.sb("half", [P, 1])
        wsum = m.sb("wsum", [P, 8])
        soft = m.sb("soft", [P, P])
        sT = m.sb("sT", [P, 2, 4, P])
        xn = m.sb("xn", [P, TB, D])
        tmp = m.sb("tmp", [P, 2, D])
        qb = m.sb("qb", [P, 2, D], BF16)
        qT = m.sb("qT", [P, 2, 4, P], BF16)
        hid = m.sb("hid", [P, TB, FF])
        xT = m.sb("xT", [P, 2, 4, P])
        row = m.sb("row", [P, 2, D])
        scal = m.sb("scal", [P, 8, TB])
        norms = Norms(nc, m, TB)
        ps_1 = m.psum("ps_1", [P, 2, 512])
        ps_2 = m.psum("ps_2", [P, 2, 512])
        ps_b = m.psum("ps_b", [P, 2, 1024], BF16)
        ps_3 = m.psum("ps_3", [P, 2, 512])

        x_in = m.sem("x_in")
        w_in = m.sem("w_in")
        link_d = m.sem("link_d")
        link_a = m.sem("link_a")
        agg_in = [m.sem(f"agg_in{k}") for k in range(2)]
        scaled = m.sem("scaled")
        measured = m.sem("measured")
        ternary = m.sem("ternary")
        totals = m.sem("totals")
        first_ok = m.primed("first_ok")
        soft_ok = m.sem("soft_ok")
        vT_ok = m.primed("vT_ok")
        sT_ok = m.primed("sT_ok")
        second_ok = m.primed("second_ok")
        x1_ok = m.primed("x1_ok")
        q_ok = m.sem("q_ok")
        qturn_ok = m.sem("qturn_ok")
        qT_ok = m.sem("qT_ok")
        up_ok = m.primed("up_ok")
        relu_ok = m.sem("relu_ok")
        q2_ok = m.sem("q2_ok")
        down_ok = m.primed("down_ok")
        x2_ok = m.primed("x2_ok")
        xn_ok = m.sem("xn_ok")
        xturn_ok = m.sem("xturn_ok")
        xT_ok = m.sem("xT_ok")
        prod_ok = m.primed("prod_ok")
        row_ok = m.primed("row_ok")
        row_out = [m.primed_dma(f"row_out{k}") for k in range(2)]
        biased = m.sem("biased")

        start_word = m.sb("start_word", [P, 2 * len(m.dma_sems)])
        block = ctx.enter_context(nc.Block())

        EVEN, ODD = (TB + 1) // 2, TB // 2

        def uses(i, j):
            return (EVEN if j % 2 == 0 else ODD) * i + j // 2 + 1

        @block.sync
        def _(sp):
            m.prime(sp, io, start_word)
            weights = [(w1s, "w1s"), (w1v, "w1v"), (w2s, "w2s"), (w2v, "w2v"), (wup, "wup"), (wdn, "wdn"), (wg, "wg")]
            for tile, name in weights:
                sp.dma_start(tile[:], io[name]).then_inc(w_in, 16)
            sp.dma_start(bias[:], io["gnn_bias"].to_broadcast([P, D])).then_inc(w_in, 16)
            sp.dma_start(acc[:], io["x"][0:NPAD, :].rearrange("(t p) d -> p t d", p=P)).then_inc(x_in, 16)
            with sp.Fori(0, NBATCH) as i:
                for j in range(TB):
                    sp.wait_ge(first_ok, ONE + i * TB + (j - 1 if j else 0))
                    sp.dma_start(agg[:, j % 2, :], io["agg"][ds((i * TB + j) * P, P), :]).then_inc(agg_in[j % 2], 16)
                for j in range(TB):
                    sp.wait_ge(row_ok, ONE + i * TB + j + 1)
                    sp.dma_start(io["table_b"][ds((i * TB + j) * P, P), :], row[:, j % 2, :]).then_inc(row_out[j % 2], 16)
            for k in range(2):
                sp.wait_ge(row_out[k], ONE_DMA + 16 * NBATCH * (EVEN, ODD)[k])

        @block.tensor
        def _(pe):
            pe.wait_ge(measured, 1)
            nc.tensor.matmul(ps_1[:, 0, 0:2], onesf[:], wsum[:, 0:2], start=True, stop=True).then_inc(totals, 1)
            pe.wait_ge(scaled, 1)
            pe.wait_ge(ternary, 1)
            with pe.Fori(0, NBATCH) as i:
                t = i * TB

                def back(j):
                    pe.wait_ge(sT_ok, ONE + t + j + 1)
                    pe.wait_ge(vT_ok, ONE + t + j + 1)
                    pe.wait_ge(x1_ok, ONE + t + (j - 1 if j else 0))
                    for k in range(4):
                        mm = nc.tensor.matmul(ps_2[:, j % 2, k * P:(k + 1) * P], sT[:, j % 2, k, :],
                                              (w2s if k == 0 else w2v)[:], start=True, stop=True)
                    mm.then_inc(second_ok, 1)

                for j in range(TB):
                    b = j % 2
                    pe.wait_ge(agg_in[b], 16 * uses(i, j))
                    pe.wait_ge(sT_ok, ONE + t + (j - 1 if j else 0))
                    pe.wait_ge(vT_ok, ONE + t + (j - 1 if j else 0))
                    for k in range(2):
                        nc.tensor.matmul(ps_1[:, b, 0:P], w1s[:, k, :], agg[:, b, k * D:k * D + P],
                                         start=(k == 0), stop=(k == 1), skip_group_check=True)
                    for k in range(2):
                        mm = nc.tensor.matmul(ps_1[:, b, P:], w1v[:, k, :], agg[:, b, k * D + P:(k + 1) * D],
                                              start=(k == 0), stop=(k == 1), skip_group_check=True)
                    mm.then_inc(first_ok, 1)
                    if j:
                        back(j - 1)
                back(TB - 1)
                for j in range(TB):
                    b = j % 2
                    pe.wait_ge(q_ok, t + j + 1)
                    for k in range(4):
                        mm = nc.tensor.transpose(ps_b[:, b, k * P:(k + 1) * P], qb[:, b, k * P:(k + 1) * P], ident_b[:])
                    mm.then_inc(qturn_ok, 1)
                    pe.wait_ge(qT_ok, 2 * t + j + 1)
                    for k in range(4):
                        mm = nc.tensor.matmul(ps_3[:, b, 0:FF], qT[:, b, k, :], qup[:, k, :], start=(k == 0), stop=(k == 3))
                    mm.then_inc(up_ok, 1)
                for j in range(TB):
                    b = j % 2
                    pe.wait_ge(q2_ok, t + j + 1)
                    for k in range(2):
                        mm = nc.tensor.transpose(ps_b[:, b, k * P:(k + 1) * P], qb[:, b, k * P:(k + 1) * P], ident_b[:])
                    mm.then_inc(qturn_ok, 1)
                    pe.wait_ge(qT_ok, 2 * t + TB + j + 1)
                    pe.wait_ge(x2_ok, ONE + t + (j - 1 if j else 0))
                    for k in range(2):
                        mm = nc.tensor.matmul(ps_2[:, b, :], qT[:, b, k, :], qdn[:, k, :], start=(k == 0), stop=(k == 1))
                    mm.then_inc(down_ok, 1)
                for j in range(TB):
                    b = j % 2
                    pe.wait_ge(xn_ok, t + j + 1)
                    for k in range(4):
                        mm = nc.tensor.transpose(ps_3[:, b, k * P:(k + 1) * P], xn[:, j, k * P:(k + 1) * P], ident)
                    mm.then_inc(xturn_ok, 1)
                    pe.wait_ge(xT_ok, t + j + 1)
                    pe.wait_ge(row_ok, ONE + t + (j - 1 if j else 0))
                    for k in range(4):
                        mm = nc.tensor.matmul(ps_1[:, b, :], xT[:, b, k, :], wg[:, k, :], start=(k == 0), stop=(k == 3))
                    mm.then_inc(prod_ok, 1)

        @block.scalar
        def _(act):
            act.wait_ge(w_in, 16 * 8)
            nc.scalar.mul(w1s[:], w1s[:], float(1 / np.sqrt(2 * P)))
            nc.scalar.mul(w1v[:], w1v[:], float(1 / np.sqrt(2 * P)))
            nc.scalar.mul(w2s[:], w2s[:], float(1 / np.sqrt(P)))
            nc.scalar.mul(w2v[:], w2v[:], float(1 / np.sqrt(P))).then_inc(scaled, 1)
            act.wait_ge(ternary, 1)
            link = Link(act, link_a)
            with act.Fori(0, NBATCH) as i:
                t = i * TB
                link.enter(i, 2 * TB)
                for j in range(TB):
                    b = j % 2
                    act.wait_ge(first_ok, ONE + t + j + 1)
                    act.wait_ge(second_ok, ONE + t + (j - 1 if j else 0))
                    nc.scalar.copy(sT[:, b, 1:4, :], ps_1[:, b, P:].rearrange("p (k n) -> p k n", k=3)).then_inc(vT_ok, 1)
                    act.wait_ge(sT_ok, ONE + t + j)
                    link(nc.scalar.activation(soft[:], ps_1[:, b, 0:P], ACT.Abs))
                    link(nc.scalar.activation(soft[:], soft[:], ACT.Exp, scale=-1.0))
                    nc.scalar.activation(soft[:], soft[:], ACT.Ln, bias=half[:], scale=0.5).then_inc(soft_ok, 1)
                norms.root(act, 2 * i + 1)
                for j in range(TB):
                    b = j % 2
                    act.wait_ge(qturn_ok, 2 * t + j + 1)
                    act.wait_ge(up_ok, ONE + t + (j - 1 if j else 0))
                    nc.scalar.copy(qT[:, b], ps_b[:, b, 0:D].rearrange("p (k n) -> p k n", k=4)).then_inc(qT_ok, 1)
                    act.wait_ge(up_ok, ONE + t + j + 1)
                    nc.scalar.activation(hid[:, j, :], ps_3[:, b, 0:FF], ACT.Relu, scale=scal[:, 2, j:j + 1]).then_inc(relu_ok, 1)
                for j in range(TB):
                    b = j % 2
                    act.wait_ge(qturn_ok, 2 * t + TB + j + 1)
                    act.wait_ge(down_ok, ONE + t + (j - 1 if j else 0))
                    nc.scalar.copy(qT[:, b, 0:2], ps_b[:, b, 0:FF].rearrange("p (k n) -> p k n", k=2)).then_inc(qT_ok, 1)
                norms.root(act, 2 * i + 2)
                for j in range(TB):
                    b = j % 2
                    act.wait_ge(xturn_ok, t + j + 1)
                    act.wait_ge(prod_ok, ONE + t + (j - 1 if j else 0))
                    nc.scalar.copy(xT[:, b], ps_3[:, b].rearrange("p (k n) -> p k n", k=4)).then_inc(xT_ok, 1)
                    act.wait_ge(prod_ok, ONE + t + j + 1)
                    act.wait_ge(row_out[b], ONE_DMA + 16 * (uses(i, j) - 1))
                    nc.scalar.copy(row[:, b, :], ps_1[:, b, :]).then_inc(row_ok, 1)
                link.leave(NBATCH)

        @block.gpsimd
        def _(pool):
            pool.wait_ge(w_in, 16 * 8)
            with pool.Fori(0, NB) as t:
                pool.wait_ge(xn_ok, t + 1)
                nc.gpsimd.tensor_tensor(acc[:, ds(t, 1), :], acc[:, ds(t, 1), :], bias[:].unsqueeze(1), ALU.add)\
                  .then_inc(biased, 1)

        @block.vector
        def _(dve):
            link = Link(dve, link_d)
            nc.vector.memset(half[:], 0.5)
            link(nc.vector.memset(wsum[:], 0.0))
            link(nc.vector.memset(onesf[:], 1.0))
            link(nc.vector.tensor_copy(ident_b[:], ident))
            dve.wait_ge(w_in, 16 * 8)
            for k, w in ((0, wup), (1, wdn)):
                last = nc.vector.tensor_reduce(wsum[:, k:k + 1], w[:], AX.XY, ALU.add, apply_absolute_value=True)
                link(last)
            nc.vector.tensor_copy(wsum[:, 6:8], wsum[:, 0:2]).then_inc(measured, 1)
            dve.wait_ge(totals, 1)
            link(nc.vector.tensor_scalar(wsum[:, 2:4], ps_1[:, 0, 0:2], 1.0 / (D * FF), EPS, ALU.mult, ALU.max))
            link(nc.vector.reciprocal(wsum[:, 4:6], wsum[:, 2:4]))
            for k, w, q in ((0, wup, qup), (1, wdn, qdn)):
                link(nc.vector.tensor_scalar(w[:], w[:], wsum[:, 4 + k:5 + k], ROUND, ALU.mult, ALU.add))
                link(nc.vector.tensor_scalar(w[:], w[:], ROUND, 1.0, ALU.subtract, ALU.min))
                link(nc.vector.tensor_scalar(q[:], w[:], -1.0, None, ALU.max))
            nc.vector.tensor_scalar(wsum[:, 2:4], wsum[:, 2:4], 1.0 / 127.0, None, ALU.mult).then_inc(ternary, 1)
            dve.wait_ge(ternary, 1)
            dve.wait_ge(x_in, 16)

            def scales(a, k):
                link(nc.vector.tensor_scalar(scal[:, a, :], scal[:, a, :], EPS, None, ALU.max))
                link(nc.vector.reciprocal(scal[:, a + 1, :], scal[:, a, :]))
                nc.vector.tensor_scalar(scal[:, a + 1, :], scal[:, a + 1, :], 127.0, None, ALU.mult)
                link(nc.vector.tensor_scalar(scal[:, a + 2, :], scal[:, a, :], wsum[:, 2 + k:3 + k], None, ALU.mult))

            with dve.Fori(0, NBATCH) as i:
                t = i * TB
                link.enter(i, 2 * Norms.LINKS + 6 + 2 * TB + 3 * TB + TB)

                def row_of(j):
                    return acc[:, ds(t + j, 1), :].rearrange("p o d -> p (o d)")

                def add_graph(j):
                    dve.wait_ge(second_ok, ONE + t + j + 1)
                    a, o = row_of(j), ps_2[:, j % 2, :]
                    nc.vector.tensor_tensor(a[:, 0:P], a[:, 0:P], o[:, 0:P], ALU.add)
                    v = a[:, P:].rearrange("p (d c) -> p c d", c=3)
                    nc.vector.tensor_tensor(v, v, o[:, P:].rearrange("p (c d) -> p c d", c=3), ALU.add).then_inc(x1_ok, 1)
                    dve.wait_ge(x1_ok, ONE + t + j + 1)
                    norms.tile(dve, j, a)

                for j in range(TB):
                    dve.wait_ge(soft_ok, t + j + 1)
                    dve.wait_ge(second_ok, ONE + t + (j - 1 if j else 0))
                    nc.vector.scalar_tensor_tensor(out=sT[:, j % 2, 0, :], in0=ps_1[:, j % 2, 0:P], scalar=0.0,
                                                   in1=soft[:], op0=ALU.max, op1=ALU.add).then_inc(sT_ok, 1)
                    if j:
                        add_graph(j - 1)
                add_graph(TB - 1)
                norms.scale(dve, link, 2 * t + TB, 2 * i + 1)
                for j in range(TB):
                    link(norms.apply(xn[:, j, :], row_of(j), j))
                    link(nc.vector.tensor_reduce(scal[:, 0, j:j + 1], xn[:, j, :], AX.X, ALU.max, apply_absolute_value=True))
                scales(0, 0)
                for j in range(TB):
                    b = j % 2
                    if j >= 2:
                        dve.wait_ge(qturn_ok, 2 * t + j - 1)
                    link(nc.vector.tensor_scalar(tmp[:, b, :], xn[:, j, :], scal[:, 1, j:j + 1], ROUND, ALU.mult, ALU.add))
                    nc.vector.tensor_scalar(qb[:, b, :], tmp[:, b, :], ROUND, 127.0, ALU.subtract, ALU.min).then_inc(q_ok, 1)
                for j in range(TB):
                    dve.wait_ge(relu_ok, t + j + 1)
                    link(nc.vector.tensor_scalar(hid[:, j, :], hid[:, j, :], ROUND, ROUND, ALU.add, ALU.subtract))
                    link(nc.vector.tensor_scalar(hid[:, j, :], hid[:, j, :], 127.0, 0.0, ALU.min, ALU.max,
                                                 accum_out=scal[:, 3, j:j + 1]))
                scales(3, 1)

                def add_ffn(j):
                    dve.wait_ge(down_ok, ONE + t + j + 1)
                    a = row_of(j)
                    nc.vector.scalar_tensor_tensor(out=a, in0=ps_2[:, j % 2, :], scalar=scal[:, 5, j:j + 1], in1=a,
                                                   op0=ALU.mult, op1=ALU.add).then_inc(x2_ok, 1)
                    dve.wait_ge(x2_ok, ONE + t + j + 1)
                    norms.tile(dve, j, a)

                for j in range(TB):
                    b = j % 2
                    if j >= 2:
                        dve.wait_ge(qturn_ok, 2 * t + TB + j - 1)
                    link(nc.vector.tensor_scalar(tmp[:, b, 0:FF], hid[:, j, :], scal[:, 4, j:j + 1], ROUND, ALU.mult, ALU.add))
                    nc.vector.tensor_scalar(qb[:, b, 0:FF], tmp[:, b, 0:FF], ROUND, 127.0, ALU.subtract, ALU.min).then_inc(q2_ok, 1)
                    if j:
                        add_ffn(j - 1)
                add_ffn(TB - 1)
                norms.scale(dve, link, 2 * t + 2 * TB, 2 * i + 2)
                for j in range(TB):
                    norms.apply(xn[:, j, :], row_of(j), j).then_inc(xn_ok, 1)
                link.leave(NBATCH)
            dve.wait_ge(biased, NB)


def neighbour_sums(nc, io, shared):
    with ExitStack() as ctx:
        m = Space(nc, ctx, "p4")
        const, bkt_i, acc = shared["const"], shared["bkt_i"], shared["acc"]
        iota = const[:, C_IOTA:C_IOTA + P]
        rec = m.sb("rec", [P, 2, 2, 2, REC])
        got = m.sb("got", [P, 2, 4, D])
        high = m.sb("high", [P, 4, D], F32R)
        low = m.sb("low", [P, 4, D], F32R)
        hot = m.sb("hot", [P, 4, P], F32R)
        blank = m.sb("blank", [P, 512], BF16)
        ps_a = m.psum("ps_a", [P, 4, 512])
        rec_in = [m.sem(f"rec_in{k}") for k in range(2)]
        got_in = [[m.sem(f"got_in{k}{c}") for c in range(4)] for k in range(2)]
        passed = m.sem("passed")
        blank_ok = m.sem("blank_ok")
        high_ok = m.sem("high_ok")
        low_ok = m.sem("low_ok")
        spent = m.primed("spent")
        added = m.primed("added")
        block = ctx.enter_context(nc.Block())

        def load_records(sp, q, k):
            row = ds(q * 4 * P, 4 * P) if not isinstance(q, int) else slice(q * 4 * P, (q + 1) * 4 * P)
            sp.dma_start(rec[:, k].rearrange("p g j w -> p g (j w)"),
                         io["sorted"][row, :].rearrange("(g p j) w -> p g (j w)", g=2, j=2)).then_inc(rec_in[k], 16)

        @block.sync
        def _(sp):
            m.prime(sp, io)
            load_records(sp, 0, 0)
            load_records(sp, 1, 1)
            with sp.Fori(0, NQ // 2) as i:
                for u in range(2):
                    sp.wait_ge(low_ok, 8 * i + 4 * u + 4)
                    load_records(sp, 2 * i + u + 2, u)
            for k in range(2):
                sp.wait_ge(rec_in[k], 16 * (NQ // 2 + 1))

        @block.gpsimd
        def _(pool):
            def gather(k, c):
                nc.gpsimd.indirect_dma_start(
                    out=got[:, k, c, :], out_offset=None, in_=io["table_b"],
                    in_offset=bass.IndirectOffsetOnAxis(
                        ap=rec[:, k, c // 2, c % 2, R_DST:R_DST + 1].bitcast(U32), axis=0)).then_inc(got_in[k][c], 16)

            for k in range(2):
                pool.wait_ge(rec_in[k], 16)
                for c in range(4):
                    gather(k, c)
            with pool.Fori(1, NQ // 2) as i:
                for k in range(2):
                    pool.wait_ge(rec_in[k], 16 * i + 16)
                    for c in range(4):
                        pool.wait_ge(low_ok, 8 * i + 4 * k + c - 7)
                        pool.sem_inc(passed, 1)
                        gather(k, c)

        @block.tensor
        def _(pe):
            pe.wait_ge(blank_ok, 1)
            nc.tensor.matmul(ps_a[:, 3, :], blank[:, 0:P], blank[:], start=True, stop=True).then_inc(spent, 1)
            with pe.Fori(0, NQ // 2) as i:
                for c in range(8):
                    q, g = c % 4, c // 2
                    pe.wait_ge(low_ok, 8 * i + c + 1)
                    if c % 2 == 0:
                        pe.wait_ge(added, ONE + 4 * i + g - 2)
                    nc.tensor.matmul(ps_a[:, g, :], hot[:, q, :], high[:, q, :], start=(c % 2 == 0), stop=False)
                    nc.tensor.matmul(ps_a[:, g, :], hot[:, q, :], low[:, q, :], start=False, stop=(c % 2 == 1))\
                      .then_inc(spent, 1)

        @block.scalar
        def _(act):
            with act.Fori(0, NQ // 2) as i:
                for c in range(8):
                    k, q, b = c // 4, c % 4, c % 2
                    act.wait_ge(got_in[k][q], 16 * i + 16)
                    act.wait_ge(spent, ONE + 8 * i + c - 2)
                    nc.scalar.mul(high[:, q, :], got[:, k, q, :], rec[:, k, q // 2, b, R_CUT:R_CUT + 1])\
                      .then_inc(high_ok, 1)

        @block.vector
        def _(dve):
            nc.vector.memset(blank[:], 0.0).then_inc(blank_ok, 1)

            def add_group(entry, k):
                dve.wait_ge(spent, ONE + 2 * entry + 1)
                at = dve.value_load(bkt_i[0:1, ds(entry, 1)], min_val=0, max_val=NB - 1)
                a = acc[:, ds(at, 1), :].rearrange("p o d -> p (o d)")
                dve.wait_ge(added, ONE + entry)
                nc.vector.tensor_tensor(a, a, ps_a[:, k, :], ALU.add).then_inc(added, 1)

            with dve.Fori(0, NQ // 2) as i:
                for c in range(8):
                    k, q, b = c // 4, c % 4, c % 2
                    word = rec[:, k, q // 2, b]
                    dve.wait_ge(spent, ONE + 8 * i + c - 2)
                    dve.wait_ge(high_ok, 8 * i + c + 1)
                    nc.vector.tensor_scalar(hot[:, q, :], iota, word[:, R_TGT:R_TGT + 1], None, ALU.is_equal)
                    nc.vector.scalar_tensor_tensor(out=low[:, q, :], in0=got[:, k, q, :], scalar=word[:, R_CUT:R_CUT + 1],
                                                   in1=high[:, q, :].bitcast(F32), op0=ALU.mult, op1=ALU.subtract)\
                      .then_inc(low_ok, 1)
                    if b == 1:
                        add_group(4 * i + c // 2, (c // 2 - 1) % 4)
            add_group(NG, 3)
            dve.wait_ge(added, ONE + NG + 1)


def experts(nc, io, shared):
    with ExitStack() as ctx:
        m = Space(nc, ctx, "p5")
        const, acc = shared["const"], shared["acc"]
        ident = const[:, C_ID:C_ID + P]
        TB = 7
        NBATCH = NB // TB
        HALF = TB * P // 2
        E = N_EXP
        w1 = m.sb("w1", [P, E, 4, FF])
        w2 = m.sb("w2", [P, E, 2, D])
        b1 = m.sb("b1", [P, E, 2])
        b2 = m.sb("b2", [E, D])
        rw = m.sb("rw", [P, 4, E])
        rb = m.sb("rb", [P, 1, E])
        lower = m.sb("lower", [P, 1, E * E])
        xn = m.sb("xn", [P, 2, D])
        xT = m.sb("xT", [P, 4, TB * P])
        hT = m.sb("hT", [P, 2, 2, TB * P])
        prob = m.sb("prob", [P, TB, E])
        comb = m.sb("comb", [P, TB, E])
        cmp1, cmp2 = (xn[:, k, 0:TB * E * E].rearrange("p (j e f) -> p j e f", j=TB, e=E) for k in range(2))
        red = m.sb("red", [P, 3, TB])
        combT = m.sb("combT", [E, TB * P])
        norms = Norms(nc, m, TB)
        ps_t = m.psum("ps_t", [P, 2, 512])
        ps_l = m.psum("ps_l", [P, 512])
        ps_c = m.psum("ps_c", [P, 512])
        ps_h = m.psum("ps_h", [P, 2, 512])
        ps_y = m.psum("ps_y", [P, 2, 512])

        w_in = m.sem("w_in")
        link_d = m.sem("link_d")
        xn_ok = m.sem("xn_ok")
        turned = m.sem("turned")
        xT_ok = m.sem("xT_ok")
        logits_ok = m.sem("logits_ok")
        shifted = m.sem("shifted")
        exp_ok = m.sem("exp_ok")
        weight_ok = m.sem("weight_ok")
        comb_ok = m.sem("comb_ok")
        cturned = m.sem("cturned")
        combT_ok = m.sem("combT_ok")
        pre_ok = m.sem("pre_ok")
        act_ok = m.primed("act_ok")
        y_ok = m.sem("y_ok")
        y_added = m.primed("y_added")
        out_ok = m.sem("out_ok")
        NY = (E + 1) * TB
        NH = E * 4

        block = ctx.enter_context(nc.Block())

        @block.sync
        def _(sp):
            m.prime(sp, io)
            for tile, name in ((rw, "rw"), (b1, "b1"), (b2, "b2"), (w1, "ew1"), (w2, "ew2")):
                sp.dma_start(tile[:], io[name]).then_inc(w_in, 16)
            sp.dma_start(rb[:, 0, :], io["rb"].to_broadcast([P, E])).then_inc(w_in, 16)
            sp.dma_start(lower[:, 0, :], io["lower"].to_broadcast([P, E * E])).then_inc(w_in, 16)
            with sp.Fori(0, NBATCH) as i:
                sp.wait_ge(y_added, ONE + (i + 1) * NY)
                sp.dma_start(io["out"][ds(i * TB * P, TB * P), :].rearrange("(t p) d -> p t d", p=P),
                             acc[:, ds(i * TB, TB), :]).then_inc(out_ok, 16)
            sp.wait_ge(out_ok, 16 * NBATCH)

        @block.tensor
        def _(pe):
            pe.wait_ge(w_in, 16 * 7)
            with pe.Fori(0, NBATCH) as i:
                for j in range(TB):
                    b = j % 2
                    pe.wait_ge(xn_ok, i * TB + j + 1)
                    if j >= 2:
                        pe.wait_ge(xT_ok, i * TB + j - 1)
                    for k in range(4):
                        mm = nc.tensor.transpose(ps_t[:, b, k * P:(k + 1) * P], xn[:, b, k * P:(k + 1) * P], ident)
                    mm.then_inc(turned, 1)
                for j in range(TB):
                    pe.wait_ge(xT_ok, i * TB + j + 1)
                    for k in range(4):
                        mm = nc.tensor.matmul(ps_l[:, j * E:(j + 1) * E], xT[:, k, j * P:(j + 1) * P], rw[:, k, :],
                                              start=(k == 0), stop=(k == 3))
                mm.then_inc(logits_ok, 1)

                def hidden(e):
                    for part in range(4):
                        f, half = part // 2, part % 2
                        pe.wait_ge(act_ok, ONE + i * NH + max(e * 4 + part - 1, 0))
                        for k in range(4):
                            mm = nc.tensor.matmul(ps_h[:, part % 2, 0:HALF], w1[:, e, k, f * P:(f + 1) * P],
                                                  xT[:, k, half * HALF:(half + 1) * HALF],
                                                  start=(k == 0), stop=(k == 3))
                        mm.then_inc(pre_ok, 1)

                hidden(0)
                pe.wait_ge(comb_ok, i + 1)
                for half in range(2):
                    for j in range(4 * half, min(TB, 4 * half + 4)):
                        mm = nc.tensor.transpose(ps_c[0:E, (j % 4) * P:(j % 4 + 1) * P], comb[:, j, :], ident)
                    mm.then_inc(cturned, 1)
                    pe.wait_ge(combT_ok, 2 * i + half + 1)
                for j in range(TB):
                    pe.wait_ge(y_added, ONE + i * NY + max(j - 1, 0))
                    nc.tensor.matmul(ps_y[:, j % 2, :], combT[:, j * P:(j + 1) * P], b2[:], start=True, stop=True)\
                      .then_inc(y_ok, 1)
                for e in range(E):
                    if e + 1 < E:
                        hidden(e + 1)
                    pe.wait_ge(act_ok, ONE + i * NH + 4 * e + 4)
                    for j in range(TB):
                        n = (e + 1) * TB + j
                        pe.wait_ge(y_added, ONE + i * NY + n - 1)
                        for f in range(2):
                            mm = nc.tensor.matmul(ps_y[:, n % 2, :], hT[:, e % 2, f, j * P:(j + 1) * P], w2[:, e, f, :],
                                                  start=(f == 0), stop=(f == 1))
                        mm.then_inc(y_ok, 1)

        @block.scalar
        def _(act):
            act.wait_ge(w_in, 16 * 7)
            with act.Fori(0, NBATCH) as i:
                norms.root(act, i + 1)
                for j in range(TB):
                    act.wait_ge(turned, i * TB + j + 1)
                    nc.scalar.copy(xT[:, :, j * P:(j + 1) * P],
                                   ps_t[:, j % 2, :].rearrange("p (k n) -> p k n", k=4)).then_inc(xT_ok, 1)
                act.wait_ge(shifted, i + 1)
                nc.scalar.activation(prob[:], prob[:], ACT.Exp).then_inc(exp_ok, 1)

                def gelu(e):
                    for part in range(4):
                        f, half = part // 2, part % 2
                        act.wait_ge(pre_ok, i * NH + e * 4 + part + 1)
                        if e >= 2 and part == 0:
                            act.wait_ge(y_ok, i * NY + e * TB)
                        nc.scalar.activation(hT[:, e % 2, f, half * HALF:(half + 1) * HALF], ps_h[:, part % 2, 0:HALF],
                                             ACT.Gelu, bias=b1[:, e, f:f + 1]).then_inc(act_ok, 1)

                gelu(0)
                for half in range(2):
                    n = min(4, TB - 4 * half) * P
                    act.wait_ge(cturned, 2 * i + half + 1)
                    nc.scalar.copy(combT[:, 4 * half * P:4 * half * P + n], ps_c[0:E, 0:n]).then_inc(combT_ok, 1)
                for e in range(1, E):
                    gelu(e)

        @block.vector
        def _(dve):
            link = Link(dve, link_d)
            dve.wait_ge(w_in, 16 * 7)
            with dve.Fori(0, NBATCH) as i:
                link.enter(i, Norms.LINKS + 14)

                def row_of(j):
                    return acc[:, ds(i * TB + j, 1), :].rearrange("p o d -> p (o d)")

                for j in range(TB):
                    norms.tile(dve, j, row_of(j))
                norms.scale(dve, link, (i + 1) * TB, i + 1)
                for j in range(TB):
                    if j >= 2:
                        dve.wait_ge(turned, i * TB + j - 1)
                    norms.apply(xn[:, j % 2, :], row_of(j), j).then_inc(xn_ok, 1)
                dve.wait_ge(logits_ok, i + 1)
                over = [P, TB, E]
                link(nc.vector.tensor_tensor(prob[:], ps_l[:, 0:TB * E].rearrange("p (j e) -> p j e", j=TB),
                                             rb[:].to_broadcast(over), ALU.add))
                link(nc.vector.tensor_reduce(red[:, 0, :], prob[:], AX.X, ALU.max))
                nc.vector.tensor_tensor(prob[:], prob[:], red[:, 0, :].unsqueeze(2).to_broadcast(over),
                                        ALU.subtract).then_inc(shifted, 1)
                dve.wait_ge(exp_ok, i + 1)
                link(nc.vector.tensor_reduce(red[:, 1, :], prob[:], AX.X, ALU.add))
                link(nc.vector.reciprocal(red[:, 2, :], red[:, 1, :]))
                link(nc.vector.tensor_tensor(prob[:], prob[:], red[:, 2, :].unsqueeze(2).to_broadcast(over), ALU.mult))
                mine = prob[:].unsqueeze(3).to_broadcast([P, TB, E, E])
                other = prob[:].unsqueeze(2).to_broadcast([P, TB, E, E])
                link(nc.vector.tensor_tensor(cmp1, other, mine, ALU.is_gt))
                link(nc.vector.tensor_tensor(cmp2, other, mine, ALU.is_equal))
                flat1, flat2 = (xn[:, k, 0:TB * E * E].rearrange("p (j q) -> p j q", j=TB) for k in range(2))
                link(nc.vector.tensor_tensor(flat2, flat2, lower[:].to_broadcast([P, TB, E * E]), ALU.mult))
                link(nc.vector.tensor_tensor(flat1, flat1, flat2, ALU.add))
                link(nc.vector.tensor_reduce(comb[:], cmp1, AX.X, ALU.add))
                link(nc.vector.tensor_scalar(comb[:], comb[:], 2.0, None, ALU.is_lt))
                link(nc.vector.tensor_tensor(comb[:], comb[:], prob[:], ALU.mult))
                link(nc.vector.tensor_reduce(red[:, 1, :], comb[:], AX.X, ALU.add))
                link(nc.vector.tensor_scalar(red[:, 1, :], red[:, 1, :], 1e-9, None, ALU.add))
                nc.vector.reciprocal(red[:, 2, :], red[:, 1, :]).then_inc(weight_ok, 1)
                dve.wait_ge(weight_ok, i + 1)
                nc.vector.tensor_tensor(comb[:], comb[:], red[:, 2, :].unsqueeze(2).to_broadcast(over),
                                        ALU.mult).then_inc(comb_ok, 1)
                dve.wait_ge(comb_ok, i + 1)
                for e in range(-1, E):
                    for j in range(TB):
                        n = (e + 1) * TB + j
                        dve.wait_ge(y_ok, i * NY + n + 1)
                        a = row_of(j)
                        dve.wait_ge(y_added, ONE + i * NY + max(n - TB + 1, 0))
                        if e < 0:
                            nc.vector.tensor_tensor(a, ps_y[:, n % 2, :], a, ALU.add).then_inc(y_added, 1)
                        else:
                            nc.vector.scalar_tensor_tensor(out=a, in0=ps_y[:, n % 2, :], scalar=comb[:, j, e:e + 1],
                                                           in1=a, op0=ALU.mult, op1=ALU.add).then_inc(y_added, 1)
                link.leave(NBATCH)


def program(nc, io):
    with ExitStack() as ctx:
        m = Space(nc, ctx, "all")
        shared = {
            "const": m.sb("const", [P, C_KEPT]),
            "bkt_i": m.sb("bkt_i", [P, NG + 1], I32),
            "keep": m.sb("keep", [P, NG + 1]),
        }
        sort_and_embed(nc, io, shared)
        edge_sums(nc, io, shared)
        shared["acc"] = m.sb("acc", [P, NB, D])
        node_layers(nc, io, shared)
        neighbour_sums(nc, io, shared)
        experts(nc, io, shared)


def filter_order(w):
    w = w[:, :4 * P].reshape(-1, 2, P, 2)
    return np.ascontiguousarray(np.concatenate([w[:, 0, :, 0], w[:, 1, :, 0], w[:, 0, :, 1], w[:, 1, :, 1]], axis=1))


def chunks(w):
    return np.ascontiguousarray(w.reshape(-1, P, w.shape[1]).transpose(1, 0, 2))


def lay_out(a):
    f = np.float32
    consts = np.zeros((P, C_END), f)
    consts[:, C_ID:C_ID + P] = np.eye(P)
    consts[:, C_TRI:C_TRI + P] = np.triu(np.ones((P, P)), 1)
    consts[:, C_IOTA:C_IOTA + P] = np.arange(P)
    consts[:, C_BKT:C_BKT + 64] = np.arange(64)
    consts[:, C_GRP:C_END] = np.arange(C_END - C_GRP)
    x = np.zeros((NPAD + P, D), f)
    x[:N_NODES] = a["x"]
    src = np.full(EPAD, NPAD, np.int32)
    src[:N_EDGES] = a["src"]
    dst = np.zeros(EPAD, np.int32)
    dst[:N_EDGES] = a["dst"]
    edges = np.zeros((EPAD, REC), f)
    edges[:, R_Y] = 1
    edges[:N_EDGES, 0:N_RBF] = a["edge_attr_20"]
    edges[:N_EDGES, R_ONE] = 1
    edges[:N_EDGES, R_Y:R_Y + 3] = a["edge_attr_3"]
    edges[:N_EDGES, R_CUT] = a["edge_weight"]
    return {
        "consts": consts, "x": x, "src": src.reshape(P, COLS), "dst": dst.reshape(P, COLS),
        "edges": edges.reshape(P, COLS, REC),
        "wf1": np.concatenate([a["L0_gnn_Wf1"], np.asarray(a["L0_gnn_bf1"])[None]]),
        "wf2": filter_order(np.asarray(a["L0_gnn_Wf2"])), "bf2": filter_order(np.asarray(a["L0_gnn_bf2"])[None]),
        "w1s": np.asarray(a["L0_gnn_W1_s"]).reshape(P, 2, P), "w1v": np.asarray(a["L0_gnn_W1_v"]).reshape(P, 2, P),
        "w2s": np.asarray(a["L0_gnn_W2_s"]), "w2v": np.asarray(a["L0_gnn_W2_v"]),
        "wup": chunks(np.asarray(a["L0_ffn_w_up"]).T), "wdn": chunks(np.asarray(a["L0_ffn_w_down"]).T),
        "wg": chunks(np.asarray(a["L1_gnn_weight"])), "gnn_bias": np.asarray(a["L1_gnn_bias"])[None],
        "ew1": np.ascontiguousarray(np.asarray(a["L1_ffn_W1"]).reshape(N_EXP, 4, P, FF).transpose(2, 0, 1, 3)),
        "ew2": np.ascontiguousarray(np.asarray(a["L1_ffn_W2"]).reshape(N_EXP, 2, P, D).transpose(2, 0, 1, 3)),
        "b1": np.ascontiguousarray(np.asarray(a["L1_ffn_b1"]).reshape(N_EXP, 2, P).transpose(2, 0, 1)),
        "b2": np.asarray(a["L1_ffn_b2"]), "rw": chunks(np.asarray(a["L1_ffn_router_w"])),
        "rb": np.asarray(a["L1_ffn_router_b"])[None],
        "lower": np.tril(np.ones((N_EXP, N_EXP), f), -1).reshape(1, -1),
        "w_in_s": np.asarray(a["L0_gnn_W_in2f_s"]), "w_in_v": np.asarray(a["L0_gnn_W_in2f_v"]),
    }


SCRATCH = {"sorted": [NG_ROWS * GE, REC], "table_a": [NPAD, D], "agg": [NPAD, 2 * D], "table_b": [NPAD, D]}


def kernel(**inputs):
    import concourse.bacc as bacc
    from concourse.bass_utils import run_bass_kernel_spmd

    nc = bacc.Bacc("TRN2", target_bir_lowering=False, num_devices=1)
    arrays = {f"in_{k}": np.ascontiguousarray(v) for k, v in lay_out({k: np.asarray(v) for k, v in inputs.items()}).items()}
    io = {k[3:]: nc.dram_tensor(k, v.shape, mybir.dt.from_np(v.dtype), kind="ExternalInput").ap()
          for k, v in arrays.items()}
    for k, shape in SCRATCH.items():
        io[k] = nc.dram_tensor(k, shape, F32).ap()
    io["out"] = nc.dram_tensor("out", [NPAD, D], F32, kind="ExternalOutput").ap()
    program(nc, io)
    result = run_bass_kernel_spmd(nc, [arrays], core_ids=[0])
    return result.results[0]["out"][:N_NODES]
```

```python
from contextlib import ExitStack

import numpy as np

import concourse.bass as bass
from concourse import mybir
from concourse.bass import ds

ALU = mybir.AluOpType
ACT = mybir.ActivationFunctionType
AX = mybir.AxisListType
F32 = mybir.dt.float32
F32R = mybir.dt.float32r
BF16 = mybir.dt.bfloat16
I32 = mybir.dt.int32
U32 = mybir.dt.uint32

P = 128
D = 512
N_NODES = 6250
N_EDGES = 100000
N_RBF = 20
FF = 256
N_EXP = 8

NB = -(-N_NODES // P)
NPAD = NB * P
COLS = 8 * (-(-N_EDGES // (8 * P)))
EPAD = COLS * P
NBKT = NB + 1
GC = 2
GE = GC * P
NG = 2 * (-(-((N_EDGES + NB * (GE - 1)) // GE) // 2))
NQ = NG // 2
NG_ROWS = NG + 8
assert EPAD - N_EDGES <= 2 * GE and NQ % 2 == 0
NT = 2 * (-(-((2 * NPAD + N_EXP * (P - 1)) // P) // 2))
REC = 32

R_ONE, R_Y, R_CUT, R_TGT, R_DST = 20, 21, 24, 25, 26

C_ID, C_IOTA, C_KEPT = 0, 128, 256
C_TRI, C_BKT, C_GRP, C_END = 256, 384, 448, 448 + NG + 8

EPS = 1e-5
Y0 = float(1.0 / np.sqrt(4.0 * np.pi))
Y1_SCALE = float(np.sqrt(3.0 / (4.0 * np.pi)))
ROUND = 12582912.0


class Link:

    def __init__(self, eng, sem):
        self.eng, self.sem, self.base, self.n = eng, sem, 0, 0

    def __call__(self, ins):
        self.n += 1
        ins.then_inc(self.sem, 1)
        self.eng.wait_ge(self.sem, self.base + self.n)

    def enter(self, i, per):
        self.start, self.per = self.base + self.n, per
        self.base, self.n = self.start + i * per, 0

    def leave(self, count):
        assert self.n == self.per, (self.n, self.per)
        self.base, self.n = self.start + count * self.per, 0


ONE = 4
ONE_DMA = 16


class Space:

    def __init__(self, nc, ctx, tag):
        self.nc, self.ctx, self.tag = nc, ctx, tag
        self.sems, self.dma_sems = [], []

    def sb(self, name, shape, dt=F32):
        return self.ctx.enter_context(self.nc.sbuf_tensor(f"{self.tag}_{name}", shape, dt))

    def psum(self, name, shape, dt=F32):
        return self.ctx.enter_context(self.nc.psum_tensor(f"{self.tag}_{name}", shape, dt))

    def sem(self, name):
        return self.ctx.enter_context(self.nc.semaphore(f"{self.tag}_{name}"))

    def primed(self, name):
        self.sems.append(self.sem(name))
        return self.sems[-1]

    def primed_dma(self, name):
        self.dma_sems.append(self.sem(name))
        return self.dma_sems[-1]

    def prime(self, sp, io, start_word=None):
        for sem in self.sems:
            sp.sem_inc(sem, ONE)
        for k, sem in enumerate(self.dma_sems):
            sp.dma_start(start_word[:, 2 * k:2 * k + 2], io["consts"][:, 0:2]).then_inc(sem, ONE_DMA)


def sort_and_embed(nc, io, shared):
    with ExitStack() as ctx:
        m = Space(nc, ctx, "p1")
        const = m.sb("const", [P, C_END])
        bkt_f = m.sb("bkt_f", [P, NG + 1])
        ident = const[:, C_ID:C_ID + P]
        rec = m.sb("rec", [P, COLS, REC])
        src = m.sb("src", [P, COLS], I32)
        dst = m.sb("dst", [P, COLS], I32)
        work_i = m.sb("work_i", [P, COLS], I32)
        bucket = m.sb("bucket", [P, COLS])
        match = m.sb("match", [P, COLS])
        place = m.sb("place", [P, COLS])
        pos = m.sb("pos", [P, COLS])
        pos_u = m.sb("pos_u", [P, COLS], U32)
        zero = m.sb("zero", [P, COLS])
        count = m.sb("count", [P, 64])
        before = m.sb("before", [P, 64])
        total_i = m.sb("total_i", [P, 64], I32)
        groups = m.sb("groups", [P, 64])
        first = m.sb("first", [P, 64])
        norm = m.sb("norm", [P, COLS])
        pad = m.sb("pad", [P, 4, REC])
        stage = m.sb("stage", [P, 2, 8, REC])
        stage_at = m.sb("stage_at", [P, 2, 8], U32)
        xt = m.sb("xt", [P, 2, D])
        xn = m.sb("xn", [P, D])
        xT = m.sb("xT", [P, 4, P])
        row = m.sb("row", [P, 2, D])
        stats = m.sb("stats", [P, 8])
        mv = m.sb("mv", [P, 4])
        w_s = m.sb("w_s", [P, P])
        w_v = m.sb("w_v", [P, P])
        eps = m.sb("eps", [P, 1])
        ones = m.sb("ones", [P, P])
        zeros = m.sb("zeros", [P, 2 * D])
        ps_c = m.psum("ps_c", [P, 2, 512])
        ps_t = m.psum("ps_t", [P, 4, P])
        ps_o = m.psum("ps_o", [P, 4, P])

        loaded = m.sem("loaded")
        rec_loaded = m.sem("rec_loaded")
        w_loaded = m.sem("w_loaded")
        link_d = m.sem("link_d")
        ready = m.sem("ready")
        squares = m.sem("squares")
        lengths = m.sem("lengths")
        counted = m.sem("counted")
        summed = m.sem("summed")
        placed = m.sem("placed")
        cleared = m.sem("cleared")
        pad_made = m.sem("pad_made")
        padded = m.sem("padded")
        staged = m.sem("staged")
        scattered = [m.sem(f"scattered{k}") for k in range(2)]
        x_in = [m.sem(f"x_in{k}") for k in range(2)]
        x_free = m.sem("x_free")
        stats_ok = m.sem("stats_ok")
        var_ok = m.sem("var_ok")
        std_ok = m.sem("std_ok")
        xn_ok = m.sem("xn_ok")
        turned = m.sem("turned")
        xT_ok = m.sem("xT_ok")
        embedded = m.sem("embedded")
        row_ok = m.primed("row_ok")
        row_out = [m.primed_dma(f"row_out{k}") for k in range(2)]
        scaled = m.sem("scaled")

        start_word = m.sb("start_word", [P, 2 * len(m.dma_sems)])
        block = ctx.enter_context(nc.Block())

        @block.sync
        def _(sp):
            m.prime(sp, io, start_word)
            sp.dma_start(const[:], io["consts"]).then_inc(loaded, 16)
            sp.dma_start(src[:], io["src"]).then_inc(loaded, 16)
            sp.dma_start(dst[:], io["dst"]).then_inc(loaded, 16)
            sp.dma_start(rec[:], io["edges"]).then_inc(rec_loaded, 16)
            sp.dma_start(w_s[:], io["w_in_s"]).then_inc(w_loaded, 16)
            sp.dma_start(w_v[:], io["w_in_v"]).then_inc(w_loaded, 16)
            sp.wait_ge(pad_made, 2)
            with sp.Fori(0, NG_ROWS // 2) as g:
                sp.dma_start(io["sorted"][ds(g * 4 * P, 4 * P), :].rearrange("(p j) w -> p (j w)", j=4),
                             pad[:].rearrange("p j w -> p (j w)")).then_inc(padded, 16)
            sp.wait_ge(ready, 2)
            with sp.Fori(0, NB) as b:
                sp.dma_start(io["agg"][ds(b * P, P), :], zeros[:]).then_inc(cleared, 16)
            with sp.Fori(0, NT // 2) as b:
                sp.dma_start(io["packed"][ds(b * 2 * P, 2 * P), :].rearrange("(p j) w -> p (j w)", j=2),
                             zeros[:]).then_inc(cleared, 16)
            for k in range(2):
                sp.dma_start(xt[:, k, :], io["x"][k * P:(k + 1) * P, :]).then_inc(x_in[k], 16)
            with sp.Fori(0, (NB - 1) // 2) as t:
                for k in range(2):
                    sp.wait_ge(row_ok, ONE + 2 * t + k + 1)
                    sp.dma_start(io["table_a"][ds((2 * t + k) * P, P), :],
                                 row[:, k, :]).then_inc(row_out[k], 16)
                    sp.wait_ge(xn_ok, 2 * t + k + 1)
                    sp.dma_start(xt[:, k, :], io["x"][ds((2 * t + 2 + k) * P, P), :]).then_inc(x_in[k], 16)
            sp.wait_ge(row_ok, ONE + NB)
            sp.dma_start(io["table_a"][(NB - 1) * P:NB * P, :], row[:, 0, :]).then_inc(row_out[0], 16)
            sp.wait_ge(row_out[0], ONE_DMA + 16 * (NB // 2 + 1))
            sp.wait_ge(row_out[1], ONE_DMA + 16 * (NB // 2))
            sp.wait_ge(x_in[1], 16 * (NB // 2 + 1))
            sp.wait_ge(cleared, 16 * (NB + NT // 2))

        @block.gpsimd
        def _(pool):
            nc.gpsimd.memset(pad[:], 0.0).then_inc(pad_made, 1)
            pool.wait_ge(pad_made, 1)
            nc.gpsimd.memset(pad[:, :, R_Y:R_Y + 1], 1.0).then_inc(pad_made, 1)
            pool.wait_ge(placed, 1)
            pool.wait_ge(padded, 16 * (NG_ROWS // 2))

            def scatter(q, k):
                col = q * 16 + k * 8
                cols = slice(col, col + 8) if isinstance(q, int) else ds(col, 8)
                nc.gpsimd.tensor_copy(stage[:, k], rec[:, cols, :]).then_inc(staged, 1)
                nc.gpsimd.tensor_copy(stage_at[:, k], pos_u[:, cols]).then_inc(staged, 1)
                pool.wait_ge(staged, q * 4 + k * 2 + 2)
                pool.sem_inc(shared["passed"], 1)
                for c in range(8):
                    nc.gpsimd.indirect_dma_start(
                        out=io["sorted"], out_offset=bass.IndirectOffsetOnAxis(ap=stage_at[:, k, c:c + 1], axis=0),
                        in_=stage[:, k, c, :], in_offset=None).then_inc(scattered[k], 16)

            scatter(0, 0)
            scatter(0, 1)
            with pool.Fori(1, COLS // 16) as q:
                for k in range(2):
                    pool.wait_ge(scattered[k], q * 128)
                    scatter(q, k)
            for k in range(2):
                pool.wait_ge(scattered[k], (COLS // 16) * 128)

        @block.tensor
        def _(pe):
            pe.wait_ge(counted, 1)
            nc.tensor.matmul(ps_c[:, 0, 0:64], const[:, C_TRI:C_TRI + P], count[:], start=True, stop=True)
            nc.tensor.matmul(ps_c[:, 1, 0:64], ones[:], count[:], start=True, stop=True).then_inc(summed, 1)
            pe.wait_ge(scaled, 2)
            with pe.Fori(0, NB) as t:
                pe.wait_ge(xn_ok, t + 1)
                for k in range(4):
                    part = xn[:, 0:P] if k == 0 else xn[:, P + k - 1:D:3]
                    mm = nc.tensor.transpose(ps_t[:, k, :], part, ident)
                mm.then_inc(turned, 1)
                pe.wait_ge(xT_ok, t + 1)
                pe.wait_ge(row_ok, ONE + t)
                for k in range(4):
                    mm = nc.tensor.matmul(ps_o[:, k, :], xT[:, k, :], (w_s if k == 0 else w_v)[:],
                                          start=True, stop=True)
                mm.then_inc(embedded, 1)

        @block.scalar
        def _(act):
            act.wait_ge(w_loaded, 32)
            nc.scalar.mul(w_s[:], w_s[:], float(1 / np.sqrt(P))).then_inc(scaled, 1)
            nc.scalar.mul(w_v[:], w_v[:], float(1 / np.sqrt(P))).then_inc(scaled, 1)
            act.wait_ge(squares, 1)
            nc.scalar.activation(norm[:], norm[:], ACT.Sqrt).then_inc(lengths, 1)
            act.wait_ge(ready, 1)
            with act.Fori(0, NB) as t:
                act.wait_ge(var_ok, t + 1)
                nc.scalar.activation(mv[:, 2:3], mv[:, 1:2], ACT.Sqrt, bias=eps[:]).then_inc(std_ok, 1)
                act.wait_ge(turned, t + 1)
                nc.scalar.copy(xT[:], ps_t[:]).then_inc(xT_ok, 1)

        @block.vector
        def _(dve):
            link = Link(dve, link_d)
            nc.vector.memset(eps[:], EPS).then_inc(ready, 1)
            nc.vector.memset(zeros[:], 0.0).then_inc(ready, 1)
            link(nc.vector.memset(zero[:], 0.0))
            link(nc.vector.memset(ones[:], 1.0))
            link(nc.vector.memset(pos[:], -1.0))
            link(nc.vector.memset(count[:], 0.0))
            dve.wait_ge(loaded, 48)
            link(nc.vector.tensor_scalar(work_i[:], src[:], 7, None, ALU.arith_shift_right))
            link(nc.vector.tensor_copy(bucket[:], work_i[:]))
            with dve.Fori(0, NBKT) as b:
                link.enter(b, 1)
                link(nc.vector.tensor_scalar(match[:], bucket[:], const[:, ds(C_BKT + b, 1)], 0.0,
                                             ALU.is_equal, ALU.add, accum_out=count[:, ds(b, 1)]))
                link.leave(NBKT)
            nc.vector.memset(before[:], 0.0).then_inc(counted, 1)
            dve.wait_ge(summed, 1)
            link(nc.vector.tensor_scalar(groups[:], ps_c[:, 1, 0:64], float(GE - 1), None, ALU.add))
            link(nc.vector.tensor_copy(total_i[:], groups[:]))
            link(nc.vector.tensor_scalar(total_i[:], total_i[:], 8, None, ALU.arith_shift_right))
            link(nc.vector.tensor_copy(groups[:], total_i[:]))
            link(nc.vector.memset(first[:], 0.0))
            link(nc.vector.tensor_tensor_scan(first[:, 1:64], groups[:, 0:63], zero[:, 0:63], 0.0, ALU.add, ALU.add))
            link(nc.vector.scalar_tensor_tensor(out=before[:], in0=first[:], scalar=float(GE), in1=ps_c[:, 0, 0:64],
                                                op0=ALU.mult, op1=ALU.add))
            with dve.Fori(0, NBKT) as b:
                link.enter(b, 4)
                link(nc.vector.tensor_scalar(match[:], bucket[:], const[:, ds(C_BKT + b, 1)], None, ALU.is_equal))
                link(nc.vector.tensor_tensor_scan(place[:], match[:], zero[:], before[:, ds(b, 1)], ALU.add, ALU.add))
                link(nc.vector.tensor_tensor(place[:], place[:], match[:], ALU.mult))
                link(nc.vector.tensor_tensor(pos[:], pos[:], place[:], ALU.add))
                link.leave(NBKT)
            link(nc.vector.tensor_copy(pos_u[:], pos[:]))
            dve.wait_ge(rec_loaded, 16)
            link(nc.vector.tensor_scalar(work_i[:], src[:], P - 1, None, ALU.bitwise_and))
            link(nc.vector.tensor_copy(rec[:, :, R_TGT], work_i[:]))
            link(nc.vector.tensor_copy(rec[:, :, R_DST].bitcast(I32), dst[:]))
            link(nc.vector.tensor_tensor(place[:], rec[:, :, R_Y], rec[:, :, R_Y], ALU.mult))
            for k in (1, 2):
                link(nc.vector.tensor_tensor(match[:], rec[:, :, R_Y + k], rec[:, :, R_Y + k], ALU.mult))
                link(nc.vector.tensor_tensor(place[:], place[:], match[:], ALU.add))
            nc.vector.tensor_copy(norm[:], place[:]).then_inc(squares, 1)
            dve.wait_ge(lengths, 1)
            link(nc.vector.reciprocal(norm[:], norm[:]))
            for k in range(3):
                link(nc.vector.scalar_tensor_tensor(out=rec[:, :, R_Y + k], in0=rec[:, :, R_Y + k], scalar=Y1_SCALE,
                                                    in1=norm[:], op0=ALU.mult, op1=ALU.mult))
            nc.vector.memset(zero[:], 0.0).then_inc(placed, 1)
            bkt_i, keep = shared["bkt_i"], shared["keep"]
            nc.vector.tensor_copy(shared["const"][:], const[:, 0:C_KEPT])
            link(nc.vector.memset(bkt_f[:], 0.0))
            with dve.Fori(1, NB) as b:
                link.enter(b - 1, 1)
                link(nc.vector.scalar_tensor_tensor(out=bkt_f[:, 1:], in0=const[:, C_GRP:C_GRP + NG],
                                                    scalar=first[:, ds(b, 1)], in1=bkt_f[:, 1:],
                                                    op0=ALU.is_ge, op1=ALU.add))
                link.leave(NB - 1)
            link(nc.vector.tensor_copy(bkt_i[:], bkt_f[:]))
            link(nc.vector.memset(keep[:], 0.0))
            link(nc.vector.tensor_tensor(keep[:, 2:], bkt_f[:, 2:], bkt_f[:, 1:NG], ALU.is_equal))

            def node_tile(t, k, x_count, out_count):
                dve.wait_ge(x_in[k], x_count)
                nc.vector.bn_stats(stats[:, 0:6], xt[:, k, :]).then_inc(stats_ok, 1)
                dve.wait_ge(stats_ok, t + 1)
                dve.sem_inc(shared["passed"], 1)
                nc.vector.bn_aggr(mv[:, 0:2], stats[:, 0:6]).then_inc(var_ok, 1)
                dve.wait_ge(std_ok, t + 1)
                link(nc.vector.reciprocal(mv[:, 3:4], mv[:, 2:3]))
                nc.vector.tensor_scalar(xn[:], xt[:, k, :], mv[:, 0:1], mv[:, 3:4],
                                        ALU.subtract, ALU.mult).then_inc(xn_ok, 1)
                dve.wait_ge(embedded, t + 1)
                if out_count is not None:
                    dve.wait_ge(row_out[k], ONE_DMA + out_count)
                nc.vector.tensor_copy(row[:, k, :], ps_o[:].rearrange("p k f -> p (k f)")).then_inc(row_ok, 1)

            with dve.Fori(0, NB // 2) as t:
                link.enter(t, 2)
                for k in range(2):
                    node_tile(2 * t + k, k, 16 * t + 16, 16 * t)
                link.leave(NB // 2)
            node_tile(NB - 1, 0, 16 * (NB // 2 + 1), 16 * (NB // 2))


def edge_sums(nc, io, shared):
    with ExitStack() as ctx:
        m = Space(nc, ctx, "p2")
        const, bkt_i, keep = shared["const"], shared["bkt_i"], shared["keep"]
        ident = const[:, C_ID:C_ID + P]
        iota = const[:, C_IOTA:C_IOTA + P]
        wf1 = m.sb("wf1", [N_RBF + 1, P])
        wf2 = m.sb("wf2", [P, 512])
        bf2 = m.sb("bf2", [P, 512])
        bias = m.sb("bias", [P, 512], BF16)
        b_hi = m.sb("b_hi", [P, 3, 512], BF16)
        b_rest = m.sb("b_rest", [P, 512])
        ones = m.sb("ones", [P, P], BF16)
        half = m.sb("half", [P, 1])
        blank = m.sb("blank", [P, 512], BF16)
        rec = m.sb("rec", [P, 2, 2, 2, REC])
        feat = m.sb("feat", [P, 2, 2, 2, REC])
        got = m.sb("got", [P, 2, 4, D])
        fT = m.sb("fT", [N_RBF + 1, 512])
        soft = m.sb("soft", [P, 512])
        h = m.sb("h", [P, 2, 512])
        dot0 = m.sb("dot0", [P, 2, 4, P])
        dot = m.sb("dot", [P, 2, P])
        m02 = m.sb("m02", [P, 4, 2, P])
        m1 = m.sb("m1", [P, 4, P])
        m3 = m.sb("m3", [P, 4, 3, P])
        hot = m.sb("hot", [P, 2, 4, 4, P])
        sums = m.sb("sums", [P, 2, 2 * D])
        ps_f = m.psum("ps_f", [P, 512])
        ps_h = m.psum("ps_h", [P, 512])
        ps_w = m.psum("ps_w", [P, 2, 512])
        ps_a = m.psum("ps_a", [P, 2, 2, 512])

        w_loaded = m.sem("w_loaded")
        link_a = m.sem("link_a")
        link_d = m.sem("link_d")
        weights = m.sem("weights")
        rec_in = [m.sem(f"rec_in{k}") for k in range(2)]
        feat_in = [m.sem(f"feat_in{k}") for k in range(2)]
        got_in = [[m.sem(f"got_in{k}{c}") for c in range(4)] for k in range(2)]
        passed = shared["passed"]
        turned = m.sem("turned")
        fT_ok = m.sem("fT_ok")
        pre_h = m.sem("pre_h")
        soft_ok = m.sem("soft_ok")
        h_ok = m.sem("h_ok")
        w_ok = m.sem("w_ok")
        hot_ok = m.sem("hot_ok")
        dot0_ok = m.sem("dot0_ok")
        msg_ok = m.primed("msg_ok")
        spent = m.primed("spent")
        sums_ok = m.primed("sums_ok")
        sums_out = m.primed_dma("sums_out")

        start_word = m.sb("start_word", [P, 2 * len(m.dma_sems)])
        block = ctx.enter_context(nc.Block())

        def load_records(sp, tile, q, k, sem):
            row = ds(q * 4 * P, 4 * P) if not isinstance(q, int) else slice(q * 4 * P, (q + 1) * 4 * P)
            sp.dma_start(tile[:, k].rearrange("p g j w -> p g (j w)"),
                         io["sorted"][row, :].rearrange("(g p j) w -> p g (j w)", g=2, j=2)).then_inc(sem[k], 16)

        @block.sync
        def _(sp):
            m.prime(sp, io, start_word)
            sp.dma_start(wf1[:], io["wf1"]).then_inc(w_loaded, 16)
            sp.dma_start(wf2[:], io["wf2"]).then_inc(w_loaded, 16)
            sp.dma_start(bf2[:], io["bf2"].to_broadcast([P, 512])).then_inc(w_loaded, 16)
            for k in range(2):
                load_records(sp, rec, k, k, rec_in)
                load_records(sp, feat, k, k, feat_in)
            for k in range(2):
                sp.wait_ge(turned, k + 1)
                load_records(sp, feat, k + 2, k, feat_in)

            def put_sums(entry, k):
                at = sp.value_load(bkt_i[0:1, ds(entry, 1)], min_val=0, max_val=NB - 1)
                sp.wait_ge(sums_ok, ONE + entry + 1)
                sp.sem_inc(shared["passed"], 1)
                sp.wait_ge(sums_out, ONE_DMA + entry * 16)
                sp.sem_inc(shared["passed"], 1)
                sp.dma_start(io["agg"][ds(at * P, P), :], sums[:, k, :]).then_inc(sums_out, 16)

            with sp.Fori(0, NQ // 2) as i:
                for u in range(2):
                    put_sums(4 * i + 2 * u, 1)
                    sp.wait_ge(turned, 2 * i + u + 3)
                    load_records(sp, feat, 2 * i + u + 4, u, feat_in)
                    sp.wait_ge(msg_ok, ONE + 8 * i + 4 * u + 5)
                    load_records(sp, rec, 2 * i + u + 2, u, rec_in)
                    put_sums(4 * i + 2 * u + 1, 0)
            put_sums(NG, 1)
            sp.wait_ge(sums_out, ONE_DMA + 16 * (NG + 1))
            for k in range(2):
                sp.wait_ge(rec_in[k], 16 * (NQ // 2 + 1))
                sp.wait_ge(feat_in[k], 16 * (NQ // 2 + 2))

        @block.gpsimd
        def _(pool):
            def gather(k, c):
                nc.gpsimd.indirect_dma_start(
                    out=got[:, k, c, :], out_offset=None, in_=io["table_a"],
                    in_offset=bass.IndirectOffsetOnAxis(
                        ap=rec[:, k, c // 2, c % 2, R_DST:R_DST + 1].bitcast(U32), axis=0)).then_inc(got_in[k][c], 16)

            def one_hots(k):
                for c in range(4):
                    word = rec[:, k, c // 2, c % 2]
                    last = nc.gpsimd.tensor_scalar(hot[:, k, c, 0, :], iota, word[:, R_TGT:R_TGT + 1],
                                                   word[:, R_CUT:R_CUT + 1], ALU.is_equal, ALU.mult)
                last.then_inc(hot_ok, 1)

            for k in range(2):
                pool.wait_ge(rec_in[k], 16)
                for c in range(4):
                    gather(k, c)
                one_hots(k)
            with pool.Fori(1, NQ // 2) as i:
                for k in range(2):
                    pool.wait_ge(rec_in[k], 16 * i + 16)
                    for c in range(4):
                        pool.wait_ge(msg_ok, ONE + 8 * i + 4 * k + c - 6)
                        pool.sem_inc(passed, 1)
                        gather(k, c)
                    pool.wait_ge(spent, ONE + 8 * i + 4 * k - 3)
                    pool.sem_inc(passed, 1)
                    one_hots(k)
            pool.wait_ge(msg_ok, ONE + NQ * 4 - 3)
            pool.wait_ge(rec_in[0], 16 * (NQ // 2) + 16)
            for c in range(4):
                gather(0, c)
            pool.wait_ge(spent, ONE + 4 * NQ - 3)
            one_hots(0)

        @block.tensor
        def _(pe):
            def turn(k, count):
                pe.wait_ge(feat_in[k], count)
                for c in range(4):
                    mm = nc.tensor.transpose(ps_f[0:N_RBF + 1, c * P:(c + 1) * P],
                                             feat[:, k, c // 2, c % 2, 0:N_RBF + 1], ident)
                mm.then_inc(turned, 1)

            def hidden(count):
                pe.wait_ge(fT_ok, count)
                nc.tensor.matmul(ps_h[:], wf1[:], fT[:], start=True, stop=True).then_inc(pre_h, 1)

            def filters(k, c, n=None, count=None):
                if n is not None:
                    pe.wait_ge(msg_ok, ONE + n + 2)
                if count is not None:
                    pe.wait_ge(h_ok, count)
                nc.tensor.matmul(ps_w[:, c % 2, :], ones[0:65, :], bias[0:65, :], start=True, stop=False)
                nc.tensor.matmul(ps_w[:, c % 2, :], h[:, k, c * P:(c + 1) * P], wf2[:],
                                 start=False, stop=True).then_inc(w_ok, 1)

            def add_up(q, c, n, group):
                b, g = c, c // 2
                pe.wait_ge(msg_ok, ONE + n + 2)
                one, times_y = hot[:, q, c, 0, :], hot[:, q, c, 1:4, :].rearrange("p k n -> p (k n)")
                if c % 2 == 0:
                    pe.wait_ge(sums_ok, ONE + group)
                first, last = c % 2 == 0, c % 2 == 1
                A, B = ps_a[:, g, 0, :], ps_a[:, g, 1, :]
                nc.tensor.matmul(A[:, 0:P], m02[:, b, 0, :], one, start=first, stop=False,
                                 skip_group_check=True)
                nc.tensor.matmul(A[:, P:512], m02[:, b, 1, :], times_y,
                                 start=False, stop=last, skip_group_check=True)
                nc.tensor.matmul(B[:, 0:P], m1[:, b, :], one, start=first, stop=False,
                                 skip_group_check=True)
                for k in range(3):
                    mm = nc.tensor.matmul(B[:, (k + 1) * P:(k + 2) * P], m3[:, b, k, :], one,
                                          start=False, stop=last and k == 2, skip_group_check=True)
                mm.then_inc(spent, 1)

            pe.wait_ge(weights, 3)
            for bank in range(2):
                mm = nc.tensor.matmul(ps_a[:, 1, bank, :], blank[:, 0:P], blank[:], start=True, stop=True)
            mm.then_inc(spent, 1)
            for k in range(2):
                turn(k, 16)
                hidden(k + 1)
                filters(0, k, count=1)
            with pe.Fori(0, NQ // 2) as i:
                for u in range(2):
                    n, g = 8 * i + 4 * u, 4 * i + 2 * u
                    filters(u, 2, n)
                    add_up(u, 0, n, g)
                    filters(u, 3, n + 1)
                    add_up(u, 1, n + 1, g)
                    filters(1 - u, 0, n + 2, 2 * i + u + 2)
                    turn(u, 16 * (i + 2))
                    add_up(u, 2, n + 2, g + 1)
                    filters(1 - u, 1, n + 3)
                    hidden(2 * i + u + 3)
                    add_up(u, 3, n + 3, g + 1)

        @block.scalar
        def _(act):
            link = Link(act, link_a)
            act.wait_ge(w_loaded, 48)
            nc.scalar.mul(wf2[:, 0:P], wf2[:, 0:P], Y0)
            nc.scalar.mul(wf2[:, 2 * P:3 * P], wf2[:, 2 * P:3 * P], float(1 / np.sqrt(3)))
            nc.scalar.mul(wf2[:, 3 * P:], wf2[:, 3 * P:], Y0).then_inc(weights, 1)

            def features(count):
                act.wait_ge(turned, count)
                nc.scalar.copy(fT[:], ps_f[0:N_RBF + 1, :]).then_inc(fT_ok, 1)

            def softplus(count):
                act.wait_ge(pre_h, count)
                link(nc.scalar.activation(soft[:], ps_h[:], ACT.Abs))
                link(nc.scalar.activation(soft[:], soft[:], ACT.Exp, scale=-1.0))
                nc.scalar.activation(soft[:], soft[:], ACT.Ln, bias=half[:], scale=0.5).then_inc(soft_ok, 1)

            def products(k, chunks, n, count):
                for c in chunks:
                    word = rec[:, k, c // 2, c % 2]
                    act.wait_ge(got_in[k][c], count)
                    for j in range(3):
                        nc.scalar.mul(hot[:, k, c, 1 + j, :], hot[:, k, c, 0, :], word[:, R_Y + j:R_Y + j + 1])
                    nc.scalar.mul(dot0[:, k, c, :], got[:, k, c, P:2 * P], word[:, R_Y:R_Y + 1]).then_inc(dot0_ok, 1)

            act.wait_ge(weights, 3)
            features(1)
            softplus(1)
            features(2)
            act.wait_ge(hot_ok, 1)
            products(0, range(4), 0, 16)
            with act.Fori(0, NQ // 2) as i:
                link.enter(i, 4)
                for u in range(2):
                    q = 2 * i + u + 1
                    softplus(q + 1)
                    act.wait_ge(hot_ok, q + 1)
                    products(1 - u, range(4), 4 * q, 16 * (i + 1 + u))
                    features(q + 2)
                link.leave(NQ // 2)

        @block.vector
        def _(dve):
            link = Link(dve, link_d)
            link(nc.vector.memset(half[:], 0.5))
            link(nc.vector.memset(ones[:], 1.0))
            link(nc.vector.memset(blank[:], 0.0))
            link(nc.vector.memset(bias[:], 0.0))
            link(nc.vector.memset(sums[:], 0.0))
            dve.wait_ge(w_loaded, 48)
            link(nc.vector.tensor_scalar(bf2[:, 0:P], bf2[:, 0:P], Y0, None, ALU.mult))
            link(nc.vector.tensor_scalar(bf2[:, 2 * P:3 * P], bf2[:, 2 * P:3 * P], float(1 / np.sqrt(3)), None, ALU.mult))
            link(nc.vector.tensor_scalar(bf2[:, 3 * P:], bf2[:, 3 * P:], Y0, None, ALU.mult))
            rest = bf2
            for part in range(3):
                link(nc.vector.tensor_copy(b_hi[:, part, :], rest[:]))
                link(nc.vector.tensor_copy(bias[32 * part:32 * part + 1, :], b_hi[32 * part:32 * part + 1, part, :]))
                link(nc.vector.tensor_tensor(b_rest[:], rest[:], b_hi[:, part, :], ALU.subtract))
                rest = b_rest
            nc.vector.memset(dot[:], 0.0).then_inc(weights, 1)
            nc.vector.memset(m1[:], 0.0).then_inc(weights, 1)
            dve.wait_ge(weights, 3)
            nc.vector.memset(m3[:], 0.0).then_inc(msg_ok, 1)
            dve.wait_ge(msg_ok, ONE + 1)

            def h_part(k, count):
                dve.wait_ge(soft_ok, count)
                nc.vector.scalar_tensor_tensor(out=h[:, k, :], in0=ps_h[:], scalar=0.0, in1=soft[:],
                                               op0=ALU.max, op1=ALU.add).then_inc(h_ok, 1)

            def messages(k, c, n, count):
                b = c % 2
                word = rec[:, k, c // 2, b]
                row = got[:, k, c, :]
                dve.wait_ge(spent, ONE + n - 2)
                dve.wait_ge(dot0_ok, n + 1)
                link(nc.vector.scalar_tensor_tensor(out=dot[:, b, :], in0=row[:, 2 * P:3 * P],
                                                    scalar=word[:, R_Y + 1:R_Y + 2], in1=dot0[:, k, c, :],
                                                    op0=ALU.mult, op1=ALU.add))
                link(nc.vector.scalar_tensor_tensor(out=dot[:, b, :], in0=row[:, 3 * P:4 * P],
                                                    scalar=word[:, R_Y + 2:R_Y + 3], in1=dot[:, b, :],
                                                    op0=ALU.mult, op1=ALU.add))
                dve.wait_ge(w_ok, n + 1)
                W = ps_w[:, b, :]
                nc.vector.tensor_tensor(m1[:, c, :], dot[:, b, :], W[:, 2 * P:3 * P], ALU.mult)
                nc.vector.tensor_tensor(m02[:, c], row[:, 0:P].unsqueeze(1).to_broadcast([P, 2, P]),
                                        W[:, 0:2 * P].rearrange("p (j f) -> p j f", j=2), ALU.mult)
                nc.vector.tensor_tensor(m3[:, c], row[:, P:].rearrange("p (j f) -> p j f", j=3),
                                        W[:, 3 * P:].unsqueeze(1).to_broadcast([P, 3, P]),
                                        ALU.mult).then_inc(msg_ok, 1)

            def add_group(k, entry):
                dve.wait_ge(spent, ONE + 2 * entry + 1)
                dve.wait_ge(sums_out, ONE_DMA + 16 * entry)
                dve.wait_ge(sums_ok, ONE + entry)
                nc.vector.scalar_tensor_tensor(
                    out=sums[:, k, :], in0=sums[:, 1 - k, :], scalar=keep[:, ds(entry, 1)],
                    in1=ps_a[:, k].rearrange("p b n -> p (b n)"), op0=ALU.mult, op1=ALU.add).then_inc(sums_ok, 1)

            h_part(0, 1)
            with dve.Fori(0, NQ // 2) as i:
                link.enter(i, 16)
                for u in range(2):
                    n, entry = 8 * i + 4 * u, 4 * i + 2 * u
                    messages(u, 0, n, 16 * i + 16)
                    messages(u, 1, n + 1, 16 * i + 16)
                    add_group(1, entry)
                    h_part(1 - u, 2 * i + u + 2)
                    messages(u, 2, n + 2, 16 * i + 16)
                    messages(u, 3, n + 3, 16 * i + 16)
                    add_group(0, entry + 1)
                link.leave(NQ // 2)
            add_group(1, NG)


class Norms:

    def __init__(self, nc, m, tiles, passed):
        self.nc, self.tiles = nc, tiles
        self.stats = m.sb("stats", [P, tiles, 6])
        self.mv = m.sb("mv", [P, tiles, 2])
        self.small = m.sb("small", [P, 5, tiles])
        self.stats_ok = m.sem("stats_ok")
        self.passed = passed
        self.var_ok = m.sem("var_ok")
        self.std_ok = m.sem("std_ok")

    def tile(self, dve, j, rows):
        dve.sem_inc(self.passed, 1)
        self.nc.vector.bn_stats(self.stats[:, j, :], rows).then_inc(self.stats_ok, 1)

    def scale(self, dve, link, stats_count, batch):
        v, r, t, out, std = (self.small[:, k, :] for k in range(5))
        dve.wait_ge(self.stats_ok, stats_count)
        dve.sem_inc(self.passed, 1)
        for j in range(self.tiles):
            last = self.nc.vector.bn_aggr(self.mv[:, j, :], self.stats[:, j, :])
        link(last)
        self.nc.vector.tensor_scalar(v, self.mv[:, :, 1], EPS, None, ALU.add).then_inc(self.var_ok, 1)
        dve.wait_ge(self.var_ok, batch)
        dve.wait_ge(self.std_ok, batch)
        link(self.nc.vector.reciprocal(r, std))
        link(self.nc.vector.tensor_tensor(t, r, r, ALU.mult))
        link(self.nc.vector.tensor_tensor(t, t, v, ALU.mult))
        link(self.nc.vector.tensor_scalar(t, t, -0.5, 1.5, ALU.mult, ALU.add))
        link(self.nc.vector.tensor_tensor(out, r, t, ALU.mult))

    LINKS = 6

    def root(self, act, batch):
        act.wait_ge(self.var_ok, batch)
        self.nc.scalar.activation(self.small[:, 4, :], self.small[:, 0, :], ACT.Sqrt).then_inc(self.std_ok, 1)

    def apply(self, out, rows, j):
        return self.nc.vector.tensor_scalar(out, rows, self.mv[:, j, 0:1], self.small[:, 3, j:j + 1],
                                            ALU.subtract, ALU.mult)


def node_layers(nc, io, shared):
    with ExitStack() as ctx:
        m = Space(nc, ctx, "p3")
        const, acc = shared["const"], shared["acc"]
        ident = const[:, C_ID:C_ID + P]
        TB = 7
        NBATCH = NB // TB
        agg = m.sb("agg", [P, 2, 2 * D])
        w1s = m.sb("w1s", [P, 2, P])
        w1v = m.sb("w1v", [P, 2, P])
        w2s = m.sb("w2s", [P, P])
        w2v = m.sb("w2v", [P, P])
        wup = m.sb("wup", [P, 4, FF])
        wdn = m.sb("wdn", [P, 2, D])
        qup = m.sb("qup", [P, 4, FF], BF16)
        qdn = m.sb("qdn", [P, 2, D], BF16)
        wg = m.sb("wg", [P, 4, D])
        bias = m.sb("bias", [P, D])
        ident_b = m.sb("ident_b", [P, P], BF16)
        onesf = m.sb("onesf", [P, P])
        half = m.sb("half", [P, 1])
        wsum = m.sb("wsum", [P, 8])
        soft = m.sb("soft", [P, P])
        sT = m.sb("sT", [P, 2, 4, P])
        xn = m.sb("xn", [P, TB, D])
        tmp = m.sb("tmp", [P, 2, D])
        qb = m.sb("qb", [P, 2, D], BF16)
        qT = m.sb("qT", [P, 2, 4, P], BF16)
        hid = m.sb("hid", [P, TB, FF])
        xT = m.sb("xT", [P, 2, 4, P])
        row = m.sb("row", [P, 2, D])
        scal = m.sb("scal", [P, 8, TB])
        norms = Norms(nc, m, TB, shared["passed"])
        ps_1 = m.psum("ps_1", [P, 2, 512])
        ps_2 = m.psum("ps_2", [P, 2, 512])
        ps_b = m.psum("ps_b", [P, 2, 1024], BF16)
        ps_3 = m.psum("ps_3", [P, 2, 512])

        x_in = m.sem("x_in")
        w_in = m.sem("w_in")
        link_d = m.sem("link_d")
        link_a = m.sem("link_a")
        agg_in = [m.sem(f"agg_in{k}") for k in range(2)]
        scaled = m.sem("scaled")
        measured = m.sem("measured")
        ternary = m.sem("ternary")
        totals = m.sem("totals")
        first_ok = m.primed("first_ok")
        soft_ok = m.sem("soft_ok")
        vT_ok = m.primed("vT_ok")
        sT_ok = m.primed("sT_ok")
        second_ok = m.primed("second_ok")
        x1_ok = m.primed("x1_ok")
        q_ok = m.sem("q_ok")
        qturn_ok = m.sem("qturn_ok")
        qT_ok = m.sem("qT_ok")
        up_ok = m.primed("up_ok")
        relu_ok = m.sem("relu_ok")
        q2_ok = m.sem("q2_ok")
        down_ok = m.primed("down_ok")
        x2_ok = m.primed("x2_ok")
        xn_ok = m.sem("xn_ok")
        xturn_ok = m.sem("xturn_ok")
        xT_ok = m.sem("xT_ok")
        prod_ok = m.primed("prod_ok")
        row_ok = m.primed("row_ok")
        row_out = [m.primed_dma(f"row_out{k}") for k in range(2)]
        biased = m.sem("biased")

        start_word = m.sb("start_word", [P, 2 * len(m.dma_sems)])
        block = ctx.enter_context(nc.Block())

        EVEN, ODD = (TB + 1) // 2, TB // 2

        def uses(i, j):
            return (EVEN if j % 2 == 0 else ODD) * i + j // 2 + 1

        @block.sync
        def _(sp):
            m.prime(sp, io, start_word)
            weights = [(w1s, "w1s"), (w1v, "w1v"), (w2s, "w2s"), (w2v, "w2v"), (wup, "wup"), (wdn, "wdn"), (wg, "wg")]
            for tile, name in weights:
                sp.dma_start(tile[:], io[name]).then_inc(w_in, 16)
            sp.dma_start(bias[:], io["gnn_bias"].to_broadcast([P, D])).then_inc(w_in, 16)
            sp.dma_start(acc[:], io["x"][0:NPAD, :].rearrange("(t p) d -> p t d", p=P)).then_inc(x_in, 16)
            with sp.Fori(0, NBATCH) as i:
                for j in range(TB):
                    sp.wait_ge(first_ok, ONE + i * TB + (j - 1 if j else 0))
                    sp.dma_start(agg[:, j % 2, :], io["agg"][ds((i * TB + j) * P, P), :]).then_inc(agg_in[j % 2], 16)
                for j in range(TB):
                    sp.wait_ge(row_ok, ONE + i * TB + j + 1)
                    sp.dma_start(io["table_b"][ds((i * TB + j) * P, P), :], row[:, j % 2, :]).then_inc(row_out[j % 2], 16)
            for k in range(2):
                sp.wait_ge(row_out[k], ONE_DMA + 16 * NBATCH * (EVEN, ODD)[k])

        @block.tensor
        def _(pe):
            pe.wait_ge(measured, 1)
            nc.tensor.matmul(ps_1[:, 0, 0:2], onesf[:], wsum[:, 0:2], start=True, stop=True).then_inc(totals, 1)
            pe.wait_ge(scaled, 1)
            pe.wait_ge(ternary, 1)
            with pe.Fori(0, NBATCH) as i:
                t = i * TB

                def back(j):
                    pe.wait_ge(sT_ok, ONE + t + j + 1)
                    pe.wait_ge(vT_ok, ONE + t + j + 1)
                    pe.wait_ge(x1_ok, ONE + t + (j - 1 if j else 0))
                    for k in range(4):
                        mm = nc.tensor.matmul(ps_2[:, j % 2, k * P:(k + 1) * P], sT[:, j % 2, k, :],
                                              (w2s if k == 0 else w2v)[:], start=True, stop=True)
                    mm.then_inc(second_ok, 1)

                for j in range(TB):
                    b = j % 2
                    pe.wait_ge(agg_in[b], 16 * uses(i, j))
                    pe.wait_ge(sT_ok, ONE + t + (j - 1 if j else 0))
                    pe.wait_ge(vT_ok, ONE + t + (j - 1 if j else 0))
                    for k in range(2):
                        nc.tensor.matmul(ps_1[:, b, 0:P], w1s[:, k, :], agg[:, b, k * D:k * D + P],
                                         start=(k == 0), stop=(k == 1), skip_group_check=True)
                    for k in range(2):
                        mm = nc.tensor.matmul(ps_1[:, b, P:], w1v[:, k, :], agg[:, b, k * D + P:(k + 1) * D],
                                              start=(k == 0), stop=(k == 1), skip_group_check=True)
                    mm.then_inc(first_ok, 1)
                    if j:
                        back(j - 1)
                back(TB - 1)
                for j in range(TB):
                    b = j % 2
                    pe.wait_ge(q_ok, t + j + 1)
                    for k in range(4):
                        mm = nc.tensor.transpose(ps_b[:, b, k * P:(k + 1) * P], qb[:, b, k * P:(k + 1) * P], ident_b[:])
                    mm.then_inc(qturn_ok, 1)
                    pe.wait_ge(qT_ok, 2 * t + j + 1)
                    for k in range(4):
                        mm = nc.tensor.matmul(ps_3[:, b, 0:FF], qT[:, b, k, :], qup[:, k, :], start=(k == 0), stop=(k == 3))
                    mm.then_inc(up_ok, 1)
                for j in range(TB):
                    b = j % 2
                    pe.wait_ge(q2_ok, t + j + 1)
                    for k in range(2):
                        mm = nc.tensor.transpose(ps_b[:, b, k * P:(k + 1) * P], qb[:, b, k * P:(k + 1) * P], ident_b[:])
                    mm.then_inc(qturn_ok, 1)
                    pe.wait_ge(qT_ok, 2 * t + TB + j + 1)
                    pe.wait_ge(x2_ok, ONE + t + (j - 1 if j else 0))
                    for k in range(2):
                        mm = nc.tensor.matmul(ps_2[:, b, :], qT[:, b, k, :], qdn[:, k, :], start=(k == 0), stop=(k == 1))
                    mm.then_inc(down_ok, 1)
                for j in range(TB):
                    b = j % 2
                    pe.wait_ge(xn_ok, t + j + 1)
                    for k in range(4):
                        mm = nc.tensor.transpose(ps_3[:, b, k * P:(k + 1) * P], xn[:, j, k * P:(k + 1) * P], ident)
                    mm.then_inc(xturn_ok, 1)
                    pe.wait_ge(xT_ok, t + j + 1)
                    pe.wait_ge(row_ok, ONE + t + (j - 1 if j else 0))
                    for k in range(4):
                        mm = nc.tensor.matmul(ps_1[:, b, :], xT[:, b, k, :], wg[:, k, :], start=(k == 0), stop=(k == 3))
                    mm.then_inc(prod_ok, 1)

        @block.scalar
        def _(act):
            act.wait_ge(w_in, 16 * 8)
            nc.scalar.mul(w1s[:], w1s[:], float(1 / np.sqrt(2 * P)))
            nc.scalar.mul(w1v[:], w1v[:], float(1 / np.sqrt(2 * P)))
            nc.scalar.mul(w2s[:], w2s[:], float(1 / np.sqrt(P)))
            nc.scalar.mul(w2v[:], w2v[:], float(1 / np.sqrt(P))).then_inc(scaled, 1)
            act.wait_ge(ternary, 1)
            link = Link(act, link_a)
            with act.Fori(0, NBATCH) as i:
                t = i * TB
                link.enter(i, 2 * TB)
                for j in range(TB):
                    b = j % 2
                    act.wait_ge(first_ok, ONE + t + j + 1)
                    act.wait_ge(second_ok, ONE + t + (j - 1 if j else 0))
                    nc.scalar.copy(sT[:, b, 1:4, :], ps_1[:, b, P:].rearrange("p (k n) -> p k n", k=3)).then_inc(vT_ok, 1)
                    act.wait_ge(sT_ok, ONE + t + j)
                    link(nc.scalar.activation(soft[:], ps_1[:, b, 0:P], ACT.Abs))
                    link(nc.scalar.activation(soft[:], soft[:], ACT.Exp, scale=-1.0))
                    nc.scalar.activation(soft[:], soft[:], ACT.Ln, bias=half[:], scale=0.5).then_inc(soft_ok, 1)
                norms.root(act, 2 * i + 1)
                for j in range(TB):
                    b = j % 2
                    act.wait_ge(qturn_ok, 2 * t + j + 1)
                    act.wait_ge(up_ok, ONE + t + (j - 1 if j else 0))
                    nc.scalar.copy(qT[:, b], ps_b[:, b, 0:D].rearrange("p (k n) -> p k n", k=4)).then_inc(qT_ok, 1)
                    act.wait_ge(up_ok, ONE + t + j + 1)
                    nc.scalar.activation(hid[:, j, :], ps_3[:, b, 0:FF], ACT.Relu, scale=scal[:, 2, j:j + 1]).then_inc(relu_ok, 1)
                for j in range(TB):
                    b = j % 2
                    act.wait_ge(qturn_ok, 2 * t + TB + j + 1)
                    act.wait_ge(down_ok, ONE + t + (j - 1 if j else 0))
                    nc.scalar.copy(qT[:, b, 0:2], ps_b[:, b, 0:FF].rearrange("p (k n) -> p k n", k=2)).then_inc(qT_ok, 1)
                norms.root(act, 2 * i + 2)
                for j in range(TB):
                    b = j % 2
                    act.wait_ge(xturn_ok, t + j + 1)
                    act.wait_ge(prod_ok, ONE + t + (j - 1 if j else 0))
                    nc.scalar.copy(xT[:, b], ps_3[:, b].rearrange("p (k n) -> p k n", k=4)).then_inc(xT_ok, 1)
                    act.wait_ge(prod_ok, ONE + t + j + 1)
                    act.wait_ge(row_out[b], ONE_DMA + 16 * (uses(i, j) - 1))
                    nc.scalar.copy(row[:, b, :], ps_1[:, b, :]).then_inc(row_ok, 1)
                link.leave(NBATCH)

        @block.gpsimd
        def _(pool):
            pool.wait_ge(w_in, 16 * 8)
            with pool.Fori(0, NB) as t:
                pool.wait_ge(xn_ok, t + 1)
                nc.gpsimd.tensor_tensor(acc[:, ds(t, 1), :], acc[:, ds(t, 1), :], bias[:].unsqueeze(1), ALU.add)\
                  .then_inc(biased, 1)

        @block.vector
        def _(dve):
            link = Link(dve, link_d)
            nc.vector.memset(half[:], 0.5)
            link(nc.vector.memset(wsum[:], 0.0))
            link(nc.vector.memset(onesf[:], 1.0))
            link(nc.vector.tensor_copy(ident_b[:], ident))
            dve.wait_ge(w_in, 16 * 8)
            for k, w in ((0, wup), (1, wdn)):
                last = nc.vector.tensor_reduce(wsum[:, k:k + 1], w[:], AX.XY, ALU.add, apply_absolute_value=True)
                link(last)
            nc.vector.tensor_copy(wsum[:, 6:8], wsum[:, 0:2]).then_inc(measured, 1)
            dve.wait_ge(totals, 1)
            link(nc.vector.tensor_scalar(wsum[:, 2:4], ps_1[:, 0, 0:2], 1.0 / (D * FF), EPS, ALU.mult, ALU.max))
            link(nc.vector.reciprocal(wsum[:, 4:6], wsum[:, 2:4]))
            for k, w, q in ((0, wup, qup), (1, wdn, qdn)):
                link(nc.vector.tensor_scalar(w[:], w[:], wsum[:, 4 + k:5 + k], ROUND, ALU.mult, ALU.add))
                link(nc.vector.tensor_scalar(w[:], w[:], ROUND, 1.0, ALU.subtract, ALU.min))
                link(nc.vector.tensor_scalar(q[:], w[:], -1.0, None, ALU.max))
            nc.vector.tensor_scalar(wsum[:, 2:4], wsum[:, 2:4], 1.0 / 127.0, None, ALU.mult).then_inc(ternary, 1)
            dve.wait_ge(ternary, 1)
            dve.wait_ge(x_in, 16)

            def scales(a, k):
                link(nc.vector.tensor_scalar(scal[:, a, :], scal[:, a, :], EPS, None, ALU.max))
                link(nc.vector.reciprocal(scal[:, a + 1, :], scal[:, a, :]))
                nc.vector.tensor_scalar(scal[:, a + 1, :], scal[:, a + 1, :], 127.0, None, ALU.mult)
                link(nc.vector.tensor_scalar(scal[:, a + 2, :], scal[:, a, :], wsum[:, 2 + k:3 + k], None, ALU.mult))

            with dve.Fori(0, NBATCH) as i:
                t = i * TB
                link.enter(i, 2 * Norms.LINKS + 6 + 2 * TB + 3 * TB + TB)

                def row_of(j):
                    return acc[:, ds(t + j, 1), :].rearrange("p o d -> p (o d)")

                def add_graph(j):
                    dve.wait_ge(second_ok, ONE + t + j + 1)
                    a, o = row_of(j), ps_2[:, j % 2, :]
                    nc.vector.tensor_tensor(a[:, 0:P], a[:, 0:P], o[:, 0:P], ALU.add)
                    v = a[:, P:].rearrange("p (d c) -> p c d", c=3)
                    nc.vector.tensor_tensor(v, v, o[:, P:].rearrange("p (c d) -> p c d", c=3), ALU.add).then_inc(x1_ok, 1)
                    dve.wait_ge(x1_ok, ONE + t + j + 1)
                    norms.tile(dve, j, a)

                for j in range(TB):
                    dve.wait_ge(soft_ok, t + j + 1)
                    dve.wait_ge(second_ok, ONE + t + (j - 1 if j else 0))
                    nc.vector.scalar_tensor_tensor(out=sT[:, j % 2, 0, :], in0=ps_1[:, j % 2, 0:P], scalar=0.0,
                                                   in1=soft[:], op0=ALU.max, op1=ALU.add).then_inc(sT_ok, 1)
                    if j:
                        add_graph(j - 1)
                add_graph(TB - 1)
                norms.scale(dve, link, 2 * t + TB, 2 * i + 1)
                for j in range(TB):
                    link(norms.apply(xn[:, j, :], row_of(j), j))
                    link(nc.vector.tensor_reduce(scal[:, 0, j:j + 1], xn[:, j, :], AX.X, ALU.max, apply_absolute_value=True))
                scales(0, 0)
                for j in range(TB):
                    b = j % 2
                    if j >= 2:
                        dve.wait_ge(qturn_ok, 2 * t + j - 1)
                    link(nc.vector.tensor_scalar(tmp[:, b, :], xn[:, j, :], scal[:, 1, j:j + 1], ROUND, ALU.mult, ALU.add))
                    nc.vector.tensor_scalar(qb[:, b, :], tmp[:, b, :], ROUND, 127.0, ALU.subtract, ALU.min).then_inc(q_ok, 1)
                for j in range(TB):
                    dve.wait_ge(relu_ok, t + j + 1)
                    link(nc.vector.tensor_scalar(hid[:, j, :], hid[:, j, :], ROUND, ROUND, ALU.add, ALU.subtract))
                    link(nc.vector.tensor_scalar(hid[:, j, :], hid[:, j, :], 127.0, 0.0, ALU.min, ALU.max,
                                                 accum_out=scal[:, 3, j:j + 1]))
                scales(3, 1)

                def add_ffn(j):
                    dve.wait_ge(down_ok, ONE + t + j + 1)
                    a = row_of(j)
                    nc.vector.scalar_tensor_tensor(out=a, in0=ps_2[:, j % 2, :], scalar=scal[:, 5, j:j + 1], in1=a,
                                                   op0=ALU.mult, op1=ALU.add).then_inc(x2_ok, 1)
                    dve.wait_ge(x2_ok, ONE + t + j + 1)
                    norms.tile(dve, j, a)

                for j in range(TB):
                    b = j % 2
                    if j >= 2:
                        dve.wait_ge(qturn_ok, 2 * t + TB + j - 1)
                    link(nc.vector.tensor_scalar(tmp[:, b, 0:FF], hid[:, j, :], scal[:, 4, j:j + 1], ROUND, ALU.mult, ALU.add))
                    nc.vector.tensor_scalar(qb[:, b, 0:FF], tmp[:, b, 0:FF], ROUND, 127.0, ALU.subtract, ALU.min).then_inc(q2_ok, 1)
                    if j:
                        add_ffn(j - 1)
                add_ffn(TB - 1)
                norms.scale(dve, link, 2 * t + 2 * TB, 2 * i + 2)
                for j in range(TB):
                    norms.apply(xn[:, j, :], row_of(j), j).then_inc(xn_ok, 1)
                link.leave(NBATCH)
            dve.wait_ge(biased, NB)


def neighbour_sums(nc, io, shared):
    with ExitStack() as ctx:
        m = Space(nc, ctx, "p4")
        const, bkt_i, acc = shared["const"], shared["bkt_i"], shared["acc"]
        iota = const[:, C_IOTA:C_IOTA + P]
        rec = m.sb("rec", [P, 2, 2, 2, REC])
        got = m.sb("got", [P, 2, 4, D])
        high = m.sb("high", [P, 4, D], F32R)
        low = m.sb("low", [P, 4, D], F32R)
        hot = m.sb("hot", [P, 4, P], F32R)
        blank = m.sb("blank", [P, 512], BF16)
        ps_a = m.psum("ps_a", [P, 4, 512])
        rec_in = [m.sem(f"rec_in{k}") for k in range(2)]
        got_in = [[m.sem(f"got_in{k}{c}") for c in range(4)] for k in range(2)]
        passed = shared["passed"]
        blank_ok = m.sem("blank_ok")
        high_ok = m.sem("high_ok")
        low_ok = m.sem("low_ok")
        spent = m.primed("spent")
        added = m.primed("added")
        block = ctx.enter_context(nc.Block())

        def load_records(sp, q, k):
            row = ds(q * 4 * P, 4 * P) if not isinstance(q, int) else slice(q * 4 * P, (q + 1) * 4 * P)
            sp.dma_start(rec[:, k].rearrange("p g j w -> p g (j w)"),
                         io["sorted"][row, :].rearrange("(g p j) w -> p g (j w)", g=2, j=2)).then_inc(rec_in[k], 16)

        @block.sync
        def _(sp):
            m.prime(sp, io)
            load_records(sp, 0, 0)
            load_records(sp, 1, 1)
            with sp.Fori(0, NQ // 2) as i:
                for u in range(2):
                    sp.wait_ge(low_ok, 8 * i + 4 * u + 4)
                    load_records(sp, 2 * i + u + 2, u)
            for k in range(2):
                sp.wait_ge(rec_in[k], 16 * (NQ // 2 + 1))

        @block.gpsimd
        def _(pool):
            def gather(k, c):
                nc.gpsimd.indirect_dma_start(
                    out=got[:, k, c, :], out_offset=None, in_=io["table_b"],
                    in_offset=bass.IndirectOffsetOnAxis(
                        ap=rec[:, k, c // 2, c % 2, R_DST:R_DST + 1].bitcast(U32), axis=0)).then_inc(got_in[k][c], 16)

            for k in range(2):
                pool.wait_ge(rec_in[k], 16)
                for c in range(4):
                    gather(k, c)
            with pool.Fori(1, NQ // 2) as i:
                for k in range(2):
                    pool.wait_ge(rec_in[k], 16 * i + 16)
                    for c in range(4):
                        pool.wait_ge(low_ok, 8 * i + 4 * k + c - 7)
                        pool.sem_inc(passed, 1)
                        gather(k, c)

        @block.tensor
        def _(pe):
            pe.wait_ge(blank_ok, 1)
            nc.tensor.matmul(ps_a[:, 3, :], blank[:, 0:P], blank[:], start=True, stop=True).then_inc(spent, 1)
            with pe.Fori(0, NQ // 2) as i:
                for c in range(8):
                    q, g = c % 4, c // 2
                    pe.wait_ge(low_ok, 8 * i + c + 1)
                    if c % 2 == 0:
                        pe.wait_ge(added, ONE + 4 * i + g - 2)
                    nc.tensor.matmul(ps_a[:, g, :], hot[:, q, :], high[:, q, :], start=(c % 2 == 0), stop=False)
                    nc.tensor.matmul(ps_a[:, g, :], hot[:, q, :], low[:, q, :], start=False, stop=(c % 2 == 1))\
                      .then_inc(spent, 1)

        @block.scalar
        def _(act):
            with act.Fori(0, NQ // 2) as i:
                for c in range(8):
                    k, q, b = c // 4, c % 4, c % 2
                    act.wait_ge(got_in[k][q], 16 * i + 16)
                    act.wait_ge(spent, ONE + 8 * i + c - 2)
                    nc.scalar.mul(high[:, q, :], got[:, k, q, :], rec[:, k, q // 2, b, R_CUT:R_CUT + 1])\
                      .then_inc(high_ok, 1)

        @block.vector
        def _(dve):
            nc.vector.memset(blank[:], 0.0).then_inc(blank_ok, 1)

            def add_group(entry, k):
                dve.wait_ge(spent, ONE + 2 * entry + 1)
                at = dve.value_load(bkt_i[0:1, ds(entry, 1)], min_val=0, max_val=NB - 1)
                a = acc[:, ds(at, 1), :].rearrange("p o d -> p (o d)")
                dve.wait_ge(added, ONE + entry)
                nc.vector.tensor_tensor(a, a, ps_a[:, k, :], ALU.add).then_inc(added, 1)

            with dve.Fori(0, NQ // 2) as i:
                for c in range(8):
                    k, q, b = c // 4, c % 4, c % 2
                    word = rec[:, k, q // 2, b]
                    dve.wait_ge(spent, ONE + 8 * i + c - 2)
                    dve.wait_ge(high_ok, 8 * i + c + 1)
                    nc.vector.tensor_scalar(hot[:, q, :], iota, word[:, R_TGT:R_TGT + 1], None, ALU.is_equal)
                    nc.vector.scalar_tensor_tensor(out=low[:, q, :], in0=got[:, k, q, :], scalar=word[:, R_CUT:R_CUT + 1],
                                                   in1=high[:, q, :].bitcast(F32), op0=ALU.mult, op1=ALU.subtract)\
                      .then_inc(low_ok, 1)
                    if b == 1:
                        add_group(4 * i + c // 2, (c // 2 - 1) % 4)
            add_group(NG, 3)
            dve.wait_ge(added, ONE + NG + 1)


def route(nc, io, shared):
    with ExitStack() as ctx:
        m = Space(nc, ctx, "p5a")
        const, acc = shared["const"], shared["acc"]
        ident = const[:, C_ID:C_ID + P]
        place, weight, tile_expert = shared["place"], shared["weight"], shared["tile_expert"]
        TB, E = 7, N_EXP
        NBATCH = NB // TB
        tri = m.sb("tri", [P, P])
        tile_no = m.sb("tile_no", [P, NT])
        tile_f = m.sb("tile_f", [P, NT])
        ones = m.sb("ones", [P, P])
        zero = m.sb("zero", [P, NB])
        rw = m.sb("rw", [P, 4, E])
        rb = m.sb("rb", [P, 1, E])
        lower = m.sb("lower", [P, 1, E * E])
        xn = m.sb("xn", [P, TB, D])
        xT = m.sb("xT", [P, 2, 4, P])
        at = m.sb("at", [P, TB, 2], U32)
        norm = m.sb("norm", [P, 2, NB])
        prob = m.sb("prob", [P, NB, E])
        rank = m.sb("rank", [P, NB, E])
        cmp = xn[:].rearrange("p j d -> p (j d)")[:, 0:NB * E * E]
        tie = m.sb("tie", [P, NB, E])
        picked = m.sb("picked", [P, E, NB])
        total = m.sb("total", [P, E, NB])
        until = m.sb("until", [P, E, NB])
        chosen = m.sb("chosen", [P, NB, E])
        valued = m.sb("valued", [P, NB, E])
        place_f = m.sb("place_f", [P, NB, 2])
        red = m.sb("red", [P, 3, NB])
        count = m.sb("count", [P, 4, E])
        count_i = m.sb("count_i", [P, E], I32)
        norms = Norms(nc, m, TB, shared["passed"])
        ps_t = m.psum("ps_t", [P, 2, 512])
        ps_l = m.psum("ps_l", [P, 512])
        ps_c = m.psum("ps_c", [P, 2, 512])

        w_in = m.sem("w_in")
        x_in = m.sem("x_in")
        link_d = m.sem("link_d")
        xn_ok = m.sem("xn_ok")
        turned = m.primed("turned")
        xT_ok = m.primed("xT_ok")
        logits_ok = m.primed("logits_ok")
        kept = m.primed("kept")
        shifted = m.sem("shifted")
        exp_ok = m.sem("exp_ok")
        picked_ok = m.sem("picked_ok")
        summed = m.sem("summed")
        rows_ok = m.sem("rows_ok")
        scattered = shared["moved"]

        block = ctx.enter_context(nc.Block())

        @block.sync
        def _(sp):
            m.prime(sp, io)
            sp.dma_start(tri[:], io["consts"][:, C_TRI:C_TRI + P]).then_inc(w_in, 16)
            sp.dma_start(tile_no[:], io["consts"][:, C_GRP:C_GRP + NT]).then_inc(w_in, 16)
            sp.dma_start(rw[:], io["rw"]).then_inc(w_in, 16)
            sp.dma_start(rb[:, 0, :], io["rb"].to_broadcast([P, E])).then_inc(w_in, 16)
            sp.dma_start(lower[:, 0, :], io["lower"].to_broadcast([P, E * E])).then_inc(w_in, 16)
            sp.dma_start(shared["w1"][:], io["ew1"]).then_inc(x_in, 16)
            sp.dma_start(shared["b1"][:], io["b1"].to_broadcast([P, E * FF])).then_inc(x_in, 16)
            sp.wait_ge(x_in, 16 * 2)

        @block.gpsimd
        def _(pool):
            def scatter(j, count):
                pool.wait_ge(rows_ok, count)
                pool.sem_inc(shared["passed"], 1)
                for k in range(2):
                    nc.gpsimd.indirect_dma_start(
                        out=io["packed"], out_offset=bass.IndirectOffsetOnAxis(ap=at[:, j, k:k + 1], axis=0),
                        in_=xn[:, j, :], in_offset=None).then_inc(scattered[j], 16)

            with pool.Fori(0, NBATCH) as i:
                for j in range(TB):
                    scatter(j, i * TB + j + 1)
            for j in range(TB):
                pool.wait_ge(scattered[j], 32 * NBATCH)

        @block.tensor
        def _(pe):
            pe.wait_ge(w_in, 16 * 5)
            with pe.Fori(0, NBATCH) as i:
                t = i * TB
                for j in range(TB):
                    b = j % 2
                    pe.wait_ge(xn_ok, t + j + 1)
                    pe.wait_ge(xT_ok, ONE + t + max(j - 1, 0))
                    for k in range(4):
                        mm = nc.tensor.transpose(ps_t[:, b, k * P:(k + 1) * P], xn[:, j, k * P:(k + 1) * P], ident)
                    mm.then_inc(turned, 1)
                    if j == 0:
                        pe.wait_ge(kept, ONE + i)
                    if j:
                        logits(pe, nc, xT_ok, ONE + t + j, ps_l, xT, rw, j - 1, logits_ok)
                logits(pe, nc, xT_ok, ONE + t + TB, ps_l, xT, rw, TB - 1, logits_ok)
            pe.wait_ge(picked_ok, 1)
            flat = picked[:].rearrange("p e t -> p (e t)")
            nc.tensor.matmul(ps_c[:, 0, 0:E * NB], tri[:], flat, start=True, stop=True)
            nc.tensor.matmul(ps_c[:, 1, 0:E * NB], ones[:], flat, start=True, stop=True).then_inc(summed, 1)

        @block.scalar
        def _(act):
            with act.Fori(0, NBATCH) as i:
                norms.root(act, i + 1)
                for j in range(TB):
                    act.wait_ge(turned, ONE + i * TB + j + 1)
                    act.wait_ge(logits_ok, ONE + i * TB + max(j - 1, 0))
                    nc.scalar.copy(xT[:, j % 2], ps_t[:, j % 2, :].rearrange("p (k n) -> p k n", k=4)).then_inc(xT_ok, 1)
            act.wait_ge(shifted, 1)
            nc.scalar.activation(prob[:], prob[:], ACT.Exp).then_inc(exp_ok, 1)

        @block.vector
        def _(dve):
            link = Link(dve, link_d)
            link(nc.vector.memset(ones[:], 1.0))
            link(nc.vector.memset(zero[:], 0.0))
            dve.wait_ge(w_in, 16 * 5)
            with dve.Fori(0, NBATCH) as i:
                t = i * TB
                link.enter(i, Norms.LINKS)

                def row_of(j):
                    return acc[:, ds(t + j, 1), :].rearrange("p o d -> p (o d)")

                for j in range(TB):
                    norms.tile(dve, j, row_of(j))
                norms.scale(dve, link, (i + 1) * TB, i + 1)
                nc.vector.tensor_copy(norm[:, 0, ds(t, TB)], norms.mv[:, :, 0])
                nc.vector.tensor_copy(norm[:, 1, ds(t, TB)], norms.small[:, 3, :])
                for j in range(TB):
                    dve.wait_ge(turned, ONE + t + max(j - TB + 1, 0))
                    norms.apply(xn[:, j, :], row_of(j), j).then_inc(xn_ok, 1)
                dve.wait_ge(logits_ok, ONE + t + TB)
                nc.vector.tensor_tensor(prob[:, ds(t, TB), :], ps_l[:, 0:TB * E].rearrange("p (j e) -> p j e", j=TB),
                                        rb[:].to_broadcast([P, TB, E]), ALU.add).then_inc(kept, 1)
                link.leave(NBATCH)
            dve.wait_ge(kept, ONE + NBATCH)
            over = [P, NB, E]

            def each(k):
                return red[:, k, :].unsqueeze(2).to_broadcast(over)

            link(nc.vector.tensor_reduce(red[:, 0, :], prob[:], AX.X, ALU.max))
            nc.vector.tensor_tensor(prob[:], prob[:], each(0), ALU.subtract).then_inc(shifted, 1)
            dve.wait_ge(exp_ok, 1)
            link(nc.vector.tensor_reduce(red[:, 1, :], prob[:], AX.X, ALU.add))
            link(nc.vector.reciprocal(red[:, 2, :], red[:, 1, :]))
            link(nc.vector.tensor_tensor(prob[:], prob[:], each(2), ALU.mult))
            wide = [P, NB, E, E]
            mine, other = prob[:].unsqueeze(3).to_broadcast(wide), prob[:].unsqueeze(2).to_broadcast(wide)
            cmp4 = cmp.rearrange("p (t e f) -> p t e f", t=NB, e=E)
            cmp3 = cmp.rearrange("p (t q) -> p t q", t=NB)
            link(nc.vector.tensor_tensor(cmp4, other, mine, ALU.is_equal))
            link(nc.vector.tensor_tensor(cmp3, cmp3, lower[:].to_broadcast([P, NB, E * E]), ALU.mult))
            link(nc.vector.tensor_reduce(tie[:], cmp4, AX.X, ALU.add))
            link(nc.vector.tensor_tensor(cmp4, other, mine, ALU.is_gt))
            link(nc.vector.tensor_reduce(rank[:], cmp4, AX.X, ALU.add))
            link(nc.vector.tensor_tensor(rank[:], rank[:], tie[:], ALU.add))
            nc.vector.tensor_scalar(picked[:].rearrange("p e t -> p t e"), rank[:], 2.0, None, ALU.is_lt)\
              .then_inc(picked_ok, 1)
            dve.wait_ge(summed, 1)
            rows, tiles, first, start = (count[:, k, :] for k in range(4))
            link(nc.vector.tensor_copy(total[:].rearrange("p e t -> p (e t)"), ps_c[:, 1, 0:E * NB]))
            link(nc.vector.tensor_reduce(rows, total[:], AX.X, ALU.add))
            link(nc.vector.tensor_scalar(tiles, rows, float(P - 1), None, ALU.add))
            link(nc.vector.tensor_copy(count_i[:], tiles))
            link(nc.vector.tensor_scalar(count_i[:], count_i[:], 7, None, ALU.arith_shift_right))
            link(nc.vector.tensor_copy(tiles, count_i[:]))
            link(nc.vector.memset(first, 0.0))
            link(nc.vector.tensor_tensor_scan(first[:, 1:E], tiles[:, 0:E - 1], zero[:, 0:E - 1], 0.0, ALU.add, ALU.add))
            link(nc.vector.tensor_scalar(start, first, float(P), None, ALU.mult))
            for e in range(E):
                link(nc.vector.tensor_tensor_scan(until[:, e, :], total[:, e, :], zero[:], start[:, e:e + 1],
                                                  ALU.add, ALU.add))
            link(nc.vector.tensor_tensor(until[:], until[:], total[:], ALU.subtract))
            link(nc.vector.tensor_tensor(until[:], until[:], ps_c[:, 0, 0:E * NB].rearrange("p (e t) -> p e t", e=E),
                                         ALU.add))
            for k in range(2):
                link(nc.vector.tensor_scalar(chosen[:], rank[:], float(k), None, ALU.is_equal))
                link(nc.vector.tensor_tensor(valued[:], chosen[:], until[:].rearrange("p e t -> p t e"), ALU.mult))
                link(nc.vector.tensor_reduce(place_f[:, :, k], valued[:], AX.X, ALU.add))
                link(nc.vector.tensor_tensor(valued[:], chosen[:], prob[:], ALU.mult))
                link(nc.vector.tensor_reduce(weight[:, k, :], valued[:], AX.X, ALU.add))
            link(nc.vector.tensor_copy(place[:], place_f[:]))
            link(nc.vector.tensor_tensor(red[:, 1, :], weight[:, 0, :], weight[:, 1, :], ALU.add))
            link(nc.vector.tensor_scalar(red[:, 1, :], red[:, 1, :], 1e-9, None, ALU.add))
            link(nc.vector.reciprocal(red[:, 2, :], red[:, 1, :]))
            for k in range(2):
                link(nc.vector.tensor_tensor(weight[:, k, :], weight[:, k, :], red[:, 2, :], ALU.mult))

            def send(i, first_batch):
                for j in range(TB):
                    if not first_batch:
                        dve.wait_ge(scattered[j], 32 * i)
                    t = i * TB + j
                    one = slice(t, t + 1) if first_batch else ds(t, 1)
                    nc.vector.tensor_copy(at[:, j, :].unsqueeze(1), place[:, one, :])
                    nc.vector.tensor_scalar(xn[:, j, :].unsqueeze(1), acc[:, one, :], norm[:, 0, one], norm[:, 1, one],
                                            ALU.subtract, ALU.mult).then_inc(rows_ok, 1)

            send(0, True)
            link(nc.vector.memset(tile_f[:], 0.0))
            for e in range(1, E):
                link(nc.vector.scalar_tensor_tensor(out=tile_f[:], in0=tile_no[:], scalar=first[:, e:e + 1],
                                                    in1=tile_f[:], op0=ALU.is_ge, op1=ALU.add))
            link(nc.vector.tensor_copy(tile_expert[:], tile_f[:]))
            with dve.Fori(1, NBATCH) as i:
                send(i, False)


def logits(pe, nc, ready, count, ps_l, xT, rw, j, done):
    pe.wait_ge(ready, count)
    for k in range(4):
        mm = nc.tensor.matmul(ps_l[:, j * N_EXP:(j + 1) * N_EXP], xT[:, j % 2, k, :], rw[:, k, :],
                              start=(k == 0), stop=(k == 3))
    mm.then_inc(done, 1)


def expert_tiles(nc, io, shared):
    with ExitStack() as ctx:
        m = Space(nc, ctx, "p5b")
        ident = shared["const"][:, C_ID:C_ID + P]
        w1, b1, tile_expert = (shared[k] for k in ("w1", "b1", "tile_expert"))
        w2 = m.sb("w2", [P, N_EXP, 2, D])
        b2 = m.sb("b2", [P, N_EXP * D])
        rows = m.sb("rows", [P, 2, D])
        xT = m.sb("xT", [P, 2, 4, P])
        hid = m.sb("hid", [P, 2, FF])
        hT = m.sb("hT", [P, 2, 2, P])
        y = m.sb("y", [P, 2, D])
        ps_x = m.psum("ps_x", [P, 2, 512])
        ps_h = m.psum("ps_h", [P, 2, 512])
        ps_g = m.psum("ps_g", [P, 2, 512])
        ps_y = m.psum("ps_y", [P, 2, 512])
        w_in = m.sem("w_in")
        rows_in = [m.sem(f"rows_in{k}") for k in range(2)]
        turned = m.primed("turned")
        xT_ok = m.primed("xT_ok")
        first_ok = m.primed("first_ok")
        pre_ok = m.primed("pre_ok")
        hid_ok = m.primed("hid_ok")
        hturned = m.primed("hturned")
        hT_ok = m.primed("hT_ok")
        second_ok = m.primed("second_ok")
        y_ok = m.primed("y_ok")
        y_out = [m.primed_dma(f"y_out{k}") for k in range(2)]
        start_word = m.sb("start_word", [P, 2 * len(m.dma_sems)])
        block = ctx.enter_context(nc.Block())
        N2 = NT // 2

        def at(n):
            return slice(n, n + 1) if isinstance(n, int) else ds(n, 1)

        def tile_rows(n):
            return slice(n * P, (n + 1) * P) if isinstance(n, int) else ds(n * P, P)

        @block.sync
        def _(sp):
            m.prime(sp, io, start_word)

            def load(n, k):
                sp.dma_start(rows[:, k, :], io["packed"][tile_rows(n), :]).then_inc(rows_in[k], 16)

            def store(n, k):
                sp.wait_ge(y_ok, ONE + n + 1)
                sp.dma_start(io["results"][tile_rows(n), :], y[:, k, :]).then_inc(y_out[k], 16)

            for k in range(2):
                load(k, k)
            sp.dma_start(w2[:], io["ew2"]).then_inc(w_in, 16)
            sp.dma_start(b2[:], io["b2"].to_broadcast([P, N_EXP * D])).then_inc(w_in, 16)
            for k in range(2):
                sp.wait_ge(turned, ONE + k + 1)
                load(k + 2, k)
            with sp.Fori(0, N2 - 2) as i:
                for k in range(2):
                    sp.wait_ge(turned, ONE + 2 * i + k + 3)
                    load(2 * i + k + 4, k)
                    store(2 * i + k, k)
            for n in range(NT - 4, NT):
                store(n, n % 2)
            for k in range(2):
                sp.wait_ge(y_out[k], ONE_DMA + 16 * N2)

        @block.tensor
        def _(pe):
            def turn(n, k, count):
                pe.wait_ge(rows_in[k], count)
                pe.wait_ge(xT_ok, ONE + n - 1)
                for c in range(4):
                    mm = nc.tensor.transpose(ps_x[:, k, c * P:(c + 1) * P], rows[:, k, c * P:(c + 1) * P], ident)
                mm.then_inc(turned, 1)

            def first_layer(n, k):
                e = pe.value_load(tile_expert[0:1, at(n)], min_val=0, max_val=N_EXP - 1)
                pe.wait_ge(xT_ok, ONE + n + 1)
                pe.wait_ge(pre_ok, ONE + n - 1)
                for c in range(4):
                    mm = nc.tensor.matmul(ps_h[:, k, 0:FF], xT[:, k, c, :],
                                          w1[:, ds(e, 1), c, :].rearrange("p o f -> p (o f)"),
                                          start=(c == 0), stop=(c == 3))
                mm.then_inc(first_ok, 1)

            def turn_hidden(n, k):
                pe.wait_ge(hid_ok, ONE + n + 1)
                pe.wait_ge(hT_ok, ONE + n - 1)
                for f in range(2):
                    mm = nc.tensor.transpose(ps_g[:, k, f * P:(f + 1) * P], hid[:, k, f * P:(f + 1) * P], ident)
                mm.then_inc(hturned, 1)

            def second_layer(n, k):
                e = pe.value_load(tile_expert[0:1, at(n)], min_val=0, max_val=N_EXP - 1)
                pe.wait_ge(hT_ok, ONE + n + 1)
                pe.wait_ge(y_ok, ONE + n - 1)
                for f in range(2):
                    mm = nc.tensor.matmul(ps_y[:, k, :], hT[:, k, f, :],
                                          w2[:, ds(e, 1), f, :].rearrange("p o d -> p (o d)"),
                                          start=(f == 0), stop=(f == 1))
                mm.then_inc(second_ok, 1)

            turn(0, 0, 16)
            first_layer(0, 0)
            turn(1, 1, 16)
            pe.wait_ge(w_in, 32)
            with pe.Fori(0, N2 - 1) as i:
                for k in range(2):
                    n = 2 * i + k
                    first_layer(n + 1, 1 - k)
                    turn_hidden(n, k)
                    turn(n + 2, k, 16 * (i + 2))
                    second_layer(n, k)
            first_layer(NT - 1, 1)
            for k in range(2):
                turn_hidden(NT - 2 + k, k)
                second_layer(NT - 2 + k, k)

        @block.scalar
        def _(act):
            def copy_rows(n, k):
                act.wait_ge(turned, ONE + n + 1)
                act.wait_ge(first_ok, ONE + n - 1)
                nc.scalar.copy(xT[:, k], ps_x[:, k, :].rearrange("p (c n) -> p c n", c=4)).then_inc(xT_ok, 1)

            def gelu(n, k):
                act.wait_ge(pre_ok, ONE + n + 1)
                nc.scalar.activation(hid[:, k, :], hid[:, k, :], ACT.Gelu).then_inc(hid_ok, 1)

            def copy_hidden(n, k):
                act.wait_ge(hturned, ONE + n + 1)
                act.wait_ge(second_ok, ONE + n - 1)
                nc.scalar.copy(hT[:, k], ps_g[:, k, 0:FF].rearrange("p (f n) -> p f n", f=2)).then_inc(hT_ok, 1)

            copy_rows(0, 0)
            gelu(0, 0)
            copy_rows(1, 1)
            with act.Fori(0, N2 - 1) as i:
                for k in range(2):
                    n = 2 * i + k
                    copy_hidden(n, k)
                    gelu(n + 1, 1 - k)
                    copy_rows(n + 2, k)
            copy_hidden(NT - 2, 0)
            gelu(NT - 1, 1)
            copy_hidden(NT - 1, 1)

        @block.vector
        def _(dve):
            def first_bias(n, k):
                e = dve.value_load(tile_expert[0:1, at(n)], min_val=0, max_val=N_EXP - 1)
                dve.wait_ge(first_ok, ONE + n + 1)
                dve.wait_ge(hturned, ONE + n - 1)
                nc.vector.tensor_tensor(hid[:, k, :], ps_h[:, k, 0:FF], b1[:, ds(e * FF, FF)], ALU.add)\
                  .then_inc(pre_ok, 1)

            def second_bias(n, k, out_count):
                e = dve.value_load(tile_expert[0:1, at(n)], min_val=0, max_val=N_EXP - 1)
                dve.wait_ge(second_ok, ONE + n + 1)
                dve.wait_ge(y_out[k], ONE_DMA + 16 * out_count)
                nc.vector.tensor_tensor(y[:, k, :], ps_y[:, k, :], b2[:, ds(e * D, D)], ALU.add).then_inc(y_ok, 1)

            first_bias(0, 0)
            dve.wait_ge(w_in, 32)
            with dve.Fori(0, N2 - 1) as i:
                for k in range(2):
                    first_bias(2 * i + k + 1, 1 - k)
                    second_bias(2 * i + k, k, i)
            first_bias(NT - 1, 1)
            for k in range(2):
                second_bias(NT - 2 + k, k, N2 - 1)


def combine(nc, io, shared):
    with ExitStack() as ctx:
        m = Space(nc, ctx, "p5c")
        acc, place, weight = shared["acc"], shared["place"], shared["weight"]
        TB = 7
        NBATCH = NB // TB
        pair = m.sb("pair", [P, TB, 2, D])
        at = m.sb("at", [P, TB, 2], U32)
        staged = m.sem("staged")
        got, scattered = shared["moved"], 32 * NBATCH
        added = m.sem("added")
        out_ok = m.sem("out_ok")
        block = ctx.enter_context(nc.Block())

        @block.sync
        def _(sp):
            with sp.Fori(0, NBATCH) as i:
                sp.wait_ge(added, (i + 1) * TB)
                sp.dma_start(io["out"][ds(i * TB * P, TB * P), :].rearrange("(t p) d -> p t d", p=P),
                             acc[:, ds(i * TB, TB), :]).then_inc(out_ok, 16)
            sp.wait_ge(out_ok, 16 * NBATCH)

        @block.gpsimd
        def _(pool):
            def gather(i, j, first_batch):
                t = i * TB + j
                if not first_batch:
                    pool.wait_ge(added, t - TB + 1)
                one = slice(t, t + 1) if first_batch else ds(t, 1)
                nc.gpsimd.tensor_copy(at[:, j, :].unsqueeze(1), place[:, one, :]).then_inc(staged, 1)
                pool.wait_ge(staged, t + 1)
                pool.sem_inc(shared["passed"], 1)
                for k in range(2):
                    nc.gpsimd.indirect_dma_start(
                        out=pair[:, j, k, :], out_offset=None, in_=io["results"],
                        in_offset=bass.IndirectOffsetOnAxis(ap=at[:, j, k:k + 1], axis=0)).then_inc(got[j], 16)

            for j in range(TB):
                gather(0, j, True)
            with pool.Fori(1, NBATCH) as i:
                for j in range(TB):
                    gather(i, j, False)

        link_d = m.sem("link_d")

        @block.vector
        def _(dve):
            link = Link(dve, link_d)
            with dve.Fori(0, NBATCH) as i:
                link.enter(i, TB)
                for j in range(TB):
                    t = i * TB + j
                    a = acc[:, ds(t, 1), :].rearrange("p o d -> p (o d)")
                    dve.wait_ge(got[j], scattered + 32 * i + 32)
                    link(nc.vector.scalar_tensor_tensor(out=a, in0=pair[:, j, 0, :], scalar=weight[:, 0, ds(t, 1)],
                                                        in1=a, op0=ALU.mult, op1=ALU.add))
                    nc.vector.scalar_tensor_tensor(out=a, in0=pair[:, j, 1, :], scalar=weight[:, 1, ds(t, 1)],
                                                   in1=a, op0=ALU.mult, op1=ALU.add).then_inc(added, 1)
                link.leave(NBATCH)


def experts(nc, io, shared):
    with ExitStack() as ctx:
        m = Space(nc, ctx, "p5")
        shared["place"] = m.sb("place", [P, NB, 2], U32)
        shared["weight"] = m.sb("weight", [P, 2, NB])
        shared["moved"] = [m.sem(f"moved{j}") for j in range(7)]
        with ExitStack() as inner:
            w = Space(nc, inner, "p5w")
            shared["tile_expert"] = w.sb("tile_expert", [P, NT], I32)
            shared["w1"] = w.sb("w1", [P, N_EXP, 4, FF])
            shared["b1"] = w.sb("b1", [P, N_EXP * FF])
            route(nc, io, shared)
            expert_tiles(nc, io, shared)
        combine(nc, io, shared)


def program(nc, io):
    with ExitStack() as ctx:
        m = Space(nc, ctx, "all")
        shared = {
            "const": m.sb("const", [P, C_KEPT]),
            "bkt_i": m.sb("bkt_i", [P, NG + 1], I32),
            "keep": m.sb("keep", [P, NG + 1]),
            "passed": m.sem("passed"),
        }
        sort_and_embed(nc, io, shared)
        edge_sums(nc, io, shared)
        shared["acc"] = m.sb("acc", [P, NB, D])
        node_layers(nc, io, shared)
        neighbour_sums(nc, io, shared)
        experts(nc, io, shared)


def filter_order(w):
    w = w[:, :4 * P].reshape(-1, 2, P, 2)
    return np.ascontiguousarray(np.concatenate([w[:, 0, :, 0], w[:, 1, :, 0], w[:, 0, :, 1], w[:, 1, :, 1]], axis=1))


def chunks(w):
    return np.ascontiguousarray(w.reshape(-1, P, w.shape[1]).transpose(1, 0, 2))


def lay_out(a):
    f = np.float32
    consts = np.zeros((P, C_END), f)
    consts[:, C_ID:C_ID + P] = np.eye(P)
    consts[:, C_TRI:C_TRI + P] = np.triu(np.ones((P, P)), 1)
    consts[:, C_IOTA:C_IOTA + P] = np.arange(P)
    consts[:, C_BKT:C_BKT + 64] = np.arange(64)
    consts[:, C_GRP:C_END] = np.arange(C_END - C_GRP)
    x = np.zeros((NPAD + P, D), f)
    x[:N_NODES] = a["x"]
    src = np.full(EPAD, NPAD, np.int32)
    src[:N_EDGES] = a["src"]
    dst = np.zeros(EPAD, np.int32)
    dst[:N_EDGES] = a["dst"]
    edges = np.zeros((EPAD, REC), f)
    edges[:, R_Y] = 1
    edges[:N_EDGES, 0:N_RBF] = a["edge_attr_20"]
    edges[:N_EDGES, R_ONE] = 1
    edges[:N_EDGES, R_Y:R_Y + 3] = a["edge_attr_3"]
    edges[:N_EDGES, R_CUT] = a["edge_weight"]
    return {
        "consts": consts, "x": x, "src": src.reshape(P, COLS), "dst": dst.reshape(P, COLS),
        "edges": edges.reshape(P, COLS, REC),
        "wf1": np.concatenate([a["L0_gnn_Wf1"], np.asarray(a["L0_gnn_bf1"])[None]]),
        "wf2": filter_order(np.asarray(a["L0_gnn_Wf2"])), "bf2": filter_order(np.asarray(a["L0_gnn_bf2"])[None]),
        "w1s": np.asarray(a["L0_gnn_W1_s"]).reshape(P, 2, P), "w1v": np.asarray(a["L0_gnn_W1_v"]).reshape(P, 2, P),
        "w2s": np.asarray(a["L0_gnn_W2_s"]), "w2v": np.asarray(a["L0_gnn_W2_v"]),
        "wup": chunks(np.asarray(a["L0_ffn_w_up"]).T), "wdn": chunks(np.asarray(a["L0_ffn_w_down"]).T),
        "wg": chunks(np.asarray(a["L1_gnn_weight"])), "gnn_bias": np.asarray(a["L1_gnn_bias"])[None],
        "ew1": np.ascontiguousarray(np.asarray(a["L1_ffn_W1"]).reshape(N_EXP, 4, P, FF).transpose(2, 0, 1, 3)),
        "ew2": np.ascontiguousarray(np.asarray(a["L1_ffn_W2"]).reshape(N_EXP, 2, P, D).transpose(2, 0, 1, 3)),
        "b1": np.asarray(a["L1_ffn_b1"]).reshape(1, -1),
        "b2": np.asarray(a["L1_ffn_b2"]).reshape(1, -1), "rw": chunks(np.asarray(a["L1_ffn_router_w"])),
        "rb": np.asarray(a["L1_ffn_router_b"])[None],
        "lower": np.tril(np.ones((N_EXP, N_EXP), f), -1).reshape(1, -1),
        "w_in_s": np.asarray(a["L0_gnn_W_in2f_s"]), "w_in_v": np.asarray(a["L0_gnn_W_in2f_v"]),
    }


SCRATCH = {"sorted": [NG_ROWS * GE, REC], "table_a": [NPAD, D], "agg": [NPAD, 2 * D], "table_b": [NPAD, D],
           "packed": [NT * P, D], "results": [NT * P, D]}


def kernel(**inputs):
    import concourse.bacc as bacc
    from concourse.bass_utils import run_bass_kernel_spmd

    nc = bacc.Bacc("TRN2", target_bir_lowering=False, num_devices=1)
    arrays = {f"in_{k}": np.ascontiguousarray(v) for k, v in lay_out({k: np.asarray(v) for k, v in inputs.items()}).items()}
    io = {k[3:]: nc.dram_tensor(k, v.shape, mybir.dt.from_np(v.dtype), kind="ExternalInput").ap()
          for k, v in arrays.items()}
    for k, shape in SCRATCH.items():
        io[k] = nc.dram_tensor(k, shape, F32).ap()
    io["out"] = nc.dram_tensor("out", [NPAD, D], F32, kind="ExternalOutput").ap()
    program(nc, io)
    result = run_bass_kernel_spmd(nc, [arrays], core_ids=[0])
    return result.results[0]["out"][:N_NODES]
```

```python
from contextlib import ExitStack

import numpy as np

import concourse.bass as bass
from concourse import mybir
from concourse.bass import ds

ALU = mybir.AluOpType
ACT = mybir.ActivationFunctionType
AX = mybir.AxisListType
F32 = mybir.dt.float32
BF16 = mybir.dt.bfloat16
I32 = mybir.dt.int32
U32 = mybir.dt.uint32

P = 128
D = 512
N_NODES = 6250
N_EDGES = 100000
N_RBF = 20
FF = 256
N_EXP = 8

NB = -(-N_NODES // P)
NPAD = NB * P
COLS = 8 * (-(-N_EDGES // (8 * P)))
EPAD = COLS * P
PIECES = (112, 224, 448)
PAD_J = 64
NBKT = NB + 1
GC = 2
GE = GC * P
NG = 2 * (-(-((N_EDGES + NB * (GE - 1)) // GE) // 2))
NQ = NG // 2
NG_ROWS = NG + 8
assert EPAD - N_EDGES <= 2 * GE and NQ % 4 == 0 and COLS == sum(PIECES) and all(n % 16 == 0 for n in PIECES)
assert NG_ROWS * GE % (PAD_J * P) == 0
NT = 2 * (-(-((2 * NPAD + N_EXP * (P - 1)) // P) // 2))
assert COLS // 16 == NB <= NT // 2 and NBKT % 10 == 0
REC = 32

R_ONE, R_Y, R_CUT, R_TGT, R_DST, R_PLACE = 20, 21, 24, 25, 26, 27

C_ID, C_IOTA, C_KEPT = 0, 128, 256
C_TRI, C_BKT, C_GRP, C_END = 256, 384, 448, 448 + NG + 8

EPS = 1e-5
Y0 = float(1.0 / np.sqrt(4.0 * np.pi))
Y1_SCALE = float(np.sqrt(3.0 / (4.0 * np.pi)))
ROUND = 12582912.0


class Link:

    def __init__(self, eng, sem):
        self.eng, self.sem, self.base, self.n = eng, sem, 0, 0

    def __call__(self, ins):
        self.n += 1
        ins.then_inc(self.sem, 1)
        self.eng.wait_ge(self.sem, self.base + self.n)

    def enter(self, i, per):
        self.start, self.per = self.base + self.n, per
        self.base, self.n = self.start + i * per, 0

    def leave(self, count):
        assert self.n == self.per, (self.n, self.per)
        self.base, self.n = self.start + count * self.per, 0


ONE = 4
ONE_DMA = 16


class Space:

    def __init__(self, nc, ctx, tag):
        self.nc, self.ctx, self.tag = nc, ctx, tag
        self.sems, self.dma_sems = [], []

    def sb(self, name, shape, dt=F32):
        return self.ctx.enter_context(self.nc.sbuf_tensor(f"{self.tag}_{name}", shape, dt))

    def psum(self, name, shape, dt=F32):
        return self.ctx.enter_context(self.nc.psum_tensor(f"{self.tag}_{name}", shape, dt))

    def sem(self, name):
        return self.ctx.enter_context(self.nc.semaphore(f"{self.tag}_{name}"))

    def primed(self, name):
        self.sems.append(self.sem(name))
        return self.sems[-1]

    def primed_dma(self, name):
        self.dma_sems.append(self.sem(name))
        return self.dma_sems[-1]

    def prime(self, sp, io, start_word=None):
        for sem in self.sems:
            sp.sem_inc(sem, ONE)
        for k, sem in enumerate(self.dma_sems):
            sp.dma_start(start_word[:, 2 * k:2 * k + 2], io["consts"][:, 0:2]).then_inc(sem, ONE_DMA)


def sort_and_embed(nc, io, shared):
    with ExitStack() as ctx:
        m = Space(nc, ctx, "p1")
        const = m.sb("const", [P, C_END])
        bkt_f = m.sb("bkt_f", [P, NG + 1])
        ident = const[:, C_ID:C_ID + P]
        rec = m.sb("rec", [P, COLS, REC])
        src = m.sb("src", [P, COLS], I32)
        dst = m.sb("dst", [P, COLS], I32)
        work_i = m.sb("work_i", [P, COLS], I32)
        bucket = m.sb("bucket", [P, COLS])
        match = m.sb("match", [P, COLS])
        bucket_h = m.sb("bucket_h", [P, COLS], BF16)
        match_h = m.sb("match_h", [P, 2, COLS], BF16)
        place = m.sb("place", [P, COLS])
        pos = m.sb("pos", [P, COLS])
        zero = m.sb("zero", [P, COLS])
        count = m.sb("count", [P, 64])
        before = m.sb("before", [P, 64])
        total_i = m.sb("total_i", [P, 64], I32)
        groups = m.sb("groups", [P, 64])
        first = m.sb("first", [P, 64])
        norm = m.sb("norm", [P, COLS])
        pad = m.sb("pad", [P, PAD_J, REC])
        match2 = m.sb("match2", [P, 2, max(PIECES)])
        place2 = m.sb("place2", [P, 2, max(PIECES)])
        stage = m.sb("stage", [P, 2, 8, REC])
        xt = m.sb("xt", [P, 2, D])
        xn = m.sb("xn", [P, D])
        xT = m.sb("xT", [P, 4, P])
        row = m.sb("row", [P, 2, D])
        stats = m.sb("stats", [P, 8])
        mv = m.sb("mv", [P, 4])
        w_s = m.sb("w_s", [P, P])
        w_v = m.sb("w_v", [P, P])
        eps = m.sb("eps", [P, 1])
        ones = m.sb("ones", [P, P])
        zeros = m.sb("zeros", [P, 2 * D])
        ps_c = m.psum("ps_c", [P, 2, 512])
        ps_t = m.psum("ps_t", [P, 4, P])
        ps_o = m.psum("ps_o", [P, 4, P])

        loaded = m.sem("loaded")
        rec_loaded = m.sem("rec_loaded")
        w_loaded = m.sem("w_loaded")
        link_d = m.sem("link_d")
        ready = m.sem("ready")
        squares = m.sem("squares")
        lengths = m.sem("lengths")
        counted = m.sem("counted")
        summed = m.sem("summed")
        placed = m.sem("placed")
        cleared = m.sem("cleared")
        pad_made = m.sem("pad_made")
        padded = m.sem("padded")
        link_s = m.sem("link_s")
        staged = [m.sem(f"staged{k}") for k in range(2)]
        scattered = [m.sem(f"scattered{k}") for k in range(2)]
        x_in = [m.sem(f"x_in{k}") for k in range(2)]
        x_free = m.sem("x_free")
        stats_ok = m.sem("stats_ok")
        var_ok = m.sem("var_ok")
        std_ok = m.sem("std_ok")
        xn_ok = m.sem("xn_ok")
        turned = m.sem("turned")
        xT_ok = m.sem("xT_ok")
        embedded = m.sem("embedded")
        row_ok = m.primed("row_ok")
        row_out = [m.primed_dma(f"row_out{k}") for k in range(2)]
        scaled = m.sem("scaled")

        N_PAD = NG_ROWS * GE // (PAD_J * P)
        start_word = m.sb("start_word", [P, 2 * len(m.dma_sems)])
        block = ctx.enter_context(nc.Block())

        @block.sync
        def _(sp):
            m.prime(sp, io, start_word)
            sp.dma_start(const[:], io["consts"]).then_inc(loaded, 16)
            sp.dma_start(src[:], io["src"]).then_inc(loaded, 16)
            sp.dma_start(dst[:], io["dst"]).then_inc(loaded, 16)
            sp.dma_start(rec[:], io["edges"]).then_inc(rec_loaded, 16)
            sp.dma_start(w_s[:], io["w_in_s"]).then_inc(w_loaded, 16)
            sp.dma_start(w_v[:], io["w_in_v"]).then_inc(w_loaded, 16)
            sp.wait_ge(ready, 2)
            sp.wait_ge(pad_made, 2)
            with sp.Fori(0, N_PAD) as g:
                sp.dma_start(io["sorted"][ds(g * PAD_J * P, PAD_J * P), :].rearrange("(p j) w -> p (j w)", j=PAD_J),
                             pad[:].rearrange("p j w -> p (j w)")).then_inc(padded, 16)

            def load_stage(q, k):
                col = q * 16 + k * 8
                cols = slice(col, col + 8) if isinstance(q, int) else ds(col, 8)
                sp.dma_start(stage[:, k], rec[:, cols, :]).then_inc(staged[k], 16)

            def clear(b):
                rows = slice(b * P, (b + 1) * P) if isinstance(b, int) else ds(b * P, P)
                sp.dma_start(io["agg"][rows, :], zeros[:]).then_inc(cleared, 16)

            def clear_packed(b):
                rows = slice(b * 2 * P, (b + 1) * 2 * P) if isinstance(b, int) else ds(b * 2 * P, 2 * P)
                sp.dma_start(io["packed"][rows, :].rearrange("(p j) w -> p (j w)", j=2), zeros[:]).then_inc(cleared, 16)

            sp.wait_ge(placed, 1)
            load_stage(0, 0)
            load_stage(0, 1)
            clear(0)
            for b in range(COLS // 16 - 1, NT // 2):
                clear_packed(b)
            with sp.Fori(1, COLS // 16) as q:
                sp.wait_ge(placed, q + 1)
                sp.sem_inc(shared["passed"], 1)
                for k in range(2):
                    sp.wait_ge(scattered[k], q * 128)
                    sp.sem_inc(shared["passed"], 1)
                    load_stage(q, k)
                clear(q)
                clear_packed(q - 1)
            sp.wait_ge(cleared, 16 * (NB + NT // 2))
            for k in range(2):
                sp.wait_ge(staged[k], (COLS // 16) * 16)

        @block.gpsimd
        def _(pool):
            nc.gpsimd.memset(pad[:], 0.0).then_inc(pad_made, 1)
            pool.wait_ge(pad_made, 1)
            nc.gpsimd.memset(pad[:, :, R_Y:R_Y + 1], 1.0).then_inc(pad_made, 1)
            pool.wait_ge(padded, 16 * N_PAD)
            with pool.Fori(0, COLS // 16) as q:
                for k in range(2):
                    pool.wait_ge(staged[k], 16 * q + 16)
                    pool.sem_inc(shared["passed"], 1)
                    for c in range(8):
                        nc.gpsimd.indirect_dma_start(
                            out=io["sorted"], out_offset=bass.IndirectOffsetOnAxis(
                                ap=stage[:, k, c, R_PLACE:R_PLACE + 1].bitcast(U32), axis=0),
                            in_=stage[:, k, c, :], in_offset=None).then_inc(scattered[k], 16)
            for k in range(2):
                pool.wait_ge(scattered[k], (COLS // 16) * 128)

        @block.tensor
        def _(pe):
            pe.wait_ge(counted, 1)
            nc.tensor.matmul(ps_c[:, 0, 0:64], const[:, C_TRI:C_TRI + P], count[:], start=True, stop=True)
            nc.tensor.matmul(ps_c[:, 1, 0:64], ones[:], count[:], start=True, stop=True).then_inc(summed, 1)
            pe.wait_ge(scaled, 2)
            with pe.Fori(0, NB) as t:
                pe.wait_ge(xn_ok, t + 1)
                for k in range(4):
                    part = xn[:, 0:P] if k == 0 else xn[:, P + k - 1:D:3]
                    mm = nc.tensor.transpose(ps_t[:, k, :], part, ident)
                mm.then_inc(turned, 1)
                pe.wait_ge(xT_ok, t + 1)
                pe.wait_ge(row_ok, ONE + t)
                for k in range(4):
                    mm = nc.tensor.matmul(ps_o[:, k, :], xT[:, k, :], (w_s if k == 0 else w_v)[:],
                                          start=True, stop=True)
                mm.then_inc(embedded, 1)

        @block.scalar
        def _(act):
            act.wait_ge(w_loaded, 32)
            nc.scalar.mul(w_s[:], w_s[:], float(1 / np.sqrt(P))).then_inc(scaled, 1)
            nc.scalar.mul(w_v[:], w_v[:], float(1 / np.sqrt(P))).then_inc(scaled, 1)
            act.wait_ge(squares, 1)
            nc.scalar.activation(norm[:], norm[:], ACT.Sqrt).then_inc(lengths, 1)
            act.wait_ge(ready, 2)
            for k in range(2):
                act.dma_start(xt[:, k, :], io["x"][k * P:(k + 1) * P, :]).then_inc(x_in[k], 16)

            def node_tile(t, k):
                act.wait_ge(var_ok, t + 1)
                nc.scalar.activation(mv[:, 2:3], mv[:, 1:2], ACT.Sqrt, bias=eps[:]).then_inc(std_ok, 1)
                act.wait_ge(turned, t + 1)
                nc.scalar.copy(xT[:], ps_t[:]).then_inc(xT_ok, 1)

            def table_rows(t, k):
                act.wait_ge(row_ok, ONE + t + 1)
                rows = slice(t * P, (t + 1) * P) if isinstance(t, int) else ds(t * P, P)
                act.dma_start(io["table_a"][rows, :], row[:, k, :]).then_inc(row_out[k], 16)

            with act.Fori(0, (NB - 1) // 2) as i:
                for k in range(2):
                    t = 2 * i + k
                    node_tile(t, k)
                    act.wait_ge(xn_ok, t + 1)
                    act.dma_start(xt[:, k, :], io["x"][ds((t + 2) * P, P), :]).then_inc(x_in[k], 16)
                    table_rows(t, k)
            node_tile(NB - 1, 0)
            table_rows(NB - 1, 0)
            act.wait_ge(row_out[0], ONE_DMA + 16 * (NB // 2 + 1))
            act.wait_ge(row_out[1], ONE_DMA + 16 * (NB // 2))
            act.wait_ge(x_in[1], 16 * (NB // 2 + 1))

        @block.vector
        def _(dve):
            link = Link(dve, link_d)
            nc.vector.memset(eps[:], EPS).then_inc(ready, 1)
            nc.vector.memset(zeros[:], 0.0).then_inc(ready, 1)
            link(nc.vector.memset(zero[:], 0.0))
            link(nc.vector.memset(ones[:], 1.0))
            link(nc.vector.memset(pos[:], -1.0))
            link(nc.vector.memset(count[:], 0.0))
            dve.wait_ge(loaded, 48)
            link(nc.vector.tensor_scalar(work_i[:], src[:], 7, None, ALU.arith_shift_right))
            link(nc.vector.tensor_copy(bucket[:], work_i[:]))
            link(nc.vector.tensor_copy(bucket_h[:], work_i[:]))
            with dve.Fori(0, NBKT // 5) as b5:
                link.enter(b5, 5)
                for k in range(5):
                    link.n += 1
                    if k >= 2:
                        dve.wait_ge(link_d, link.base + link.n - 2)
                    nc.vector.tensor_scalar(match_h[:, k % 2, :], bucket_h[:], const[:, ds(C_BKT + 5 * b5 + k, 1)], 0.0,
                                            ALU.is_equal, ALU.add, accum_out=count[:, ds(5 * b5 + k, 1)])\
                      .then_inc(link_d, 1)
                dve.wait_ge(link_d, link.base + link.n)
                link.leave(NBKT // 5)
            nc.vector.memset(before[:], 0.0).then_inc(counted, 1)
            dve.wait_ge(summed, 1)
            link(nc.vector.tensor_scalar(groups[:], ps_c[:, 1, 0:64], float(GE - 1), None, ALU.add))
            link(nc.vector.tensor_copy(total_i[:], groups[:]))
            link(nc.vector.tensor_scalar(total_i[:], total_i[:], 8, None, ALU.arith_shift_right))
            link(nc.vector.tensor_copy(groups[:], total_i[:]))
            link(nc.vector.memset(first[:], 0.0))
            link(nc.vector.tensor_tensor_scan(first[:, 1:64], groups[:, 0:63], zero[:, 0:63], 0.0, ALU.add, ALU.add))
            link(nc.vector.scalar_tensor_tensor(out=before[:], in0=first[:], scalar=float(GE), in1=ps_c[:, 0, 0:64],
                                                op0=ALU.mult, op1=ALU.add))
            def record_words():
                dve.wait_ge(rec_loaded, 16)
                link(nc.vector.tensor_scalar(work_i[:], src[:], P - 1, None, ALU.bitwise_and))
                link(nc.vector.tensor_copy(rec[:, :, R_TGT], work_i[:]))
                link(nc.vector.tensor_copy(rec[:, :, R_DST].bitcast(I32), dst[:]))
                link(nc.vector.tensor_tensor(place[:], rec[:, :, R_Y], rec[:, :, R_Y], ALU.mult))
                for k in (1, 2):
                    link(nc.vector.tensor_tensor(match[:], rec[:, :, R_Y + k], rec[:, :, R_Y + k], ALU.mult))
                    link(nc.vector.tensor_tensor(place[:], place[:], match[:], ALU.add))
                nc.vector.tensor_copy(norm[:], place[:]).then_inc(squares, 1)
                dve.wait_ge(lengths, 1)
                link(nc.vector.reciprocal(norm[:], norm[:]))
                for k in range(3):
                    link(nc.vector.scalar_tensor_tensor(out=rec[:, :, R_Y + k], in0=rec[:, :, R_Y + k], scalar=Y1_SCALE,
                                                        in1=norm[:], op0=ALU.mult, op1=ALU.mult))

            done = 0
            for w, size in enumerate(PIECES):
                cols = slice(done, done + size)
                with dve.Fori(0, NBKT // 10) as b10:
                    for pair in range(5):
                        base = (w * (NBKT // 2) + 5 * b10 + pair) * 10
                        at = [ds(10 * b10 + 2 * pair + k, 1) for k in range(2)]
                        for k in range(2):
                            nc.vector.tensor_scalar(match2[:, k, 0:size], bucket[:, cols],
                                                    const[:, ds(C_BKT + 10 * b10 + 2 * pair + k, 1)], None,
                                                    ALU.is_equal).then_inc(link_s, 1)
                        for k in range(2):
                            dve.wait_ge(link_s, base + 1 + k)
                            nc.vector.tensor_tensor_scan(place2[:, k, 0:size], match2[:, k, 0:size], zero[:, 0:size],
                                                         before[:, at[k]], ALU.add, ALU.add).then_inc(link_s, 1)
                        for k in range(2):
                            dve.wait_ge(link_s, base + 3 + k)
                            nc.vector.tensor_tensor(match2[:, k, 0:size], place2[:, k, 0:size], match2[:, k, 0:size],
                                                    ALU.mult).then_inc(link_s, 1)
                        for k in range(2):
                            nc.vector.tensor_copy(before[:, at[k]], place2[:, k, size - 1:size]).then_inc(link_s, 1)
                        for k in range(2):
                            dve.wait_ge(link_s, base + 8 + k)
                            nc.vector.tensor_tensor(pos[:, cols], pos[:, cols], match2[:, k, 0:size],
                                                    ALU.add).then_inc(link_s, 1)
                        dve.wait_ge(link_s, base + 10)
                if w == 0:
                    record_words()
                nc.vector.tensor_copy(rec[:, cols, R_PLACE].bitcast(U32), pos[:, cols]).then_inc(placed, size // 16)
                done += size
            bkt_i, keep = shared["bkt_i"], shared["keep"]
            nc.vector.tensor_copy(shared["const"][:], const[:, 0:C_KEPT])
            link(nc.vector.memset(bkt_f[:], 0.0))
            with dve.Fori(1, NB) as b:
                link.enter(b - 1, 1)
                link(nc.vector.scalar_tensor_tensor(out=bkt_f[:, 1:], in0=const[:, C_GRP:C_GRP + NG],
                                                    scalar=first[:, ds(b, 1)], in1=bkt_f[:, 1:],
                                                    op0=ALU.is_ge, op1=ALU.add))
                link.leave(NB - 1)
            link(nc.vector.tensor_copy(bkt_i[:], bkt_f[:]))
            link(nc.vector.memset(keep[:], 0.0))
            link(nc.vector.tensor_tensor(keep[:, 2:], bkt_f[:, 2:], bkt_f[:, 1:NG], ALU.is_equal))

            def node_tile(t, k, x_count, out_count):
                dve.wait_ge(x_in[k], x_count)
                nc.vector.bn_stats(stats[:, 0:6], xt[:, k, :]).then_inc(stats_ok, 1)
                dve.wait_ge(stats_ok, t + 1)
                dve.sem_inc(shared["passed"], 1)
                nc.vector.bn_aggr(mv[:, 0:2], stats[:, 0:6]).then_inc(var_ok, 1)
                dve.wait_ge(std_ok, t + 1)
                link(nc.vector.reciprocal(mv[:, 3:4], mv[:, 2:3]))
                nc.vector.tensor_scalar(xn[:], xt[:, k, :], mv[:, 0:1], mv[:, 3:4],
                                        ALU.subtract, ALU.mult).then_inc(xn_ok, 1)
                dve.wait_ge(embedded, t + 1)
                if out_count is not None:
                    dve.wait_ge(row_out[k], ONE_DMA + out_count)
                nc.vector.tensor_copy(row[:, k, :], ps_o[:].rearrange("p k f -> p (k f)")).then_inc(row_ok, 1)

            with dve.Fori(0, NB // 2) as t:
                link.enter(t, 2)
                for k in range(2):
                    node_tile(2 * t + k, k, 16 * t + 16, 16 * t)
                link.leave(NB // 2)
            node_tile(NB - 1, 0, 16 * (NB // 2 + 1), 16 * (NB // 2))


def edge_sums(nc, io, shared):
    with ExitStack() as ctx:
        m = Space(nc, ctx, "p2")
        const, bkt_i, keep = shared["const"], shared["bkt_i"], shared["keep"]
        ident = const[:, C_ID:C_ID + P]
        iota = const[:, C_IOTA:C_IOTA + P]
        wf1 = m.sb("wf1", [P, 4, P])
        wf2 = m.sb("wf2", [P, 512])
        bf2 = m.sb("bf2", [P, 512])
        bias = m.sb("bias", [P, 512], BF16)
        b_hi = m.sb("b_hi", [P, 3, 512], BF16)
        b_rest = m.sb("b_rest", [P, 512])
        ones = m.sb("ones", [P, P], BF16)
        half = m.sb("half", [P, 1])
        blank = m.sb("blank", [P, 512], BF16)
        rec = m.sb("rec", [P, 2, 2, 2, REC])
        feat = m.sb("feat", [P, 2, 2, 2, REC])
        got = m.sb("got", [P, 2, 4, D])
        fT = m.sb("fT", [P, P])
        soft = m.sb("soft", [P, 512])
        h = m.sb("h", [P, 2, 512])
        dot0 = m.sb("dot0", [P, 2, 4, P])
        dot = m.sb("dot", [P, 2, P])
        m02 = m.sb("m02", [P, 4, 2, P])
        m1 = m.sb("m1", [P, 4, P])
        m3 = m.sb("m3", [P, 4, 3, P])
        hot = m.sb("hot", [P, 2, 4, 4, P])
        sums = m.sb("sums", [P, 2, 2 * D])
        ps_f = m.psum("ps_f", [P, 512])
        ps_h = m.psum("ps_h", [P, 512])
        ps_w = m.psum("ps_w", [P, 2, 512])
        ps_a = m.psum("ps_a", [P, 2, 2, 512])

        w_loaded = m.sem("w_loaded")
        link_a = m.sem("link_a")
        link_d = m.sem("link_d")
        wf1_clear = m.sem("wf1_clear")
        weights = m.sem("weights")
        rec_in = [m.sem(f"rec_in{k}") for k in range(2)]
        feat_in = [m.sem(f"feat_in{k}") for k in range(2)]
        got_in = [[m.sem(f"got_in{k}{c}") for c in range(4)] for k in range(2)]
        passed = shared["passed"]
        turned = m.sem("turned")
        fT_ok = m.sem("fT_ok")
        pre_h = m.sem("pre_h")
        soft_ok = m.sem("soft_ok")
        h_ok = m.sem("h_ok")
        w_ok = m.sem("w_ok")
        hot_ok = m.sem("hot_ok")
        dot0_ok = m.sem("dot0_ok")
        msg_ok = m.primed("msg_ok")
        spent = m.primed("spent")
        sums_ok = m.primed("sums_ok")
        sums_out = m.primed_dma("sums_out")

        start_word = m.sb("start_word", [P, 2 * len(m.dma_sems)])
        block = ctx.enter_context(nc.Block())

        def load_records(sp, tile, q, k, sem):
            row = ds(q * 4 * P, 4 * P) if not isinstance(q, int) else slice(q * 4 * P, (q + 1) * 4 * P)
            sp.dma_start(tile[:, k].rearrange("p g j w -> p g (j w)"),
                         io["sorted"][row, :].rearrange("(g p j) w -> p g (j w)", g=2, j=2)).then_inc(sem[k], 16)

        @block.sync
        def _(sp):
            m.prime(sp, io, start_word)
            sp.wait_ge(wf1_clear, 1)
            for c in range(4):
                sp.dma_start(wf1[c * REC:c * REC + N_RBF + 1, c, :], io["wf1"]).then_inc(w_loaded, 16)
            sp.dma_start(wf2[:], io["wf2"]).then_inc(w_loaded, 16)
            sp.dma_start(bf2[:], io["bf2"].to_broadcast([P, 512])).then_inc(w_loaded, 16)
            for k in range(2):
                load_records(sp, rec, k, k, rec_in)
                load_records(sp, feat, k, k, feat_in)
            for k in range(2):
                sp.wait_ge(turned, k + 1)
                load_records(sp, feat, k + 2, k, feat_in)

            def put_sums(entry, k):
                at = sp.value_load(bkt_i[0:1, ds(entry, 1)], min_val=0, max_val=NB - 1)
                sp.wait_ge(sums_ok, ONE + entry + 1)
                sp.sem_inc(shared["passed"], 1)
                sp.wait_ge(sums_out, ONE_DMA + entry * 16)
                sp.sem_inc(shared["passed"], 1)
                sp.dma_start(io["agg"][ds(at * P, P), :], sums[:, k, :]).then_inc(sums_out, 16)

            with sp.Fori(0, NQ // 2) as i:
                for u in range(2):
                    put_sums(4 * i + 2 * u, 1)
                    sp.wait_ge(turned, 2 * i + u + 3)
                    load_records(sp, feat, 2 * i + u + 4, u, feat_in)
                    sp.wait_ge(msg_ok, ONE + 8 * i + 4 * u + 5)
                    load_records(sp, rec, 2 * i + u + 2, u, rec_in)
                    put_sums(4 * i + 2 * u + 1, 0)
            put_sums(NG, 1)
            sp.wait_ge(sums_out, ONE_DMA + 16 * (NG + 1))
            for k in range(2):
                sp.wait_ge(rec_in[k], 16 * (NQ // 2 + 1))
                sp.wait_ge(feat_in[k], 16 * (NQ // 2 + 2))

        @block.gpsimd
        def _(pool):
            def gather(k, c):
                nc.gpsimd.indirect_dma_start(
                    out=got[:, k, c, :], out_offset=None, in_=io["table_a"],
                    in_offset=bass.IndirectOffsetOnAxis(
                        ap=rec[:, k, c // 2, c % 2, R_DST:R_DST + 1].bitcast(U32), axis=0)).then_inc(got_in[k][c], 16)

            def one_hots(k):
                for c in range(4):
                    word = rec[:, k, c // 2, c % 2]
                    last = nc.gpsimd.tensor_scalar(hot[:, k, c, 0, :], iota, word[:, R_TGT:R_TGT + 1],
                                                   word[:, R_CUT:R_CUT + 1], ALU.is_equal, ALU.mult)
                last.then_inc(hot_ok, 1)

            for k in range(2):
                pool.wait_ge(rec_in[k], 16)
                for c in range(4):
                    gather(k, c)
                one_hots(k)
            with pool.Fori(1, NQ // 2) as i:
                for k in range(2):
                    pool.wait_ge(rec_in[k], 16 * i + 16)
                    for c in range(4):
                        pool.wait_ge(msg_ok, ONE + 8 * i + 4 * k + c - 6)
                        pool.sem_inc(passed, 1)
                        gather(k, c)
                    pool.wait_ge(spent, ONE + 8 * i + 4 * k - 3)
                    pool.sem_inc(passed, 1)
                    one_hots(k)
            pool.wait_ge(msg_ok, ONE + NQ * 4 - 3)
            pool.wait_ge(rec_in[0], 16 * (NQ // 2) + 16)
            for c in range(4):
                gather(0, c)
            pool.wait_ge(spent, ONE + 4 * NQ - 3)
            one_hots(0)

        @block.tensor
        def _(pe):
            def turn(k, count):
                pe.wait_ge(feat_in[k], count)
                nc.tensor.transpose(ps_f[:, 0:P], feat[:, k].rearrange("p g j w -> p (g j w)"), ident)\
                  .then_inc(turned, 1)

            def hidden(count):
                pe.wait_ge(fT_ok, count)
                for c in range(4):
                    mm = nc.tensor.matmul(ps_h[:, c * P:(c + 1) * P], wf1[:, c, :], fT[:], start=True, stop=True)
                mm.then_inc(pre_h, 1)

            def filters(k, c, n=None, count=None):
                if n is not None:
                    pe.wait_ge(msg_ok, ONE + n + 2)
                if count is not None:
                    pe.wait_ge(h_ok, count)
                nc.tensor.matmul(ps_w[:, c % 2, :], ones[0:65, :], bias[0:65, :], start=True, stop=False)
                nc.tensor.matmul(ps_w[:, c % 2, :], h[:, k, c * P:(c + 1) * P], wf2[:],
                                 start=False, stop=True).then_inc(w_ok, 1)

            def add_up(q, c, n, group):
                b, g = c, c // 2
                pe.wait_ge(msg_ok, ONE + n + 2)
                one, times_y = hot[:, q, c, 0, :], hot[:, q, c, 1:4, :].rearrange("p k n -> p (k n)")
                if c % 2 == 0:
                    pe.wait_ge(sums_ok, ONE + group)
                first, last = c % 2 == 0, c % 2 == 1
                A, B = ps_a[:, g, 0, :], ps_a[:, g, 1, :]
                nc.tensor.matmul(A[:, 0:P], m02[:, b, 0, :], one, start=first, stop=False,
                                 skip_group_check=True)
                nc.tensor.matmul(A[:, P:512], m02[:, b, 1, :], times_y,
                                 start=False, stop=last, skip_group_check=True)
                nc.tensor.matmul(B[:, 0:P], m1[:, b, :], one, start=first, stop=False,
                                 skip_group_check=True)
                for k in range(3):
                    mm = nc.tensor.matmul(B[:, (k + 1) * P:(k + 2) * P], m3[:, b, k, :], one,
                                          start=False, stop=last and k == 2, skip_group_check=True)
                mm.then_inc(spent, 1)

            pe.wait_ge(weights, 3)
            for bank in range(2):
                mm = nc.tensor.matmul(ps_a[:, 1, bank, :], blank[:, 0:P], blank[:], start=True, stop=True)
            mm.then_inc(spent, 1)
            for k in range(2):
                turn(k, 16)
                hidden(k + 1)
                filters(0, k, count=1)
            with pe.Fori(0, NQ // 2) as i:
                for u in range(2):
                    n, g = 8 * i + 4 * u, 4 * i + 2 * u
                    filters(u, 2, n)
                    add_up(u, 0, n, g)
                    filters(u, 3, n + 1)
                    turn(u, 16 * (i + 2))
                    add_up(u, 1, n + 1, g)
                    filters(1 - u, 0, n + 2, 2 * i + u + 2)
                    add_up(u, 2, n + 2, g + 1)
                    filters(1 - u, 1, n + 3)
                    hidden(2 * i + u + 3)
                    add_up(u, 3, n + 3, g + 1)

        @block.scalar
        def _(act):
            link = Link(act, link_a)
            act.wait_ge(w_loaded, 96)
            nc.scalar.mul(wf2[:, 0:P], wf2[:, 0:P], Y0)
            nc.scalar.mul(wf2[:, 2 * P:3 * P], wf2[:, 2 * P:3 * P], float(1 / np.sqrt(3)))
            nc.scalar.mul(wf2[:, 3 * P:], wf2[:, 3 * P:], Y0).then_inc(weights, 1)

            def features(count):
                act.wait_ge(turned, count)
                nc.scalar.copy(fT[:], ps_f[:, 0:P]).then_inc(fT_ok, 1)

            def softplus(count):
                act.wait_ge(pre_h, count)
                link(nc.scalar.activation(soft[:], ps_h[:], ACT.Abs))
                link(nc.scalar.activation(soft[:], soft[:], ACT.Exp, scale=-1.0))
                nc.scalar.activation(soft[:], soft[:], ACT.Ln, bias=half[:], scale=0.5).then_inc(soft_ok, 1)

            def products(k, chunks, n, count):
                for c in chunks:
                    word = rec[:, k, c // 2, c % 2]
                    act.wait_ge(got_in[k][c], count)
                    for j in range(3):
                        nc.scalar.mul(hot[:, k, c, 1 + j, :], hot[:, k, c, 0, :], word[:, R_Y + j:R_Y + j + 1])
                    nc.scalar.mul(dot0[:, k, c, :], got[:, k, c, P:2 * P], word[:, R_Y:R_Y + 1]).then_inc(dot0_ok, 1)

            act.wait_ge(weights, 3)
            features(1)
            softplus(1)
            features(2)
            act.wait_ge(hot_ok, 1)
            products(0, range(4), 0, 16)
            with act.Fori(0, NQ // 2) as i:
                link.enter(i, 4)
                for u in range(2):
                    q = 2 * i + u + 1
                    softplus(q + 1)
                    act.wait_ge(hot_ok, q + 1)
                    products(1 - u, range(4), 4 * q, 16 * (i + 1 + u))
                    features(q + 2)
                link.leave(NQ // 2)

        @block.vector
        def _(dve):
            link = Link(dve, link_d)
            nc.vector.memset(wf1[:], 0.0).then_inc(wf1_clear, 1)
            link(nc.vector.memset(half[:], 0.5))
            link(nc.vector.memset(ones[:], 1.0))
            link(nc.vector.memset(blank[:], 0.0))
            link(nc.vector.memset(bias[:], 0.0))
            link(nc.vector.memset(sums[:], 0.0))
            dve.wait_ge(w_loaded, 96)
            link(nc.vector.tensor_scalar(bf2[:, 0:P], bf2[:, 0:P], Y0, None, ALU.mult))
            link(nc.vector.tensor_scalar(bf2[:, 2 * P:3 * P], bf2[:, 2 * P:3 * P], float(1 / np.sqrt(3)), None, ALU.mult))
            link(nc.vector.tensor_scalar(bf2[:, 3 * P:], bf2[:, 3 * P:], Y0, None, ALU.mult))
            rest = bf2
            for part in range(3):
                link(nc.vector.tensor_copy(b_hi[:, part, :], rest[:]))
                link(nc.vector.tensor_copy(bias[32 * part:32 * part + 1, :], b_hi[32 * part:32 * part + 1, part, :]))
                link(nc.vector.tensor_tensor(b_rest[:], rest[:], b_hi[:, part, :], ALU.subtract))
                rest = b_rest
            nc.vector.memset(dot[:], 0.0).then_inc(weights, 1)
            nc.vector.memset(m1[:], 0.0).then_inc(weights, 1)
            dve.wait_ge(weights, 3)
            nc.vector.memset(m3[:], 0.0).then_inc(msg_ok, 1)
            dve.wait_ge(msg_ok, ONE + 1)

            def h_part(k, count):
                dve.wait_ge(soft_ok, count)
                nc.vector.scalar_tensor_tensor(out=h[:, k, :], in0=ps_h[:], scalar=0.0, in1=soft[:],
                                               op0=ALU.max, op1=ALU.add).then_inc(h_ok, 1)

            def messages(k, c, n, count):
                b = c % 2
                word = rec[:, k, c // 2, b]
                row = got[:, k, c, :]
                dve.wait_ge(spent, ONE + n - 2)
                dve.wait_ge(dot0_ok, n + 1)
                link(nc.vector.scalar_tensor_tensor(out=dot[:, b, :], in0=row[:, 2 * P:3 * P],
                                                    scalar=word[:, R_Y + 1:R_Y + 2], in1=dot0[:, k, c, :],
                                                    op0=ALU.mult, op1=ALU.add))
                link(nc.vector.scalar_tensor_tensor(out=dot[:, b, :], in0=row[:, 3 * P:4 * P],
                                                    scalar=word[:, R_Y + 2:R_Y + 3], in1=dot[:, b, :],
                                                    op0=ALU.mult, op1=ALU.add))
                dve.wait_ge(w_ok, n + 1)
                W = ps_w[:, b, :]
                nc.vector.tensor_tensor(m1[:, c, :], dot[:, b, :], W[:, 2 * P:3 * P], ALU.mult)
                nc.vector.tensor_tensor(m02[:, c], row[:, 0:P].unsqueeze(1).to_broadcast([P, 2, P]),
                                        W[:, 0:2 * P].rearrange("p (j f) -> p j f", j=2), ALU.mult)
                nc.vector.tensor_tensor(m3[:, c], row[:, P:].rearrange("p (j f) -> p j f", j=3),
                                        W[:, 3 * P:].unsqueeze(1).to_broadcast([P, 3, P]),
                                        ALU.mult).then_inc(msg_ok, 1)

            def add_group(k, entry):
                dve.wait_ge(spent, ONE + 2 * entry + 1)
                dve.wait_ge(sums_out, ONE_DMA + 16 * entry)
                dve.wait_ge(sums_ok, ONE + entry)
                nc.vector.scalar_tensor_tensor(
                    out=sums[:, k, :], in0=sums[:, 1 - k, :], scalar=keep[:, ds(entry, 1)],
                    in1=ps_a[:, k].rearrange("p b n -> p (b n)"), op0=ALU.mult, op1=ALU.add).then_inc(sums_ok, 1)

            h_part(0, 1)
            with dve.Fori(0, NQ // 2) as i:
                link.enter(i, 16)
                for u in range(2):
                    n, entry = 8 * i + 4 * u, 4 * i + 2 * u
                    messages(u, 0, n, 16 * i + 16)
                    messages(u, 1, n + 1, 16 * i + 16)
                    add_group(1, entry)
                    messages(u, 2, n + 2, 16 * i + 16)
                    h_part(1 - u, 2 * i + u + 2)
                    messages(u, 3, n + 3, 16 * i + 16)
                    add_group(0, entry + 1)
                link.leave(NQ // 2)
            add_group(1, NG)


class Norms:

    def __init__(self, nc, m, tiles, passed):
        self.nc, self.tiles = nc, tiles
        self.stats = m.sb("stats", [P, tiles, 6])
        self.mv = m.sb("mv", [P, tiles, 2])
        self.small = m.sb("small", [P, 5, tiles])
        self.stats_ok = m.sem("stats_ok")
        self.passed = passed
        self.var_ok = m.sem("var_ok")
        self.std_ok = m.sem("std_ok")

    def tile(self, dve, j, rows):
        dve.sem_inc(self.passed, 1)
        self.nc.vector.bn_stats(self.stats[:, j, :], rows).then_inc(self.stats_ok, 1)

    def scale(self, dve, link, stats_count, batch):
        v, r, t, out, std = (self.small[:, k, :] for k in range(5))
        dve.wait_ge(self.stats_ok, stats_count)
        dve.sem_inc(self.passed, 1)
        for j in range(self.tiles):
            last = self.nc.vector.bn_aggr(self.mv[:, j, :], self.stats[:, j, :])
        link(last)
        self.nc.vector.tensor_scalar(v, self.mv[:, :, 1], EPS, None, ALU.add).then_inc(self.var_ok, 1)
        dve.wait_ge(self.var_ok, batch)
        dve.wait_ge(self.std_ok, batch)
        link(self.nc.vector.reciprocal(r, std))
        link(self.nc.vector.tensor_tensor(t, r, r, ALU.mult))
        link(self.nc.vector.tensor_tensor(t, t, v, ALU.mult))
        link(self.nc.vector.tensor_scalar(t, t, -0.5, 1.5, ALU.mult, ALU.add))
        link(self.nc.vector.tensor_tensor(out, r, t, ALU.mult))

    LINKS = 6

    def root(self, act, batch):
        act.wait_ge(self.var_ok, batch)
        self.nc.scalar.activation(self.small[:, 4, :], self.small[:, 0, :], ACT.Sqrt).then_inc(self.std_ok, 1)

    def apply(self, out, rows, j):
        return self.nc.vector.tensor_scalar(out, rows, self.mv[:, j, 0:1], self.small[:, 3, j:j + 1],
                                            ALU.subtract, ALU.mult)


def node_layers(nc, io, shared):
    with ExitStack() as ctx:
        m = Space(nc, ctx, "p3")
        const, acc = shared["const"], shared["acc"]
        ident = const[:, C_ID:C_ID + P]
        TB = 7
        NBATCH = NB // TB
        agg = m.sb("agg", [P, TB, 2 * D])
        w1s = m.sb("w1s", [P, 2, P])
        w1v = m.sb("w1v", [P, 2, P])
        w2s = m.sb("w2s", [P, P])
        w2v = m.sb("w2v", [P, P])
        qup = m.sb("qup", [P, 4, FF], BF16)
        qdn = m.sb("qdn", [P, 2, D], BF16)
        wg = m.sb("wg", [P, 4, D])
        bias = m.sb("bias", [P, D])
        ident_b = m.sb("ident_b", [P, P], BF16)
        onesf = m.sb("onesf", [P, P])
        half = m.sb("half", [P, 1])
        wsum = m.sb("wsum", [P, 8])
        soft = m.sb("soft", [P, TB, P])
        sT = agg[:, :, 0:D].rearrange("p j (k n) -> p j k n", k=4)
        xn = m.sb("xn", [P, TB, D])
        xp = m.sb("xp", [P, TB, D])
        wup = xp[:, 0:2, :].rearrange("p a (b f) -> p (a b) f", f=FF)
        wdn = xp[:, 2:4, :]
        tmp = m.sb("tmp", [P, 2, D])
        qb = m.sb("qb", [P, 2, D], BF16)
        qT = m.sb("qT", [P, 2, 4, P], BF16)
        hid = m.sb("hid", [P, TB, FF])
        xT = m.sb("xT", [P, 2, 4, P])
        row = m.sb("row", [P, 2, D])
        scal = m.sb("scal", [P, 8, TB])
        norms = Norms(nc, m, TB, shared["passed"])
        ps_1 = m.psum("ps_1", [P, 2, 512])
        ps_2 = m.psum("ps_2", [P, 2, 512])
        ps_b = m.psum("ps_b", [P, 2, 1024], BF16)
        ps_3 = m.psum("ps_3", [P, 2, 512])

        x_in = m.sem("x_in")
        w_in = m.sem("w_in")
        link_d = m.sem("link_d")
        link_a = m.sem("link_a")
        agg_in = [m.sem(f"agg_in{k}") for k in range(TB)]
        scaled = m.sem("scaled")
        measured = m.sem("measured")
        ternary = m.sem("ternary")
        totals = m.sem("totals")
        first_ok = m.primed("first_ok")
        soft_ok = m.sem("soft_ok")
        vT_ok = m.primed("vT_ok")
        sT_ok = m.primed("sT_ok")
        second_ok = m.primed("second_ok")
        x1_ok = m.primed("x1_ok")
        q_ok = m.sem("q_ok")
        qturn_ok = m.sem("qturn_ok")
        qT_ok = m.sem("qT_ok")
        up_ok = m.primed("up_ok")
        relu_ok = m.sem("relu_ok")
        q2_ok = m.sem("q2_ok")
        down_ok = m.primed("down_ok")
        x2_ok = m.primed("x2_ok")
        xn_ok = m.sem("xn_ok")
        xturn_ok = m.sem("xturn_ok")
        xT_ok = m.sem("xT_ok")
        prod_ok = m.primed("prod_ok")
        row_ok = m.primed("row_ok")
        row_out = [m.primed_dma(f"row_out{k}") for k in range(2)]
        biased = m.sem("biased")

        start_word = m.sb("start_word", [P, 2 * len(m.dma_sems)])
        block = ctx.enter_context(nc.Block())

        EVEN, ODD = (TB + 1) // 2, TB // 2

        def uses(i, j):
            return (EVEN if j % 2 == 0 else ODD) * i + j // 2 + 1

        @block.sync
        def _(sp):
            m.prime(sp, io, start_word)
            weights = [(w1s, "w1s"), (w1v, "w1v"), (w2s, "w2s"), (w2v, "w2v"), (wup, "wup"), (wdn, "wdn"), (wg, "wg")]
            for tile, name in weights:
                sp.dma_start(tile[:], io[name]).then_inc(w_in, 16)
            sp.dma_start(bias[:], io["gnn_bias"].to_broadcast([P, D])).then_inc(w_in, 16)
            sp.dma_start(acc[:], io["x"][0:NPAD, :].rearrange("(t p) d -> p t d", p=P)).then_inc(x_in, 16)

            def load_sums(t, j):
                rows = slice(t * P, (t + 1) * P) if isinstance(t, int) else ds(t * P, P)
                sp.dma_start(agg[:, j, :], io["agg"][rows, :]).then_inc(agg_in[j], 16)

            def store_rows(t, j):
                sp.wait_ge(row_ok, ONE + t + 1)
                rows = slice(t * P, (t + 1) * P) if isinstance(t, int) else ds(t * P, P)
                sp.dma_start(io["table_b"][rows, :], row[:, j % 2, :]).then_inc(row_out[j % 2], 16)

            for j in range(TB):
                load_sums(j, j)

            def next_sums(i):
                for j in range(TB):
                    sp.wait_ge(second_ok, ONE + i * TB + j + 1)
                    sp.sem_inc(shared["passed"], 1)
                    load_sums((i + 1) * TB + j, j)

            next_sums(0)
            with sp.Fori(1, NBATCH - 1) as i:
                next_sums(i)
                for j in range(TB):
                    store_rows((i - 1) * TB + j, j)
            for t in range((NBATCH - 2) * TB, NB):
                store_rows(t, t % TB)
            for k in range(2):
                sp.wait_ge(row_out[k], ONE_DMA + 16 * NBATCH * (EVEN, ODD)[k])

        @block.tensor
        def _(pe):
            pe.wait_ge(measured, 1)
            nc.tensor.matmul(ps_1[:, 0, 0:2], onesf[:], wsum[:, 0:2], start=True, stop=True).then_inc(totals, 1)
            pe.wait_ge(scaled, 1)
            pe.wait_ge(ternary, 1)

            def products(i, tiles):
                for j in tiles:
                    t, b = i * TB, j % 2
                    pe.wait_ge(xn_ok, t + j + 1)
                    for k in range(4):
                        mm = nc.tensor.transpose(ps_2[:, b, k * P:(k + 1) * P], xp[:, j, k * P:(k + 1) * P], ident)
                    mm.then_inc(xturn_ok, 1)
                    pe.wait_ge(xT_ok, t + j + 1)
                    pe.wait_ge(row_ok, ONE + t + (j - 1 if j else 0))
                    for k in range(4):
                        mm = nc.tensor.matmul(ps_1[:, b, :], xT[:, b, k, :], wg[:, k, :], start=(k == 0), stop=(k == 3))
                    mm.then_inc(prod_ok, 1)

            def batch(i, first):
                t = i * TB

                def back(j):
                    pe.wait_ge(x1_ok, ONE + t + (j - 1 if j else 0))
                    for k in range(4):
                        mm = nc.tensor.matmul(ps_2[:, j % 2, k * P:(k + 1) * P], sT[:, j, k, :],
                                              (w2s if k == 0 else w2v)[:], start=True, stop=True)
                    mm.then_inc(second_ok, 1)

                for j in range(TB):
                    b = j % 2
                    pe.wait_ge(agg_in[j], 16 * i + 16)
                    if j == 0 and not first:
                        pe.wait_ge(row_ok, ONE + t - TB)
                    pe.wait_ge(vT_ok, ONE + t + (j - 1 if j else 0))
                    for k in range(2):
                        nc.tensor.matmul(ps_1[:, b, 0:P], w1s[:, k, :], agg[:, j, k * D:k * D + P],
                                         start=(k == 0), stop=(k == 1), skip_group_check=True)
                    for k in range(2):
                        mm = nc.tensor.matmul(ps_1[:, b, P:], w1v[:, k, :], agg[:, j, k * D + P:(k + 1) * D],
                                              start=(k == 0), stop=(k == 1), skip_group_check=True)
                    mm.then_inc(first_ok, 1)
                pe.wait_ge(sT_ok, ONE + i + 1)
                for j in range(TB):
                    back(j)
                if not first:
                    pe.wait_ge(vT_ok, ONE + t + TB)
                    pe.wait_ge(x1_ok, ONE + t + TB)
                    products(i - 1, range(0, 4))
                for j in range(TB):
                    b = j % 2
                    pe.wait_ge(q_ok, t + j + 1)
                    for k in range(4):
                        mm = nc.tensor.transpose(ps_b[:, b, k * P:(k + 1) * P], qb[:, b, k * P:(k + 1) * P], ident_b[:])
                    mm.then_inc(qturn_ok, 1)
                    pe.wait_ge(qT_ok, 2 * t + j + 1)
                    for k in range(4):
                        mm = nc.tensor.matmul(ps_3[:, b, 0:FF], qT[:, b, k, :], qup[:, k, :], start=(k == 0), stop=(k == 3))
                    mm.then_inc(up_ok, 1)
                if not first:
                    products(i - 1, range(4, TB))
                for j in range(TB):
                    b = j % 2
                    pe.wait_ge(q2_ok, t + j + 1)
                    for k in range(2):
                        mm = nc.tensor.transpose(ps_b[:, b, k * P:(k + 1) * P], qb[:, b, k * P:(k + 1) * P], ident_b[:])
                    mm.then_inc(qturn_ok, 1)
                    pe.wait_ge(qT_ok, 2 * t + TB + j + 1)
                    pe.wait_ge(x2_ok, ONE + t + (j - 1 if j else 0))
                    for k in range(2):
                        mm = nc.tensor.matmul(ps_2[:, b, :], qT[:, b, k, :], qdn[:, k, :], start=(k == 0), stop=(k == 1))
                    mm.then_inc(down_ok, 1)

            batch(0, True)
            with pe.Fori(1, NBATCH) as i:
                batch(i, False)
            pe.wait_ge(x2_ok, ONE + NB)
            products(NBATCH - 1, range(TB))

        @block.scalar
        def _(act):
            act.wait_ge(w_in, 16 * 8)
            nc.scalar.mul(w1s[:], w1s[:], float(1 / np.sqrt(2 * P)))
            nc.scalar.mul(w1v[:], w1v[:], float(1 / np.sqrt(2 * P)))
            nc.scalar.mul(w2s[:], w2s[:], float(1 / np.sqrt(P)))
            nc.scalar.mul(w2v[:], w2v[:], float(1 / np.sqrt(P))).then_inc(scaled, 1)
            act.wait_ge(ternary, 1)
            link = Link(act, link_a)

            def products(i, tiles):
                for j in tiles:
                    t, b = i * TB, j % 2
                    act.wait_ge(xturn_ok, t + j + 1)
                    act.wait_ge(prod_ok, ONE + t + (j - 1 if j else 0))
                    nc.scalar.copy(xT[:, b], ps_2[:, b].rearrange("p (k n) -> p k n", k=4)).then_inc(xT_ok, 1)
                    act.wait_ge(prod_ok, ONE + t + j + 1)
                    act.wait_ge(row_out[b], ONE_DMA + 16 * (uses(i, j) - 1))
                    nc.scalar.copy(row[:, b, :], ps_1[:, b, :]).then_inc(row_ok, 1)

            def batch(i, first):
                t = i * TB
                for j in range(TB):
                    act.wait_ge(first_ok, ONE + t + j + 1)
                    nc.scalar.copy(sT[:, j], ps_1[:, j % 2, :].rearrange("p (k n) -> p k n", k=4)).then_inc(vT_ok, 1)
                act.wait_ge(sT_ok, ONE + i)
                act.wait_ge(vT_ok, ONE + t + TB)
                link(nc.scalar.activation(soft[:], sT[:, :, 0, :], ACT.Abs))
                link(nc.scalar.activation(soft[:], soft[:], ACT.Exp, scale=-1.0))
                nc.scalar.activation(soft[:], soft[:], ACT.Ln, bias=half[:], scale=0.5).then_inc(soft_ok, 1)
                norms.root(act, 2 * i + 1)
                if not first:
                    products(i - 1, range(0, 4))
                for j in range(TB):
                    b = j % 2
                    act.wait_ge(qturn_ok, 2 * t + j + 1)
                    act.wait_ge(up_ok, ONE + t + (j - 1 if j else 0))
                    nc.scalar.copy(qT[:, b], ps_b[:, b, 0:D].rearrange("p (k n) -> p k n", k=4)).then_inc(qT_ok, 1)
                    act.wait_ge(up_ok, ONE + t + j + 1)
                    nc.scalar.activation(hid[:, j, :], ps_3[:, b, 0:FF], ACT.Relu, scale=scal[:, 2, j:j + 1]).then_inc(relu_ok, 1)
                if not first:
                    products(i - 1, range(4, TB))
                for j in range(TB):
                    b = j % 2
                    act.wait_ge(qturn_ok, 2 * t + TB + j + 1)
                    act.wait_ge(down_ok, ONE + t + (j - 1 if j else 0))
                    nc.scalar.copy(qT[:, b, 0:2], ps_b[:, b, 0:FF].rearrange("p (k n) -> p k n", k=2)).then_inc(qT_ok, 1)
                norms.root(act, 2 * i + 2)

            batch(0, True)
            with act.Fori(1, NBATCH) as i:
                link.enter(i - 1, 2)
                batch(i, False)
                link.leave(NBATCH - 1)
            products(NBATCH - 1, range(TB))

        @block.gpsimd
        def _(pool):
            pool.wait_ge(w_in, 16 * 8)
            with pool.Fori(0, NB) as t:
                pool.wait_ge(xn_ok, t + 1)
                nc.gpsimd.tensor_tensor(acc[:, ds(t, 1), :], acc[:, ds(t, 1), :], bias[:].unsqueeze(1), ALU.add)\
                  .then_inc(biased, 1)

        @block.vector
        def _(dve):
            link = Link(dve, link_d)
            nc.vector.memset(half[:], 0.5)
            link(nc.vector.memset(wsum[:], 0.0))
            link(nc.vector.memset(onesf[:], 1.0))
            link(nc.vector.tensor_copy(ident_b[:], ident))
            dve.wait_ge(w_in, 16 * 8)
            for k, w in ((0, wup), (1, wdn)):
                last = nc.vector.tensor_reduce(wsum[:, k:k + 1], w[:], AX.XY, ALU.add, apply_absolute_value=True)
                link(last)
            nc.vector.tensor_copy(wsum[:, 6:8], wsum[:, 0:2]).then_inc(measured, 1)
            dve.wait_ge(totals, 1)
            link(nc.vector.tensor_scalar(wsum[:, 2:4], ps_1[:, 0, 0:2], 1.0 / (D * FF), EPS, ALU.mult, ALU.max))
            link(nc.vector.reciprocal(wsum[:, 4:6], wsum[:, 2:4]))
            for k, w, q in ((0, wup, qup), (1, wdn, qdn)):
                link(nc.vector.tensor_scalar(w[:], w[:], wsum[:, 4 + k:5 + k], ROUND, ALU.mult, ALU.add))
                link(nc.vector.tensor_scalar(w[:], w[:], ROUND, 1.0, ALU.subtract, ALU.min))
                link(nc.vector.tensor_scalar(q[:], w[:], -1.0, None, ALU.max))
            nc.vector.tensor_scalar(wsum[:, 2:4], wsum[:, 2:4], 1.0 / 127.0, None, ALU.mult).then_inc(ternary, 1)
            dve.wait_ge(ternary, 1)
            dve.wait_ge(x_in, 16)

            def scales(a, k):
                link(nc.vector.tensor_scalar(scal[:, a, :], scal[:, a, :], EPS, None, ALU.max))
                link(nc.vector.reciprocal(scal[:, a + 1, :], scal[:, a, :]))
                nc.vector.tensor_scalar(scal[:, a + 1, :], scal[:, a + 1, :], 127.0, None, ALU.mult)
                link(nc.vector.tensor_scalar(scal[:, a + 2, :], scal[:, a, :], wsum[:, 2 + k:3 + k], None, ALU.mult))

            def batch(i, first):
                t = i * TB

                def row_of(j):
                    return acc[:, ds(t + j, 1), :].rearrange("p o d -> p (o d)")

                def add_graph(j):
                    dve.wait_ge(second_ok, ONE + t + j + 1)
                    a, o = row_of(j), ps_2[:, j % 2, :]
                    nc.vector.tensor_tensor(a[:, 0:P], a[:, 0:P], o[:, 0:P], ALU.add)
                    v = a[:, P:].rearrange("p (d c) -> p c d", c=3)
                    nc.vector.tensor_tensor(v, v, o[:, P:].rearrange("p (c d) -> p c d", c=3), ALU.add).then_inc(x1_ok, 1)
                    dve.wait_ge(x1_ok, ONE + t + j + 1)
                    norms.tile(dve, j, a)

                dve.wait_ge(soft_ok, i + 1)
                nc.vector.scalar_tensor_tensor(out=sT[:, :, 0, :], in0=sT[:, :, 0, :], scalar=0.0, in1=soft[:],
                                               op0=ALU.max, op1=ALU.add).then_inc(sT_ok, 1)
                for j in range(TB):
                    add_graph(j)
                norms.scale(dve, link, 2 * t + TB, 2 * i + 1)
                for j in range(TB):
                    link(norms.apply(xn[:, j, :], row_of(j), j))
                    link(nc.vector.tensor_reduce(scal[:, 0, j:j + 1], xn[:, j, :], AX.X, ALU.max, apply_absolute_value=True))
                scales(0, 0)
                for j in range(TB):
                    b = j % 2
                    if j >= 2:
                        dve.wait_ge(qturn_ok, 2 * t + j - 1)
                    link(nc.vector.tensor_scalar(tmp[:, b, :], xn[:, j, :], scal[:, 1, j:j + 1], ROUND, ALU.mult, ALU.add))
                    nc.vector.tensor_scalar(qb[:, b, :], tmp[:, b, :], ROUND, 127.0, ALU.subtract, ALU.min).then_inc(q_ok, 1)
                for j in range(TB):
                    dve.wait_ge(relu_ok, t + j + 1)
                    link(nc.vector.tensor_scalar(hid[:, j, :], hid[:, j, :], ROUND, ROUND, ALU.add, ALU.subtract))
                    link(nc.vector.tensor_scalar(hid[:, j, :], hid[:, j, :], 127.0, 0.0, ALU.min, ALU.max,
                                                 accum_out=scal[:, 3, j:j + 1]))
                scales(3, 1)

                def add_ffn(j):
                    dve.wait_ge(down_ok, ONE + t + j + 1)
                    a = row_of(j)
                    nc.vector.scalar_tensor_tensor(out=a, in0=ps_2[:, j % 2, :], scalar=scal[:, 5, j:j + 1], in1=a,
                                                   op0=ALU.mult, op1=ALU.add).then_inc(x2_ok, 1)
                    dve.wait_ge(x2_ok, ONE + t + j + 1)
                    norms.tile(dve, j, a)

                for j in range(TB):
                    b = j % 2
                    if j >= 2:
                        dve.wait_ge(qturn_ok, 2 * t + TB + j - 1)
                    link(nc.vector.tensor_scalar(tmp[:, b, 0:FF], hid[:, j, :], scal[:, 4, j:j + 1], ROUND, ALU.mult, ALU.add))
                    nc.vector.tensor_scalar(qb[:, b, 0:FF], tmp[:, b, 0:FF], ROUND, 127.0, ALU.subtract, ALU.min).then_inc(q2_ok, 1)
                    if j:
                        add_ffn(j - 1)
                add_ffn(TB - 1)
                norms.scale(dve, link, 2 * t + 2 * TB, 2 * i + 2)
                for j in range(TB):
                    if not first:
                        dve.wait_ge(xturn_ok, t - TB + j + 1)
                    norms.apply(xp[:, j, :], row_of(j), j).then_inc(xn_ok, 1)

            batch(0, True)
            with dve.Fori(1, NBATCH) as i:
                link.enter(i - 1, 2 * Norms.LINKS + 6 + 2 * TB + 3 * TB + TB)
                batch(i, False)
                link.leave(NBATCH - 1)
            dve.wait_ge(biased, NB)


def neighbour_sums(nc, io, shared):
    with ExitStack() as ctx:
        m = Space(nc, ctx, "p4")
        const, bkt_i, acc = shared["const"], shared["bkt_i"], shared["acc"]
        passed = shared["passed"]
        iota = const[:, C_IOTA:C_IOTA + P]
        QB = 4
        STEPS = NQ // QB
        rec = m.sb("rec", [P, QB, 2, 2, REC])
        got = m.sb("got", [P, QB, 4, D])
        hot = m.sb("hot", [P, 2, 4, P])
        blank = m.sb("blank", [P, 512], BF16)
        ps_a = m.psum("ps_a", [P, 4, 512])
        rec_in = [m.sem(f"rec_in{k}") for k in range(QB)]
        got_in = [m.sem(f"got_in{k}") for k in range(QB)]
        blank_ok = m.sem("blank_ok")
        hot_ok = m.sem("hot_ok")
        spent = m.primed("spent")
        added = m.primed("added")
        block = ctx.enter_context(nc.Block())

        def load_records(sp, q, k):
            row = ds(q * 4 * P, 4 * P) if not isinstance(q, int) else slice(q * 4 * P, (q + 1) * 4 * P)
            sp.dma_start(rec[:, k].rearrange("p g j w -> p g (j w)"),
                         io["sorted"][row, :].rearrange("(g p j) w -> p g (j w)", g=2, j=2)).then_inc(rec_in[k], 16)

        @block.sync
        def _(sp):
            m.prime(sp, io)
            for k in range(QB):
                load_records(sp, k, k)
            with sp.Fori(0, STEPS) as i:
                for u in range(QB):
                    sp.wait_ge(spent, ONE + 4 * (QB * i + u) + 5)
                    load_records(sp, QB * i + u + QB, u)
            for k in range(QB):
                sp.wait_ge(rec_in[k], 16 * (STEPS + 1))

        @block.gpsimd
        def _(pool):
            def gather(k):
                for c in range(4):
                    nc.gpsimd.indirect_dma_start(
                        out=got[:, k, c, :], out_offset=None, in_=io["table_b"],
                        in_offset=bass.IndirectOffsetOnAxis(
                            ap=rec[:, k, c // 2, c % 2, R_DST:R_DST + 1].bitcast(U32), axis=0)).then_inc(got_in[k], 16)

            for k in range(QB):
                pool.wait_ge(rec_in[k], 16)
                gather(k)
            with pool.Fori(1, STEPS) as i:
                for k in range(QB):
                    pool.wait_ge(rec_in[k], 16 * i + 16)
                    pool.wait_ge(spent, ONE + 4 * (QB * i + k - QB) + 5)
                    pool.sem_inc(passed, 1)
                    gather(k)

        @block.tensor
        def _(pe):
            pe.wait_ge(blank_ok, 1)
            nc.tensor.matmul(ps_a[:, 3, :], blank[:, 0:P], blank[:], start=True, stop=True).then_inc(spent, 1)
            with pe.Fori(0, STEPS) as i:
                for u in range(QB):
                    q = QB * i + u
                    pe.wait_ge(hot_ok, q + 1)
                    pe.wait_ge(got_in[u], 64 * i + 64)
                    for c in range(4):
                        g = (2 * u + c // 2) % 4
                        if c % 2 == 0:
                            pe.wait_ge(added, ONE + 2 * q + c // 2 - 2)
                        nc.tensor.matmul(ps_a[:, g, :], hot[:, u % 2, c, :], got[:, u, c, :],
                                         start=(c % 2 == 0), stop=(c % 2 == 1)).then_inc(spent, 1)

        @block.vector
        def _(dve):
            nc.vector.memset(blank[:], 0.0).then_inc(blank_ok, 1)

            def one_hots(q, k, count):
                dve.wait_ge(rec_in[k], count)
                if not isinstance(q, int):
                    dve.wait_ge(spent, ONE + 4 * q - 3)
                for c in range(4):
                    word = rec[:, k, c // 2, c % 2]
                    last = nc.vector.tensor_scalar(hot[:, k % 2, c, :], iota, word[:, R_TGT:R_TGT + 1],
                                                   word[:, R_CUT:R_CUT + 1], ALU.is_equal, ALU.mult)
                last.then_inc(hot_ok, 1)

            def add_group(entry, k):
                dve.wait_ge(spent, ONE + 2 * entry + 1)
                at = dve.value_load(bkt_i[0:1, ds(entry, 1)], min_val=0, max_val=NB - 1)
                a = acc[:, ds(at, 1), :].rearrange("p o d -> p (o d)")
                dve.wait_ge(added, ONE + entry)
                nc.vector.tensor_tensor(a, a, ps_a[:, k, :], ALU.add).then_inc(added, 1)

            one_hots(0, 0, 16)
            with dve.Fori(0, STEPS) as i:
                for u in range(QB):
                    q = QB * i + u
                    one_hots(q + 1, (u + 1) % QB, 16 * i + 16 * (1 + (u + 1) // QB))
                    add_group(2 * q, (2 * u - 1) % 4)
                    add_group(2 * q + 1, 2 * u % 4)
            add_group(NG, 3)
            dve.wait_ge(added, ONE + NG + 1)


def route(nc, io, shared):
    with ExitStack() as ctx:
        m = Space(nc, ctx, "p5a")
        const, acc = shared["const"], shared["acc"]
        ident = const[:, C_ID:C_ID + P]
        place, weight, tile_expert = shared["place"], shared["weight"], shared["tile_expert"]
        TB, E = 7, N_EXP
        NBATCH = NB // TB
        tri = m.sb("tri", [P, P])
        tile_no = m.sb("tile_no", [P, NT])
        tile_f = m.sb("tile_f", [P, NT])
        ones = m.sb("ones", [P, P])
        zero = m.sb("zero", [P, NB])
        rw = m.sb("rw", [P, 4, E])
        rb = m.sb("rb", [P, 1, E])
        lower = m.sb("lower", [P, 1, E * E])
        xn = m.sb("xn", [P, TB, D])
        xT = m.sb("xT", [P, 2, 4, P])
        at = m.sb("at", [P, TB, 2], U32)
        norm = m.sb("norm", [P, 2, NB])
        prob = m.sb("prob", [P, NB, E])
        rank = m.sb("rank", [P, NB, E])
        cmp = xn[:].rearrange("p j d -> p (j d)")[:, 0:NB * E * E]
        tie = m.sb("tie", [P, NB, E])
        picked = m.sb("picked", [P, E, NB])
        total = m.sb("total", [P, E, NB])
        until = m.sb("until", [P, E, NB])
        chosen = m.sb("chosen", [P, NB, E])
        valued = m.sb("valued", [P, NB, E])
        place_f = m.sb("place_f", [P, NB, 2])
        red = m.sb("red", [P, 3, NB])
        count = m.sb("count", [P, 4, E])
        count_i = m.sb("count_i", [P, E], I32)
        norms = Norms(nc, m, TB, shared["passed"])
        ps_t = m.psum("ps_t", [P, 2, 512])
        ps_l = m.psum("ps_l", [P, 512])
        ps_c = m.psum("ps_c", [P, 2, 512])

        w_in = m.sem("w_in")
        x_in = m.sem("x_in")
        link_d = m.sem("link_d")
        xn_ok = m.sem("xn_ok")
        turned = m.primed("turned")
        xT_ok = m.primed("xT_ok")
        logits_ok = m.primed("logits_ok")
        kept = m.primed("kept")
        shifted = m.sem("shifted")
        exp_ok = m.sem("exp_ok")
        picked_ok = m.sem("picked_ok")
        summed = m.sem("summed")
        rows_ok = m.sem("rows_ok")
        scattered = shared["moved"]

        block = ctx.enter_context(nc.Block())

        @block.sync
        def _(sp):
            m.prime(sp, io)
            sp.dma_start(tri[:], io["consts"][:, C_TRI:C_TRI + P]).then_inc(w_in, 16)
            sp.dma_start(tile_no[:], io["consts"][:, C_GRP:C_GRP + NT]).then_inc(w_in, 16)
            sp.dma_start(rw[:], io["rw"]).then_inc(w_in, 16)
            sp.dma_start(rb[:, 0, :], io["rb"].to_broadcast([P, E])).then_inc(w_in, 16)
            sp.dma_start(lower[:, 0, :], io["lower"].to_broadcast([P, E * E])).then_inc(w_in, 16)
            sp.dma_start(shared["w1"][:], io["ew1"]).then_inc(x_in, 16)
            sp.dma_start(shared["b1"][:], io["b1"].to_broadcast([P, E * FF])).then_inc(x_in, 16)
            sp.wait_ge(x_in, 16 * 2)

        @block.gpsimd
        def _(pool):
            def scatter(j, count):
                pool.wait_ge(rows_ok, count)
                pool.sem_inc(shared["passed"], 1)
                for k in range(2):
                    nc.gpsimd.indirect_dma_start(
                        out=io["packed"], out_offset=bass.IndirectOffsetOnAxis(ap=at[:, j, k:k + 1], axis=0),
                        in_=xn[:, j, :], in_offset=None).then_inc(scattered[j], 16)

            with pool.Fori(0, NBATCH) as i:
                for j in range(TB):
                    scatter(j, i * TB + j + 1)
            for j in range(TB):
                pool.wait_ge(scattered[j], 32 * NBATCH)

        @block.tensor
        def _(pe):
            pe.wait_ge(w_in, 16 * 5)
            with pe.Fori(0, NBATCH) as i:
                t = i * TB
                for j in range(TB):
                    b = j % 2
                    pe.wait_ge(xn_ok, t + j + 1)
                    pe.wait_ge(xT_ok, ONE + t + max(j - 1, 0))
                    for k in range(4):
                        mm = nc.tensor.transpose(ps_t[:, b, k * P:(k + 1) * P], xn[:, j, k * P:(k + 1) * P], ident)
                    mm.then_inc(turned, 1)
                    if j == 0:
                        pe.wait_ge(kept, ONE + i)
                    if j:
                        logits(pe, nc, xT_ok, ONE + t + j, ps_l, xT, rw, j - 1, logits_ok)
                logits(pe, nc, xT_ok, ONE + t + TB, ps_l, xT, rw, TB - 1, logits_ok)
            pe.wait_ge(picked_ok, 1)
            flat = picked[:].rearrange("p e t -> p (e t)")
            nc.tensor.matmul(ps_c[:, 0, 0:E * NB], tri[:], flat, start=True, stop=True)
            nc.tensor.matmul(ps_c[:, 1, 0:E * NB], ones[:], flat, start=True, stop=True).then_inc(summed, 1)

        @block.scalar
        def _(act):
            with act.Fori(0, NBATCH) as i:
                norms.root(act, i + 1)
                for j in range(TB):
                    act.wait_ge(turned, ONE + i * TB + j + 1)
                    act.wait_ge(logits_ok, ONE + i * TB + max(j - 1, 0))
                    nc.scalar.copy(xT[:, j % 2], ps_t[:, j % 2, :].rearrange("p (k n) -> p k n", k=4)).then_inc(xT_ok, 1)
            act.wait_ge(shifted, 1)
            nc.scalar.activation(prob[:], prob[:], ACT.Exp).then_inc(exp_ok, 1)

        @block.vector
        def _(dve):
            link = Link(dve, link_d)
            link(nc.vector.memset(ones[:], 1.0))
            link(nc.vector.memset(zero[:], 0.0))
            dve.wait_ge(w_in, 16 * 5)

            def keep_logits(t):
                dve.wait_ge(logits_ok, ONE + t)
                nc.vector.tensor_tensor(prob[:, t - TB:t, :] if isinstance(t, int) else prob[:, ds(t - TB, TB), :],
                                        ps_l[:, 0:TB * E].rearrange("p (j e) -> p j e", j=TB),
                                        rb[:].to_broadcast([P, TB, E]), ALU.add).then_inc(kept, 1)

            def batch(i, first):
                t = i * TB

                def row_of(j):
                    return acc[:, ds(t + j, 1), :].rearrange("p o d -> p (o d)")

                for j in range(TB):
                    norms.tile(dve, j, row_of(j))
                if not first:
                    keep_logits(t)
                norms.scale(dve, link, (i + 1) * TB, i + 1)
                nc.vector.tensor_copy(norm[:, 0, ds(t, TB)], norms.mv[:, :, 0])
                nc.vector.tensor_copy(norm[:, 1, ds(t, TB)], norms.small[:, 3, :])
                for j in range(TB):
                    dve.wait_ge(turned, ONE + t + max(j - TB + 1, 0))
                    norms.apply(xn[:, j, :], row_of(j), j).then_inc(xn_ok, 1)

            batch(0, True)
            with dve.Fori(1, NBATCH) as i:
                link.enter(i - 1, Norms.LINKS)
                batch(i, False)
                link.leave(NBATCH - 1)
            keep_logits(NB)
            dve.wait_ge(kept, ONE + NBATCH)
            over = [P, NB, E]

            def each(k):
                return red[:, k, :].unsqueeze(2).to_broadcast(over)

            link(nc.vector.tensor_reduce(red[:, 0, :], prob[:], AX.X, ALU.max))
            nc.vector.tensor_tensor(prob[:], prob[:], each(0), ALU.subtract).then_inc(shifted, 1)
            dve.wait_ge(exp_ok, 1)
            link(nc.vector.tensor_reduce(red[:, 1, :], prob[:], AX.X, ALU.add))
            link(nc.vector.reciprocal(red[:, 2, :], red[:, 1, :]))
            link(nc.vector.tensor_tensor(prob[:], prob[:], each(2), ALU.mult))
            wide = [P, NB, E, E]
            mine, other = prob[:].unsqueeze(3).to_broadcast(wide), prob[:].unsqueeze(2).to_broadcast(wide)
            cmp4 = cmp.rearrange("p (t e f) -> p t e f", t=NB, e=E)
            cmp3 = cmp.rearrange("p (t q) -> p t q", t=NB)
            link(nc.vector.tensor_tensor(cmp4, other, mine, ALU.is_equal))
            link(nc.vector.tensor_tensor(cmp3, cmp3, lower[:].to_broadcast([P, NB, E * E]), ALU.mult))
            link(nc.vector.tensor_reduce(tie[:], cmp4, AX.X, ALU.add))
            link(nc.vector.tensor_tensor(cmp4, other, mine, ALU.is_gt))
            link(nc.vector.tensor_reduce(rank[:], cmp4, AX.X, ALU.add))
            link(nc.vector.tensor_tensor(rank[:], rank[:], tie[:], ALU.add))
            nc.vector.tensor_scalar(picked[:].rearrange("p e t -> p t e"), rank[:], 2.0, None, ALU.is_lt)\
              .then_inc(picked_ok, 1)
            dve.wait_ge(summed, 1)
            rows, tiles, first, start = (count[:, k, :] for k in range(4))
            link(nc.vector.tensor_copy(total[:].rearrange("p e t -> p (e t)"), ps_c[:, 1, 0:E * NB]))
            link(nc.vector.tensor_reduce(rows, total[:], AX.X, ALU.add))
            link(nc.vector.tensor_scalar(tiles, rows, float(P - 1), None, ALU.add))
            link(nc.vector.tensor_copy(count_i[:], tiles))
            link(nc.vector.tensor_scalar(count_i[:], count_i[:], 7, None, ALU.arith_shift_right))
            link(nc.vector.tensor_copy(tiles, count_i[:]))
            link(nc.vector.memset(first, 0.0))
            link(nc.vector.tensor_tensor_scan(first[:, 1:E], tiles[:, 0:E - 1], zero[:, 0:E - 1], 0.0, ALU.add, ALU.add))
            link(nc.vector.tensor_scalar(start, first, float(P), None, ALU.mult))
            for e in range(E):
                link(nc.vector.tensor_tensor_scan(until[:, e, :], total[:, e, :], zero[:], start[:, e:e + 1],
                                                  ALU.add, ALU.add))
            link(nc.vector.tensor_tensor(until[:], until[:], total[:], ALU.subtract))
            link(nc.vector.tensor_tensor(until[:], until[:], ps_c[:, 0, 0:E * NB].rearrange("p (e t) -> p e t", e=E),
                                         ALU.add))
            for k in range(2):
                link(nc.vector.tensor_scalar(chosen[:], rank[:], float(k), None, ALU.is_equal))
                link(nc.vector.tensor_tensor(valued[:], chosen[:], until[:].rearrange("p e t -> p t e"), ALU.mult))
                link(nc.vector.tensor_reduce(place_f[:, :, k], valued[:], AX.X, ALU.add))
                link(nc.vector.tensor_tensor(valued[:], chosen[:], prob[:], ALU.mult))
                link(nc.vector.tensor_reduce(weight[:, k, :], valued[:], AX.X, ALU.add))
            link(nc.vector.tensor_copy(place[:], place_f[:]))
            link(nc.vector.tensor_tensor(red[:, 1, :], weight[:, 0, :], weight[:, 1, :], ALU.add))
            link(nc.vector.tensor_scalar(red[:, 1, :], red[:, 1, :], 1e-9, None, ALU.add))
            link(nc.vector.reciprocal(red[:, 2, :], red[:, 1, :]))
            for k in range(2):
                link(nc.vector.tensor_tensor(weight[:, k, :], weight[:, k, :], red[:, 2, :], ALU.mult))

            def send(i, first_batch):
                for j in range(TB):
                    if not first_batch:
                        dve.wait_ge(scattered[j], 32 * i)
                    t = i * TB + j
                    one = slice(t, t + 1) if first_batch else ds(t, 1)
                    nc.vector.tensor_copy(at[:, j, :].unsqueeze(1), place[:, one, :])
                    nc.vector.tensor_scalar(xn[:, j, :].unsqueeze(1), acc[:, one, :], norm[:, 0, one], norm[:, 1, one],
                                            ALU.subtract, ALU.mult).then_inc(rows_ok, 1)

            send(0, True)
            link(nc.vector.memset(tile_f[:], 0.0))
            for e in range(1, E):
                link(nc.vector.scalar_tensor_tensor(out=tile_f[:], in0=tile_no[:], scalar=first[:, e:e + 1],
                                                    in1=tile_f[:], op0=ALU.is_ge, op1=ALU.add))
            link(nc.vector.tensor_copy(tile_expert[:], tile_f[:]))
            with dve.Fori(1, NBATCH) as i:
                send(i, False)


def logits(pe, nc, ready, count, ps_l, xT, rw, j, done):
    pe.wait_ge(ready, count)
    for k in range(4):
        mm = nc.tensor.matmul(ps_l[:, j * N_EXP:(j + 1) * N_EXP], xT[:, j % 2, k, :], rw[:, k, :],
                              start=(k == 0), stop=(k == 3))
    mm.then_inc(done, 1)


def expert_tiles(nc, io, shared):
    with ExitStack() as ctx:
        m = Space(nc, ctx, "p5b")
        ident = shared["const"][:, C_ID:C_ID + P]
        w1, b1, tile_expert = (shared[k] for k in ("w1", "b1", "tile_expert"))
        w2 = m.sb("w2", [P, N_EXP, 2, D])
        b2 = m.sb("b2", [P, N_EXP * D])
        rows = m.sb("rows", [P, 2, D])
        xT = m.sb("xT", [P, 2, 4, P])
        hid = m.sb("hid", [P, 2, FF])
        hT = m.sb("hT", [P, 2, 2, P])
        y = m.sb("y", [P, 2, D])
        ps_x = m.psum("ps_x", [P, 2, 512])
        ps_h = m.psum("ps_h", [P, 2, 512])
        ps_g = m.psum("ps_g", [P, 2, 512])
        ps_y = m.psum("ps_y", [P, 2, 512])
        w_in = m.sem("w_in")
        rows_in = [m.sem(f"rows_in{k}") for k in range(2)]
        turned = m.primed("turned")
        xT_ok = m.primed("xT_ok")
        first_ok = m.primed("first_ok")
        pre_ok = m.primed("pre_ok")
        hid_ok = m.primed("hid_ok")
        hturned = m.primed("hturned")
        hT_ok = m.primed("hT_ok")
        second_ok = m.primed("second_ok")
        y_ok = m.primed("y_ok")
        y_out = [m.primed_dma(f"y_out{k}") for k in range(2)]
        start_word = m.sb("start_word", [P, 2 * len(m.dma_sems)])
        block = ctx.enter_context(nc.Block())
        N2 = NT // 2

        def at(n):
            return slice(n, n + 1) if isinstance(n, int) else ds(n, 1)

        def tile_rows(n):
            return slice(n * P, (n + 1) * P) if isinstance(n, int) else ds(n * P, P)

        @block.sync
        def _(sp):
            m.prime(sp, io, start_word)

            def load(n, k):
                sp.dma_start(rows[:, k, :], io["packed"][tile_rows(n), :]).then_inc(rows_in[k], 16)

            def store(n, k):
                sp.wait_ge(y_ok, ONE + n + 1)
                sp.dma_start(io["results"][tile_rows(n), :], y[:, k, :]).then_inc(y_out[k], 16)

            for k in range(2):
                load(k, k)
            sp.dma_start(w2[:], io["ew2"]).then_inc(w_in, 16)
            sp.dma_start(b2[:], io["b2"].to_broadcast([P, N_EXP * D])).then_inc(w_in, 16)
            for k in range(2):
                sp.wait_ge(turned, ONE + k + 1)
                load(k + 2, k)
            with sp.Fori(0, N2 - 2) as i:
                for k in range(2):
                    sp.wait_ge(turned, ONE + 2 * i + k + 3)
                    load(2 * i + k + 4, k)
                    store(2 * i + k, k)
            for n in range(NT - 4, NT):
                store(n, n % 2)
            for k in range(2):
                sp.wait_ge(y_out[k], ONE_DMA + 16 * N2)

        @block.tensor
        def _(pe):
            def turn(n, k, count):
                pe.wait_ge(rows_in[k], count)
                pe.wait_ge(xT_ok, ONE + n - 1)
                for c in range(4):
                    mm = nc.tensor.transpose(ps_x[:, k, c * P:(c + 1) * P], rows[:, k, c * P:(c + 1) * P], ident)
                mm.then_inc(turned, 1)

            def first_layer(n, k):
                e = pe.value_load(tile_expert[0:1, at(n)], min_val=0, max_val=N_EXP - 1)
                pe.wait_ge(xT_ok, ONE + n + 1)
                pe.wait_ge(pre_ok, ONE + n - 1)
                for c in range(4):
                    mm = nc.tensor.matmul(ps_h[:, k, 0:FF], xT[:, k, c, :],
                                          w1[:, ds(e, 1), c, :].rearrange("p o f -> p (o f)"),
                                          start=(c == 0), stop=(c == 3))
                mm.then_inc(first_ok, 1)

            def turn_hidden(n, k):
                pe.wait_ge(hid_ok, ONE + n + 1)
                pe.wait_ge(hT_ok, ONE + n - 1)
                for f in range(2):
                    mm = nc.tensor.transpose(ps_g[:, k, f * P:(f + 1) * P], hid[:, k, f * P:(f + 1) * P], ident)
                mm.then_inc(hturned, 1)

            def second_layer(n, k):
                e = pe.value_load(tile_expert[0:1, at(n)], min_val=0, max_val=N_EXP - 1)
                pe.wait_ge(hT_ok, ONE + n + 1)
                pe.wait_ge(y_ok, ONE + n - 1)
                for f in range(2):
                    mm = nc.tensor.matmul(ps_y[:, k, :], hT[:, k, f, :],
                                          w2[:, ds(e, 1), f, :].rearrange("p o d -> p (o d)"),
                                          start=(f == 0), stop=(f == 1))
                mm.then_inc(second_ok, 1)

            turn(0, 0, 16)
            first_layer(0, 0)
            turn(1, 1, 16)
            pe.wait_ge(w_in, 32)
            with pe.Fori(0, N2 - 1) as i:
                for k in range(2):
                    n = 2 * i + k
                    first_layer(n + 1, 1 - k)
                    turn_hidden(n, k)
                    turn(n + 2, k, 16 * (i + 2))
                    second_layer(n, k)
            first_layer(NT - 1, 1)
            for k in range(2):
                turn_hidden(NT - 2 + k, k)
                second_layer(NT - 2 + k, k)

        @block.scalar
        def _(act):
            def copy_rows(n, k):
                act.wait_ge(turned, ONE + n + 1)
                act.wait_ge(first_ok, ONE + n - 1)
                nc.scalar.copy(xT[:, k], ps_x[:, k, :].rearrange("p (c n) -> p c n", c=4)).then_inc(xT_ok, 1)

            def gelu(n, k):
                act.wait_ge(pre_ok, ONE + n + 1)
                nc.scalar.activation(hid[:, k, :], hid[:, k, :], ACT.Gelu).then_inc(hid_ok, 1)

            def copy_hidden(n, k):
                act.wait_ge(hturned, ONE + n + 1)
                act.wait_ge(second_ok, ONE + n - 1)
                nc.scalar.copy(hT[:, k], ps_g[:, k, 0:FF].rearrange("p (f n) -> p f n", f=2)).then_inc(hT_ok, 1)

            copy_rows(0, 0)
            gelu(0, 0)
            copy_rows(1, 1)
            with act.Fori(0, N2 - 1) as i:
                for k in range(2):
                    n = 2 * i + k
                    copy_hidden(n, k)
                    gelu(n + 1, 1 - k)
                    copy_rows(n + 2, k)
            copy_hidden(NT - 2, 0)
            gelu(NT - 1, 1)
            copy_hidden(NT - 1, 1)

        @block.vector
        def _(dve):
            def first_bias(n, k):
                e = dve.value_load(tile_expert[0:1, at(n)], min_val=0, max_val=N_EXP - 1)
                dve.wait_ge(first_ok, ONE + n + 1)
                dve.wait_ge(hturned, ONE + n - 1)
                nc.vector.tensor_tensor(hid[:, k, :], ps_h[:, k, 0:FF], b1[:, ds(e * FF, FF)], ALU.add)\
                  .then_inc(pre_ok, 1)

            def second_bias(n, k, out_count):
                e = dve.value_load(tile_expert[0:1, at(n)], min_val=0, max_val=N_EXP - 1)
                dve.wait_ge(second_ok, ONE + n + 1)
                dve.wait_ge(y_out[k], ONE_DMA + 16 * out_count)
                nc.vector.tensor_tensor(y[:, k, :], ps_y[:, k, :], b2[:, ds(e * D, D)], ALU.add).then_inc(y_ok, 1)

            first_bias(0, 0)
            dve.wait_ge(w_in, 32)
            with dve.Fori(0, N2 - 1) as i:
                for k in range(2):
                    first_bias(2 * i + k + 1, 1 - k)
                    second_bias(2 * i + k, k, i)
            first_bias(NT - 1, 1)
            for k in range(2):
                second_bias(NT - 2 + k, k, N2 - 1)


def combine(nc, io, shared):
    with ExitStack() as ctx:
        m = Space(nc, ctx, "p5c")
        acc, place, weight = shared["acc"], shared["place"], shared["weight"]
        TB = 7
        NBATCH = NB // TB
        pair = m.sb("pair", [P, TB, 2, D])
        at = m.sb("at", [P, TB, 2], U32)
        staged = m.sem("staged")
        got, scattered = shared["moved"], 32 * NBATCH
        added = m.sem("added")
        out_ok = m.sem("out_ok")
        block = ctx.enter_context(nc.Block())

        @block.sync
        def _(sp):
            with sp.Fori(0, NBATCH) as i:
                sp.wait_ge(added, (i + 1) * TB)
                sp.dma_start(io["out"][ds(i * TB * P, TB * P), :].rearrange("(t p) d -> p t d", p=P),
                             acc[:, ds(i * TB, TB), :]).then_inc(out_ok, 16)
            sp.wait_ge(out_ok, 16 * NBATCH)

        @block.gpsimd
        def _(pool):
            def gather(i, j, first_batch):
                t = i * TB + j
                if not first_batch:
                    pool.wait_ge(added, t - TB + 1)
                one = slice(t, t + 1) if first_batch else ds(t, 1)
                nc.gpsimd.tensor_copy(at[:, j, :].unsqueeze(1), place[:, one, :]).then_inc(staged, 1)
                pool.wait_ge(staged, t + 1)
                pool.sem_inc(shared["passed"], 1)
                for k in range(2):
                    nc.gpsimd.indirect_dma_start(
                        out=pair[:, j, k, :], out_offset=None, in_=io["results"],
                        in_offset=bass.IndirectOffsetOnAxis(ap=at[:, j, k:k + 1], axis=0)).then_inc(got[j], 16)

            for j in range(TB):
                gather(0, j, True)
            with pool.Fori(1, NBATCH) as i:
                for j in range(TB):
                    gather(i, j, False)

        link_d = m.sem("link_d")

        @block.vector
        def _(dve):
            link = Link(dve, link_d)
            with dve.Fori(0, NBATCH) as i:
                link.enter(i, TB)
                for j in range(TB):
                    t = i * TB + j
                    a = acc[:, ds(t, 1), :].rearrange("p o d -> p (o d)")
                    dve.wait_ge(got[j], scattered + 32 * i + 32)
                    link(nc.vector.scalar_tensor_tensor(out=a, in0=pair[:, j, 0, :], scalar=weight[:, 0, ds(t, 1)],
                                                        in1=a, op0=ALU.mult, op1=ALU.add))
                    nc.vector.scalar_tensor_tensor(out=a, in0=pair[:, j, 1, :], scalar=weight[:, 1, ds(t, 1)],
                                                   in1=a, op0=ALU.mult, op1=ALU.add).then_inc(added, 1)
                link.leave(NBATCH)


def experts(nc, io, shared):
    with ExitStack() as ctx:
        m = Space(nc, ctx, "p5")
        shared["place"] = m.sb("place", [P, NB, 2], U32)
        shared["weight"] = m.sb("weight", [P, 2, NB])
        shared["moved"] = [m.sem(f"moved{j}") for j in range(7)]
        with ExitStack() as inner:
            w = Space(nc, inner, "p5w")
            shared["tile_expert"] = w.sb("tile_expert", [P, NT], I32)
            shared["w1"] = w.sb("w1", [P, N_EXP, 4, FF])
            shared["b1"] = w.sb("b1", [P, N_EXP * FF])
            route(nc, io, shared)
            expert_tiles(nc, io, shared)
        combine(nc, io, shared)


def program(nc, io):
    with ExitStack() as ctx:
        m = Space(nc, ctx, "all")
        shared = {
            "const": m.sb("const", [P, C_KEPT]),
            "bkt_i": m.sb("bkt_i", [P, NG + 1], I32),
            "keep": m.sb("keep", [P, NG + 1]),
            "passed": m.sem("passed"),
        }
        sort_and_embed(nc, io, shared)
        edge_sums(nc, io, shared)
        shared["acc"] = m.sb("acc", [P, NB, D])
        node_layers(nc, io, shared)
        neighbour_sums(nc, io, shared)
        experts(nc, io, shared)


def filter_order(w):
    w = w[:, :4 * P].reshape(-1, 2, P, 2)
    return np.ascontiguousarray(np.concatenate([w[:, 0, :, 0], w[:, 1, :, 0], w[:, 0, :, 1], w[:, 1, :, 1]], axis=1))


def chunks(w):
    return np.ascontiguousarray(w.reshape(-1, P, w.shape[1]).transpose(1, 0, 2))


def lay_out(a):
    f = np.float32
    consts = np.zeros((P, C_END), f)
    consts[:, C_ID:C_ID + P] = np.eye(P)
    consts[:, C_TRI:C_TRI + P] = np.triu(np.ones((P, P)), 1)
    consts[:, C_IOTA:C_IOTA + P] = np.arange(P)
    consts[:, C_BKT:C_BKT + 64] = np.arange(64)
    consts[:, C_GRP:C_END] = np.arange(C_END - C_GRP)
    x = np.zeros((NPAD + P, D), f)
    x[:N_NODES] = a["x"]
    src = np.full(EPAD, NPAD, np.int32)
    src[:N_EDGES] = a["src"]
    dst = np.zeros(EPAD, np.int32)
    dst[:N_EDGES] = a["dst"]
    edges = np.zeros((EPAD, REC), f)
    edges[:, R_Y] = 1
    edges[:N_EDGES, 0:N_RBF] = a["edge_attr_20"]
    edges[:N_EDGES, R_ONE] = 1
    edges[:N_EDGES, R_Y:R_Y + 3] = a["edge_attr_3"]
    edges[:N_EDGES, R_CUT] = a["edge_weight"]
    return {
        "consts": consts, "x": x, "src": src.reshape(P, COLS), "dst": dst.reshape(P, COLS),
        "edges": edges.reshape(P, COLS, REC),
        "wf1": np.concatenate([a["L0_gnn_Wf1"], np.asarray(a["L0_gnn_bf1"])[None]]),
        "wf2": filter_order(np.asarray(a["L0_gnn_Wf2"])), "bf2": filter_order(np.asarray(a["L0_gnn_bf2"])[None]),
        "w1s": np.asarray(a["L0_gnn_W1_s"]).reshape(P, 2, P), "w1v": np.asarray(a["L0_gnn_W1_v"]).reshape(P, 2, P),
        "w2s": np.asarray(a["L0_gnn_W2_s"]), "w2v": np.asarray(a["L0_gnn_W2_v"]),
        "wup": chunks(np.asarray(a["L0_ffn_w_up"]).T), "wdn": chunks(np.asarray(a["L0_ffn_w_down"]).T),
        "wg": chunks(np.asarray(a["L1_gnn_weight"])), "gnn_bias": np.asarray(a["L1_gnn_bias"])[None],
        "ew1": np.ascontiguousarray(np.asarray(a["L1_ffn_W1"]).reshape(N_EXP, 4, P, FF).transpose(2, 0, 1, 3)),
        "ew2": np.ascontiguousarray(np.asarray(a["L1_ffn_W2"]).reshape(N_EXP, 2, P, D).transpose(2, 0, 1, 3)),
        "b1": np.asarray(a["L1_ffn_b1"]).reshape(1, -1),
        "b2": np.asarray(a["L1_ffn_b2"]).reshape(1, -1), "rw": chunks(np.asarray(a["L1_ffn_router_w"])),
        "rb": np.asarray(a["L1_ffn_router_b"])[None],
        "lower": np.tril(np.ones((N_EXP, N_EXP), f), -1).reshape(1, -1),
        "w_in_s": np.asarray(a["L0_gnn_W_in2f_s"]), "w_in_v": np.asarray(a["L0_gnn_W_in2f_v"]),
    }


SCRATCH = {"sorted": [NG_ROWS * GE, REC], "table_a": [NPAD, D], "agg": [NPAD, 2 * D], "table_b": [NPAD, D],
           "packed": [NT * P, D], "results": [NT * P, D]}


def kernel(**inputs):
    import concourse.bacc as bacc
    from concourse.bass_utils import run_bass_kernel_spmd

    nc = bacc.Bacc("TRN2", target_bir_lowering=False, num_devices=1)
    arrays = {f"in_{k}": np.ascontiguousarray(v) for k, v in lay_out({k: np.asarray(v) for k, v in inputs.items()}).items()}
    io = {k[3:]: nc.dram_tensor(k, v.shape, mybir.dt.from_np(v.dtype), kind="ExternalInput").ap()
          for k, v in arrays.items()}
    for k, shape in SCRATCH.items():
        io[k] = nc.dram_tensor(k, shape, F32).ap()
    io["out"] = nc.dram_tensor("out", [NPAD, D], F32, kind="ExternalOutput").ap()
    program(nc, io)
    result = run_bass_kernel_spmd(nc, [arrays], core_ids=[0])
    return result.results[0]["out"][:N_NODES]
```
